# Optimizing a Trainium2 kernel written in Bass

```python
import numpy as np
import jax
import jax.numpy as jnp

def _softmax(x, axis=-1):
    return jax.nn.softmax(x, axis=axis)

def _gelu(x):
    return jax.nn.gelu(x, approximate=True)

def _silu(x):
    return jax.nn.silu(x)

def _sigmoid(x):
    return jax.nn.sigmoid(x)

def _layernorm(x, axis=-1, eps=1e-05):
    m = jnp.mean(x, axis=axis, keepdims=True)
    v = jnp.var(x, axis=axis, keepdims=True)
    return (x - m) / jnp.sqrt(v + eps)

def _scatter_add(tgt, idx, src, axis=0):
    return tgt.at[idx].add(src)

def _segment_sum(src, seg, n):
    return jax.ops.segment_sum(src, seg, n)
kernel_name = 'mk_early_fusion_d1_tok_img768_r4_7f7ecd'

def setup_inputs(seed: int=0):
    np.random.seed(seed)
    _w = jnp.asarray

    def _rec_inputs():
        import jax
        import jax.numpy as jnp
        _rk = jax.random.key(seed)
        x = -0.000356955 + 1 * jax.random.normal(jax.random.fold_in(_rk, 1), (16, 3, 224, 224), jnp.float32)
        txt = -6.28402e-05 + 0.577654 * jax.random.normal(jax.random.fold_in(_rk, 2), (16, 512, 192), jnp.float32)
        return (x, txt)
    x, txt = _rec_inputs()

    def _L0_tok_setup():
        import jax, jax.numpy as jnp
        import numpy as np
        PATCH = 16
        EMBED = 192
        IN_DIM = PATCH * PATCH * 3

        def extract_patches(x, p):
            B, C, H, Wd = x.shape
            h, w = (H // p, Wd // p)
            xr = x.reshape(B, C, h, p, w, p)
            xr = xr.transpose(0, 2, 4, 3, 5, 1)
            return xr.reshape(B, h * w, p * p * C)
        key = jax.random.key(seed)
        kx, kw, kb = jax.random.split(key, 3)
        x = jax.random.normal(kx, (128, 3, 224, 224), dtype=jnp.float32)
        bound = 1.0 / np.sqrt(IN_DIM)
        W = jax.random.uniform(kw, (EMBED, IN_DIM), jnp.float32, -bound, bound)
        b = jax.random.uniform(kb, (EMBED,), jnp.float32, -bound, bound)
        return {'x': x, 'W': W, 'b': b}
    _L0_tok_all = _L0_tok_setup()
    _L0_tok_in = {k: v for k, v in _L0_tok_all.items() if k in ('W', 'b')}
    del _L0_tok_all

    def _L0_attn_setup():
        import jax, jax.numpy as jnp
        import numpy as np
        D_MODEL = 192
        D_STATE = 64
        EXPAND = 2
        HEADDIM = 64
        D_INNER = EXPAND * D_MODEL
        NHEADS = D_INNER // HEADDIM
        CONV_CH = D_INNER + 2 * D_STATE
        D_IN_PROJ = 2 * D_INNER + 2 * D_STATE + NHEADS
        SEQ_LEN = 64
        BATCH = 8
        D_CONV = 4
        EPS = 1e-05

        def _mamba_scan(seq, W_in, conv_w, conv_b, dt_bias, A_log, D, norm_w, W_out):
            B = seq.shape[1]
            A = -jnp.exp(A_log)
            w_last = conv_w[:, -1]

            def step(h, x_t):
                zxbcdt = x_t @ W_in
                z = zxbcdt[:, :D_INNER]
                xBC = zxbcdt[:, D_INNER:D_INNER + CONV_CH]
                dt = zxbcdt[:, D_INNER + CONV_CH:]
                xBC = jax.nn.silu(xBC * w_last + conv_b)
                x = xBC[:, :D_INNER].reshape(B, NHEADS, HEADDIM)
                Bm = xBC[:, D_INNER:D_INNER + D_STATE]
                Cm = xBC[:, D_INNER + D_STATE:]
                dt = jax.nn.softplus(dt + dt_bias)
                dA = jnp.exp(dt * A)
                h = h * dA[:, :, None, None] + (dt[:, :, None] * x)[..., None] * Bm[:, None, None, :]
                y = jnp.einsum('bhpn,bn->bhp', h, Cm) + D[None, :, None] * x
                y = y.reshape(B, D_INNER) * jax.nn.silu(z)
                y = y * jax.lax.rsqrt(jnp.mean(y * y, axis=-1, keepdims=True) + EPS) * norm_w
                out = y @ W_out
                return (h, (out, h))
            h0 = jnp.zeros((B, NHEADS, HEADDIM, D_STATE), dtype=seq.dtype)
            _, (outputs, states) = jax.lax.scan(step, h0, seq)
            return (outputs, states)

        def _reference_tuple_inner(seq, W_in, conv_w, conv_b, dt_bias, A_log, D, norm_w, W_out):
            return _mamba_scan(seq, W_in, conv_w, conv_b, dt_bias, A_log, D, norm_w, W_out)
        key = jax.random.key(seed)
        ks = jax.random.split(key, 8)
        seq = jax.random.normal(ks[0], (SEQ_LEN, BATCH, D_MODEL), dtype=jnp.float32)
        W_in = jax.random.normal(ks[1], (D_MODEL, D_IN_PROJ), dtype=jnp.float32) * D_MODEL ** (-0.5)
        conv_w = jax.random.uniform(ks[2], (CONV_CH, D_CONV), dtype=jnp.float32, minval=-0.5, maxval=0.5)
        conv_b = jax.random.uniform(ks[3], (CONV_CH,), dtype=jnp.float32, minval=-0.1, maxval=0.1)
        dt_bias = jax.random.uniform(ks[4], (NHEADS,), dtype=jnp.float32, minval=-4.0, maxval=-1.0)
        A_log = jnp.log(jax.random.uniform(ks[5], (NHEADS,), dtype=jnp.float32, minval=1.0, maxval=16.0))
        D = jnp.ones((NHEADS,), dtype=jnp.float32) + 0.1 * jax.random.normal(ks[6], (NHEADS,), dtype=jnp.float32)
        norm_w = jnp.ones((D_INNER,), dtype=jnp.float32)
        W_out = jax.random.normal(ks[7], (D_INNER, D_MODEL), dtype=jnp.float32) * D_INNER ** (-0.5)
        return {'seq': seq, 'W_in': W_in, 'conv_w': conv_w, 'conv_b': conv_b, 'dt_bias': dt_bias, 'A_log': A_log, 'D': D, 'norm_w': norm_w, 'W_out': W_out}
    _L0_attn_all = _L0_attn_setup()
    _L0_attn_in = {k: v for k, v in _L0_attn_all.items() if k in ('W_in', 'conv_w', 'conv_b', 'dt_bias', 'A_log', 'D', 'norm_w', 'W_out')}
    del _L0_attn_all

    def _L0_ffn_setup():
        import jax, jax.numpy as jnp
        import numpy as np
        D_MODEL = 192
        D_FF = 768
        N_EXPERTS = 9
        key = jax.random.key(seed)
        ks = jax.random.split(key, 7)
        scale = 0.02
        return {'x': jax.random.normal(ks[0], (2, 256, D_MODEL), jnp.float32), 'Ws': jax.random.normal(ks[1], (D_MODEL, N_EXPERTS), jnp.float32) * scale, 'bs': jnp.zeros((N_EXPERTS,), jnp.float32), 'W1': jax.random.normal(ks[2], (N_EXPERTS, D_MODEL, D_FF), jnp.float32) * scale, 'b1': jnp.zeros((N_EXPERTS, D_FF), jnp.float32), 'W2': jax.random.normal(ks[3], (N_EXPERTS, D_FF, D_MODEL), jnp.float32) * scale, 'b2': jnp.zeros((N_EXPERTS, D_MODEL), jnp.float32)}
    _L0_ffn_all = _L0_ffn_setup()
    _L0_ffn_in = {k: v for k, v in _L0_ffn_all.items() if k in ('Ws', 'bs', 'W1', 'b1', 'W2', 'b2')}
    del _L0_ffn_all
    return {'x': x, 'txt': txt, 'L0_tok_W': _L0_tok_in['W'], 'L0_tok_b': _L0_tok_in['b'], 'L0_attn_W_in': _L0_attn_in['W_in'], 'L0_attn_conv_w': _L0_attn_in['conv_w'], 'L0_attn_conv_b': _L0_attn_in['conv_b'], 'L0_attn_dt_bias': _L0_attn_in['dt_bias'], 'L0_attn_A_log': _L0_attn_in['A_log'], 'L0_attn_D': _L0_attn_in['D'], 'L0_attn_norm_w': _L0_attn_in['norm_w'], 'L0_attn_W_out': _L0_attn_in['W_out'], 'L0_ffn_Ws': _L0_ffn_in['Ws'], 'L0_ffn_bs': _L0_ffn_in['bs'], 'L0_ffn_W1': _L0_ffn_in['W1'], 'L0_ffn_b1': _L0_ffn_in['b1'], 'L0_ffn_W2': _L0_ffn_in['W2'], 'L0_ffn_b2': _L0_ffn_in['b2']}

def reference(x, txt, L0_tok_W, L0_tok_b, L0_attn_W_in, L0_attn_conv_w, L0_attn_conv_b, L0_attn_dt_bias, L0_attn_A_log, L0_attn_D, L0_attn_norm_w, L0_attn_W_out, L0_ffn_Ws, L0_ffn_bs, L0_ffn_W1, L0_ffn_b1, L0_ffn_W2, L0_ffn_b2):
    import jax
    import jax.numpy as jnp

    def _L0_tok_ref(x, W, b):
        import jax, jax.numpy as jnp
        import numpy as np
        PATCH = 16
        EMBED = 192
        IN_DIM = PATCH * PATCH * 3

        def extract_patches(x, p):
            B, C, H, Wd = x.shape
            h, w = (H // p, Wd // p)
            xr = x.reshape(B, C, h, p, w, p)
            xr = xr.transpose(0, 2, 4, 3, 5, 1)
            return xr.reshape(B, h * w, p * p * C)
        patches = extract_patches(x, PATCH)
        return jnp.einsum('bnd,ed->bne', patches, W) + b

    def _L0_attn_ref(seq, W_in, conv_w, conv_b, dt_bias, A_log, D, norm_w, W_out):
        import jax, jax.numpy as jnp
        import numpy as np
        D_MODEL = 192
        D_STATE = 64
        EXPAND = 2
        HEADDIM = 64
        D_INNER = EXPAND * D_MODEL
        NHEADS = D_INNER // HEADDIM
        CONV_CH = D_INNER + 2 * D_STATE
        D_IN_PROJ = 2 * D_INNER + 2 * D_STATE + NHEADS
        SEQ_LEN = 64
        BATCH = 8
        D_CONV = 4
        EPS = 1e-05

        def _mamba_scan(seq, W_in, conv_w, conv_b, dt_bias, A_log, D, norm_w, W_out):
            B = seq.shape[1]
            A = -jnp.exp(A_log)
            w_last = conv_w[:, -1]

            def step(h, x_t):
                zxbcdt = x_t @ W_in
                z = zxbcdt[:, :D_INNER]
                xBC = zxbcdt[:, D_INNER:D_INNER + CONV_CH]
                dt = zxbcdt[:, D_INNER + CONV_CH:]
                xBC = jax.nn.silu(xBC * w_last + conv_b)
                x = xBC[:, :D_INNER].reshape(B, NHEADS, HEADDIM)
                Bm = xBC[:, D_INNER:D_INNER + D_STATE]
                Cm = xBC[:, D_INNER + D_STATE:]
                dt = jax.nn.softplus(dt + dt_bias)
                dA = jnp.exp(dt * A)
                h = h * dA[:, :, None, None] + (dt[:, :, None] * x)[..., None] * Bm[:, None, None, :]
                y = jnp.einsum('bhpn,bn->bhp', h, Cm) + D[None, :, None] * x
                y = y.reshape(B, D_INNER) * jax.nn.silu(z)
                y = y * jax.lax.rsqrt(jnp.mean(y * y, axis=-1, keepdims=True) + EPS) * norm_w
                out = y @ W_out
                return (h, (out, h))
            h0 = jnp.zeros((B, NHEADS, HEADDIM, D_STATE), dtype=seq.dtype)
            _, (outputs, states) = jax.lax.scan(step, h0, seq)
            return (outputs, states)

        def _reference_tuple_inner(seq, W_in, conv_w, conv_b, dt_bias, A_log, D, norm_w, W_out):
            return _mamba_scan(seq, W_in, conv_w, conv_b, dt_bias, A_log, D, norm_w, W_out)
        return _reference_tuple_inner(seq, W_in, conv_w, conv_b, dt_bias, A_log, D, norm_w, W_out)[0]

    def _L0_ffn_ref(x, Ws, bs, W1, b1, W2, b2):
        import jax, jax.numpy as jnp
        import numpy as np
        D_MODEL = 192
        D_FF = 768
        N_EXPERTS = 9
        B, S, d = x.shape
        xt = x.reshape(-1, d)
        route_prob = jax.nn.softmax(xt @ Ws + bs, axis=-1)
        p = jnp.max(route_prob, axis=-1)
        routes = jnp.argmax(route_prob, axis=-1)
        h = jax.nn.gelu(jnp.einsum('td,edf->tef', xt, W1) + b1, approximate=False)
        out = jnp.einsum('tef,efd->ted', h, W2) + b2
        common = out[:, 0, :]
        sel = jnp.take_along_axis(out, routes[:, None, None], axis=1)[:, 0, :]
        scaling = (p / jax.lax.stop_gradient(p))[:, None]
        pe = p[:, None]
        final = jnp.where((routes == 0)[:, None], common * scaling, pe * sel + (1.0 - pe) * common)
        return final.reshape(B, S, d)
    h = _L0_tok_ref(x, L0_tok_W, L0_tok_b)
    h = jnp.concatenate([h, txt], axis=1)
    h = h + _L0_attn_ref(_layernorm(h, axis=-1), L0_attn_W_in, L0_attn_conv_w, L0_attn_conv_b, L0_attn_dt_bias, L0_attn_A_log, L0_attn_D, L0_attn_norm_w, L0_attn_W_out)
    h = h + _L0_ffn_ref(_layernorm(h, axis=-1), L0_ffn_Ws, L0_ffn_bs, L0_ffn_W1, L0_ffn_b1, L0_ffn_W2, L0_ffn_b2)
    return h

_drawn_inputs = setup_inputs


def setup_inputs(seed=0):
    import zlib

    import numpy as np

    out = dict(_drawn_inputs(seed))
    spreads = {'L0_attn_norm_w': (1.0, 0.2),
     'L0_ffn_bs': (0.0, 0.714),
     'L0_ffn_b1': (0.0, 0.37),
     'L0_ffn_b2': (0.0, 0.1)}
    factors = {'L0_attn_dt_bias': 30.224, 'L0_attn_A_log': 8.0, 'L0_ffn_Ws': 3.157}
    for name, (base, spread) in spreads.items():
        noise = np.random.default_rng([zlib.crc32(name.encode()), seed]).standard_normal(out[name].shape)
        drawn = base * np.exp(spread * noise) if base else spread * noise
        out[name] = jnp.asarray(drawn.astype(out[name].dtype))
    for name, factor in factors.items():
        out[name] = (out[name] * factor).astype(out[name].dtype)
    return out
```

```python
import numpy as np
from contextlib import ExitStack

import concourse.bass as bass
from concourse import mybir

TIMES = 16
N_PATCH = 196
N_TEXT = 512
POSITIONS = N_PATCH + N_TEXT
D = 192
DK0 = 128
DK1 = D - DK0
P = 128
POS_TILE = P // TIMES
GT = 3
GROUPS = -(-POSITIONS // (POS_TILE * GT))
TILES = GROUPS * GT
TOKENS = POSITIONS * TIMES
ROWS = TILES * P
D_INNER = 384
HEADS = 6
HEADDIM = 64
D_STATE = 64
PIX = 768
EXPERTS = 9
D_FF = 768
FCH = D_FF // P
SLOT_TILES = TOKENS // P + EXPERTS
ROW_W = 2 * D + 1
EPS = 1e-5
LOG1P_TERMS = 8


class Group:

    def __init__(self, j, r, cycle=2):
        self.j, self.r, self.cycle = j, r, cycle
        self.par = r % 2

    @property
    def n(self):
        return self.j * self.cycle + self.r

    def shift(self, d):
        q = self.r + d
        return Group(self.j + q // self.cycle, q % self.cycle, self.cycle)


def at_least(eng, sem, value):
    if isinstance(value, int) and value <= 0:
        return
    eng.wait_ge(sem, value)


def settle(eng, always):
    eng.sem_inc(always, 1)


class Chain:

    def __init__(self, eng, sem, n, per):
        self.eng, self.sem, self.n, self.per, self.k = eng, sem, n, per, 0

    def step(self, ins):
        self.k += 1
        ins.then_inc(self.sem, 1)

    def sync(self):
        at_least(self.eng, self.sem, self.n * self.per + self.k)

    def link(self, ins):
        self.step(ins)
        self.sync()

    def done(self):
        assert self.k == self.per, (self.k, self.per)


def build_kernel(nc, x, txt, tok_W, tok_b, W_in, conv_w, conv_b, dt_bias, A_log, D_skip, norm_w, W_out,
                 Ws, bs, W1, b1, W2, b2, out):
    f32, bf16, i32 = mybir.dt.float32, mybir.dt.bfloat16, mybir.dt.int32
    ALU, ACT, AX = mybir.AluOpType, mybir.ActivationFunctionType, mybir.AxisListType

    h_rows = nc.dram_tensor("h_rows", (ROWS, D), f32).ap()
    ffn_rows = nc.dram_tensor("ffn_rows", (ROWS, ROW_W), f32).ap()

    ctx = ExitStack()
    with ctx:
        def sb(name, shape, dt=f32):
            return ctx.enter_context(nc.sbuf_tensor(name, shape, dt))

        def sem(name):
            return ctx.enter_context(nc.semaphore(name))

        def sems(name, n):
            return [sem(f"{name}{i}") for i in range(n)]

        ident = sb("ident", [P, P])
        later = sb("later", [P, P])
        causal = sb("causal", [P, P])
        causal16 = sb("causal16", [P, TIMES])
        ones = sb("ones", [P, P])
        earlier_rows = sb("earlier_rows", [P, P])
        minus_half = sb("minus_half", [P, 4])
        iota9p9 = sb("iota9p9", [P, EXPERTS])
        tok_b_bc = sb("tok_b_bc", [P, D])
        neg_A = sb("neg_A", [P, HEADS])
        D_bc = sb("D_bc", [P, HEADS])
        small_in = sb("small_in", [P, 16])
        PROJ = 2 * D_INNER + HEADS
        IN_W = PROJ + 2 * D_STATE
        Wa = sb("Wa", [P, IN_W])
        Wb = sb("Wb", [DK1 + 1, IN_W])
        Wo = sb("Wo", [P, 3, D])
        Wsa = sb("Wsa", [P, EXPERTS])
        Wsb = sb("Wsb", [DK1 + 1, EXPERTS])
        patch_WT = sb("patch_WT", [P, 3, 2, D])
        routes = sb("routes", [P, TILES])
        W1a = sb("W1a", [P, EXPERTS, D_FF])
        W1b = sb("W1b", [DK1 + 1, EXPERTS, D_FF])
        W2s = sb("W2s", [P, EXPERTS, FCH, D])
        b2r = sb("b2r", [1, EXPERTS, D])
        w1_flat = W1a[:, :, :].rearrange("p e f -> p (e f)")
        w2_flat = W2s[:, :, :, :].rearrange("p e c d -> p (e c d)")
        HALF = 8 * 224
        RB = 2 * 3 * 14
        pix = [w1_flat[0:RB, u * HALF:(u + 1) * HALF] for u in range(2)]
        hp = [w2_flat[:, 4608 + u * D:4608 + (u + 1) * D] for u in range(2)]
        zeros = w2_flat[:, 5120:5120 + 384]
        pix_by_patch = [w2_flat[0:RB, 5632 + u * HALF:5632 + (u + 1) * HALF] for u in range(2)]
        conv_bc = w2_flat[:, 0:2048]
        patch_W = w2_flat[0:96, 2048:2048 + 2 * PIX].rearrange("p (a k) -> p a k", a=2)
        nw = w2_flat[:, 4096:4099]
        ARENA = 2 * 3 * N_PATCH * TIMES + 3800
        arena = sb("arena", [P, ARENA])
        XT = arena[:, 0:2 * 3 * N_PATCH * TIMES].rearrange("p (i c q b) -> p i c q b", i=2, c=3, b=TIMES)

        class Area:
            def __init__(self):
                self.at = 0

            def take(self, size, parts=P):
                a = arena[0:parts, self.at:self.at + size]
                self.at += size
                assert self.at <= ARENA, self.at
                return a

        ar = Area()
        k3 = lambda ap, w: ap.rearrange("p (k w) -> p k w", w=w)
        h_in = [k3(ar.take(GT * D), D) for _ in range(2)]
        h_res = [k3(ar.take(GT * D), D) for _ in range(2)]
        xn = [k3(ar.take(GT * D), D) for _ in range(2)]
        xT0 = [ar.take(GT * P) for _ in range(2)]
        xT1 = [ar.take(GT * P, DK1 + 1) for _ in range(2)]
        zs = [k3(ar.take(GT * D_INNER), D_INNER) for _ in range(2)]
        xs = [k3(ar.take(GT * D_INNER), D_INNER) for _ in range(2)]
        Bs = [ar.take(GT * P, D_STATE) for _ in range(2)]
        Cs = [ar.take(GT * P, D_STATE) for _ in range(2)]
        rows = [k3(ar.take(GT * ROW_W), ROW_W) for _ in range(2)]
        n2T0 = [ar.take(GT * P) for _ in range(2)]
        n2T1 = [ar.take(GT * P, DK1 + 1) for _ in range(2)]
        decay_in = ar.take(GT * HEADS * TIMES)
        decay = ar.take(GT * HEADS * TIMES)
        G_m = k3(ar.take(GT * P), P)
        M_all = ar.take(GT * HEADS * P).rearrange("p (k h t) -> p k h t", k=GT, h=HEADS)
        xD = k3(ar.take(GT * D_INNER), D_INNER)
        y = k3(ar.take(GT * D_INNER), D_INNER)
        yT = k3(ar.take(GT * D_INNER), D_INNER)
        sq = ar.take(D_INNER)
        st1 = ar.take(GT * 6)
        mv1 = ar.take(GT * 2)
        var1 = ar.take(GT)
        rs1 = ar.take(GT)
        st2 = ar.take(GT * 6)
        mv2 = ar.take(GT * 2)
        var2 = ar.take(GT)
        rs2 = ar.take(GT)
        ssq = ar.take(GT)
        ms = ar.take(GT)
        rsy = ar.take(GT)
        SH = GT * HEADS
        dtv, nabs, u_, den, rec, s_, w_, ser, relu, dts, a_ = [ar.take(SH) for _ in range(11)]
        lmax, rsum, rrec, pmax = [ar.take(GT) for _ in range(4)]
        ld_, le_, pr_, eq_, cand = [ar.take(GT * EXPERTS) for _ in range(5)]

        rt = Area()
        onehot = rt.take(EXPERTS * TILES).rearrange("p (e k) -> p e k", e=EXPERTS)
        running = rt.take(EXPERTS * TILES)
        no_add = rt.take(EXPERTS * TILES)
        to_slot = rt.take(EXPERTS * TILES).rearrange("p (e k) -> p e k", e=EXPERTS)
        iota_q = rt.take(P)
        iota_i = rt.take(SLOT_TILES)
        row_p1 = rt.take(1)
        seg0, count, before, total_e, tiles_e, tile_end, slot0 = [rt.take(EXPERTS) for _ in range(7)]
        slot, slot_q, slot_i, is_pad = [rt.take(TILES) for _ in range(4)]
        at_q = rt.take(TILES * P // 2).bitcast(bf16).rearrange("p (k q) -> p k q", q=P)
        at_i = rt.take(TILES * SLOT_TILES).bitcast(bf16).rearrange("p (k t i) -> p k t i", t=2, i=SLOT_TILES)
        SL = SLOT_TILES
        sums, = [rt.take(2 * SL)]
        row_f, empty, time_f, past = rt.take(SL), rt.take(SL), rt.take(SL), rt.take(SL * EXPERTS).rearrange("p (i e) -> p i e", e=EXPERTS)
        expert_f = rt.take(SL)
        ints = [rt.take(TILES).bitcast(i32) for _ in range(3)]
        cnt_i = rt.take(EXPERTS).bitcast(i32)
        row_ids = rt.take(SL).bitcast(i32)
        row_tmp = rt.take(SL).bitcast(i32)
        out_ids = rt.take(SL).bitcast(i32)
        expert_ids = rt.take(SL).bitcast(i32)
        ex = Area()
        tok_row = [ex.take(ROW_W) for _ in range(4)]
        fT0 = [ex.take(P) for _ in range(2)]
        fT1 = [ex.take(P, DK1 + 1) for _ in range(2)]
        g_common = [ex.take(D_FF).rearrange("p (c t) -> p c t", t=P) for _ in range(2)]
        g_tok = ex.take(D_FF)
        g_own = [ex.take(D_FF).rearrange("p (c t) -> p c t", t=P) for _ in range(2)]
        mixed = [ex.take(D) for _ in range(2)]
        one_minus_w = ex.take(2)
        ids_in = ex.take(4).bitcast(i32)
        ids_out = ex.take(4).bitcast(i32)
        assert ex.at < TILES * EXPERTS * 4 + P + 600 + TILES * (P + SL) // 2

        ps = ctx.enter_context(nc.psum_tensor("ps", [P, 8, 512], f32))

        ld_w = sem("ld_w")
        ld_pix = sems("ld_pix", 2)
        txt_copied = sem("txt_copied")
        pad_zeroed = sem("pad_zeroed")
        ld_experts = sem("ld_experts")
        settled_v, settled_g = sem("settled_v"), sem("settled_g")
        prep_v = sem("prep_v")
        prep_g = sem("prep_g")
        prep_a = sem("prep_a")
        prep_pe = sem("prep_pe")
        pix_cut = sem("pix_cut")
        pix_T = sem("pix_T")
        pix_ev_a = sem("pix_ev_a")
        pix_ev_v = sem("pix_ev_v")
        emb_mm = sem("emb_mm")
        emb_v = sem("emb_v")
        st_emb = sems("st_emb", 2)

        ld_h = sems("ld_h", 2)
        ld_res = sems("ld_res", 2)
        ln1_c = sem("ln1_c")
        ln1_p = sem("ln1_p")
        xn_done = sem("xn_done")
        t1_mm = sem("t1_mm")
        t1_ev = sem("t1_ev")
        proj_mm = sem("proj_mm")
        th_done = sem("th_done")
        silu_done = sem("silu_done")
        dt_c = sem("dt_c")
        u_done = sem("u_done")
        dts_done = sem("dts_done")
        dec_in_done = sem("dec_in_done")
        L_mm = sem("L_mm")
        E_done = sem("E_done")
        dec_done = sem("dec_done")
        G_mm = sem("G_mm")
        Gm_done = sem("Gm_done")
        M_v = sem("M_v")
        M_g = sem("M_g")
        xD_done = sem("xD_done")
        y_mm = sem("y_mm")
        y1_done = sem("y1_done")
        y2_done = sem("y2_done")
        sq_done = sem("sq_done")
        t2_mm = sem("t2_mm")
        t2_ev = sem("t2_ev")
        rsy_c = sem("rsy_c")
        o_mm = sem("o_mm")
        h2_done = sem("h2_done")
        ln2_c = sem("ln2_c")
        ln2_p = sem("ln2_p")
        n2_done = sem("n2_done")
        t3_mm = sem("t3_mm")
        t3_ev = sem("t3_ev")
        lg_mm = sem("lg_mm")
        lg_read = sem("lg_read")
        sm_exp = sem("sm_exp")
        sm_c = sem("sm_c")
        row_done = sem("row_done")
        st_rows = sems("st_rows", 2)

        rt_g = sem("rt_g")
        rt_v = sem("rt_v")
        rt_a = sem("rt_a")
        rt_count = sem("rt_count")
        rt_slots = sem("rt_slots")
        rt_done = sem("rt_done")
        f_ids = sem("f_ids")
        f_rows = sems("f_rows", 4)
        f_out = sems("f_out", 4)
        fx_mm = sem("fx_mm")
        fx_ev = sem("fx_ev")
        own1_mm = sem("own1_mm")
        com1_mm = sem("com1_mm")
        own_gelu = sem("own_gelu")
        com_gelu = sem("com_gelu")
        gT_mm = sem("gT_mm")
        gT_ev = sem("gT_ev")
        two_mm = sem("two_mm")
        mix_c = sem("mix_c")
        mix_done = sem("mix_done")

        block = ctx.enter_context(nc.Block())

        def pair(q):
            return 2 + 2 * (q % 2)

        EMB_TILES = N_PATCH * TIMES // P
        EMB_LAST = N_PATCH * TIMES - EMB_TILES * P
        x_blocks = x.rearrange("b c (h i) w -> (b c h) (i w)", i=16)
        out_rows = out.rearrange("b n d -> (b n) d")

        N_SMALL_LOADS = 19
        PREP_V = 20
        DT_LINKS = 9 + LOG1P_TERMS - 1
        RT_COUNT, RT_SLOT, RT_HOT = 16, 35, 39
        SM_LINKS = 8
        WP_BANKS = ((0, 5), (5, 5), (10, 4))
        T2_BANK = (0, 1, 0)
        Y_BANK = (7, 6, 7)
        O_BANK, O_COL = (1, 1, 0), (0, D, 0)

        def pix_move(u, q, w0, nw_, c, bt):
            src = ps[:, 1 + 3 * u + q, 0:nw_ * RB].rearrange("p (w b c h) -> p w b c h", b=2, c=3, h=14)[:, :, :, c, :]
            dst = XT[:, u, c, :, bass.ds(bt * 2, 2)].rearrange("p (h w) b -> p w b h", w=14)[:, w0:w0 + nw_]
            return dst, src

        def valid(group, total=GROUPS):
            n = group.n
            return not isinstance(n, int) or 0 <= n < total

        LOOP0, LOOP1 = 4, 28
        SLOT_LOOP0, SLOT_LOOP1 = 4, 92

        def pipeline(eng, step, first=-1, loop0=LOOP0, loop1=LOOP1, last=GROUPS + 2, cycle=2):
            for n in range(first, loop0):
                step(Group(n // cycle, n % cycle, cycle))
            with eng.Fori(loop0 // cycle, loop1 // cycle) as j:
                for r in range(cycle):
                    step(Group(j, r, cycle))
            for n in range(loop1, last):
                step(Group(n // cycle, n % cycle, cycle))

        def slot_pipeline(eng, step):
            pipeline(eng, step, -2, SLOT_LOOP0, SLOT_LOOP1, SLOT_TILES + 1, 4)

        def slot_valid(group):
            return valid(group, SLOT_TILES)

        def form_M(eng, k):
            g = G_m[:, k, :].rearrange("p (n j) -> p n j", j=TIMES).unsqueeze(1).to_broadcast([P, HEADS, POS_TILE, TIMES])
            d = decay.rearrange("p (k h j) -> p k h j", k=GT, h=HEADS)[:, k].unsqueeze(2).to_broadcast([P, HEADS, POS_TILE, TIMES])
            return eng.tensor_tensor(M_all[:, k].rearrange("p h (n j) -> p h n j", j=TIMES), g, d, ALU.mult)

        @block.sync
        def _(sp):
            sp.dma_start(patch_W, tok_W.rearrange("(a p) k -> p a k", a=2)).then_inc(ld_w, 16)
            sp.dma_start(pix[0], x_blocks[0:RB, 0:HALF]).then_inc(ld_pix[0], 16)
            sp.dma_start(pix[1], x_blocks[0:RB, HALF:2 * HALF]).then_inc(ld_pix[1], 16)
            sp.dma_start(tok_b_bc[:, :], tok_b.rearrange("(a d) -> a d", a=1).to_broadcast([P, D])).then_inc(ld_w, 16)
            sp.dma_start(conv_bc, conv_w.rearrange("(a c) k -> a (c k)", a=1).to_broadcast([P, 2048])).then_inc(ld_w, 16)
            for dst, rows_ in ((Wa[:, :], W_in[0:DK0, :]), (Wb[0:DK1, :], W_in[DK0:D, :])):
                sp.dma_start(dst[:, 0:768], rows_[:, 0:768]).then_inc(ld_w, 16)
                sp.dma_start(dst[:, PROJ:IN_W], rows_[:, 768:896]).then_inc(ld_w, 16)
                sp.dma_start(dst[:, 768:PROJ], rows_[:, 896:902]).then_inc(ld_w, 16)
            cb = conv_b.rearrange("(a c) -> a c", a=1)
            sp.dma_start(Wb[DK1:DK1 + 1, 384:768], cb[:, 0:384]).then_inc(ld_w, 16)
            sp.dma_start(Wb[DK1:DK1 + 1, PROJ:IN_W], cb[:, 384:512]).then_inc(ld_w, 16)
            sp.dma_start(Wb[DK1:DK1 + 1, 768:PROJ], dt_bias.rearrange("(a c) -> a c", a=1)).then_inc(ld_w, 16)
            sp.dma_start(small_in[:, 0:6], A_log.rearrange("(a c) -> a c", a=1).to_broadcast([P, 6])).then_inc(ld_w, 16)
            sp.dma_start(D_bc[:, :], D_skip.rearrange("(a c) -> a c", a=1).to_broadcast([P, 6])).then_inc(ld_w, 16)
            sp.dma_start(Wo[:, :, :], W_out.rearrange("(c p) d -> p c d", p=P)).then_inc(ld_w, 16)
            sp.dma_start(Wsa[:, :], Ws[0:DK0, :]).then_inc(ld_w, 16)
            sp.dma_start(Wsb[0:DK1, :], Ws[DK0:D, :]).then_inc(ld_w, 16)
            sp.dma_start(Wsb[DK1:DK1 + 1, :], bs.rearrange("(a c) -> a c", a=1)).then_inc(ld_w, 16)
            sp.dma_start(nw, norm_w.rearrange("(c p) -> p c", p=P), allow_slow_non_contiguous=True).then_inc(ld_w, 16)
            with sp.Fori(1, 8) as bt:
                for u in range(2):
                    row0 = sp.snap(bt * RB)
                    sp.wait_ge(pix_cut, bt * 2 + u - 1)
                    sp.dma_start(pix[u], x_blocks[bass.ds(row0, RB), u * HALF:(u + 1) * HALF]).then_inc(ld_pix[u], 16)
            for t in range(EMB_TILES + 1):
                n = P if t < EMB_TILES else EMB_LAST
                sp.wait_ge(emb_v, t + 1)
                sp.dma_start(h_rows[t * P:t * P + n, :], hp[t % 2][0:n, :]).then_inc(st_emb[t % 2], 16)
            sp.wait_ge(prep_v, PREP_V)
            sp.wait_ge(pad_zeroed, 16)
            sp.wait_ge(st_emb[0], 16 * 13)
            sp.wait_ge(st_emb[1], 16 * 12)
            sp.wait_ge(txt_copied, 16)

            def load_rows(dst, group, s):
                row0 = group.n * (GT * P)
                if not isinstance(row0, int):
                    row0 = sp.snap(row0)
                return dst, row0, s

            def load_h(group):
                dst, row0, s = load_rows(h_in[group.par], group, ld_h)
                at_least(sp, xn_done, 3 * (group.n - 1))
                sp.dma_start(dst, h_rows[bass.ds(row0, GT * P), :].rearrange("(k p) d -> p k d", p=P)).then_inc(ld_h[group.par], 16)

            def load_res(group):
                dst, row0, s = load_rows(h_res[group.par], group, ld_res)
                at_least(sp, h2_done, 3 * (group.n - 1))
                sp.dma_start(dst, h_rows[bass.ds(row0, GT * P), :].rearrange("(k p) d -> p k d", p=P)).then_inc(ld_res[group.par], 16)

            def store_rows(group):
                row0 = group.n * (GT * P)
                if not isinstance(row0, int):
                    row0 = sp.snap(row0)
                at_least(sp, row_done, group.n + 1)
                sp.dma_start(ffn_rows[bass.ds(row0, GT * P), :].rearrange("(k p) d -> p k d", p=P), rows[group.par]).then_inc(st_rows[group.par], 16)

            def step(group):
                if valid(group.shift(2)):
                    load_h(group.shift(2))
                if valid(group.shift(1)):
                    load_res(group.shift(1))
                if valid(group.shift(-2)):
                    store_rows(group.shift(-2))

            load_h(Group(0, 0))
            pipeline(sp, step)

            for r in range(4):
                sp.wait_ge(f_out[r], 16 * ((SLOT_TILES - r + 3) // 4))

        @block.gpsimd
        def _(pool):
            pool.memset(zeros, 0.0).then_inc(prep_g, 1)
            pool.memset(ident[:, :], 0.0).then_inc(prep_g, 1)
            pool.wait_ge(prep_g, 2)
            pool.affine_select(out=ident[:, :], in_=ident[:, :], compare_op=ALU.not_equal, fill=1.0, base=0,
                               pattern=[[-1, P]], channel_multiplier=1).then_inc(prep_g, 1)
            pool.memset(later[:, :], 1.0).then_inc(prep_g, 1)
            pool.memset(causal[:, :], 1.0).then_inc(prep_g, 1)
            pool.memset(minus_half[:, :], -0.5).then_inc(prep_g, 1)
            pool.wait_ge(prep_g, 6)
            pool.dma_start(h_rows[TOKENS:ROWS, :].rearrange("(p a) d -> p (a d)", p=96),
                           zeros[0:96, :]).then_inc(pad_zeroed, 16)
            pool.dma_start(h_rows[N_PATCH * TIMES:TOKENS, :].rearrange("(n b) d -> n b d", b=TIMES),
                           txt.rearrange("b n d -> n b d")).then_inc(txt_copied, 16)
            blocks = [[-TIMES, POS_TILE], [0, TIMES]]
            up_blocks = [[TIMES, POS_TILE], [0, TIMES]]
            pool.affine_select(out=later[:, :], in_=later[:, :], compare_op=ALU.is_gt, fill=0.0, base=0,
                               pattern=[[-1, P]], channel_multiplier=1).then_inc(prep_g, 1)
            pool.affine_select(out=causal[:, :], in_=causal[:, :], compare_op=ALU.is_ge, fill=0.0, base=0,
                               pattern=[[1, P]], channel_multiplier=-1).then_inc(prep_g, 1)
            pool.wait_ge(prep_g, 8)
            pool.affine_select(out=later[:, :], in_=later[:, :], compare_op=ALU.is_ge, fill=0.0, base=TIMES - 1,
                               pattern=up_blocks, channel_multiplier=-1).then_inc(prep_g, 1)
            pool.affine_select(out=causal[:, :], in_=causal[:, :], compare_op=ALU.is_ge, fill=0.0, base=0,
                               pattern=blocks, channel_multiplier=1).then_inc(prep_g, 1)
            pool.iota(iota9p9[:, :], [[1, EXPERTS]], base=9, channel_multiplier=0,
                      allow_small_or_imprecise_dtypes=True).then_inc(prep_g, 1)

            def cut_pixels(bt):
                for u in range(2):
                    pool.wait_ge(ld_pix[u], bt * 16 + 16)
                    at_least(pool, pix_T, bt * 2 + u - 1)
                    settle(pool, settled_g)
                    pool.tensor_copy(pix_by_patch[u].rearrange("p (w i j) -> p w i j", i=8, j=16),
                                     pix[u].rearrange("p (i w j) -> p w i j", i=8, j=16)).then_inc(pix_cut, 1)

            cut_pixels(0)
            with pool.Fori(1, 8) as bt:
                cut_pixels(bt)

            def power(src, dst, sem_, group, scale, ready, count):
                ch = Chain(pool, sem_, group.n, 2)
                at_least(pool, ready, count)
                settle(pool, settled_g)
                tmp = {id(rs1): var1, id(rs2): var2, id(rsy): ms}[id(dst)]
                ch.link(pool.tensor_scalar(tmp, src, scale, EPS, ALU.mult, ALU.add))
                ch.step(pool.tensor_tensor(dst, tmp, minus_half[:, 0:GT], ALU.pow))
                ch.done()

            def step(group):
                nxt, prv = group.shift(1), group.shift(-1)
                if valid(nxt):
                    power(mv1.rearrange("p (k s) -> p s k", s=2)[:, 1, :], rs1, ln1_p, nxt, 1.0, ln1_c, 6 * (nxt.n + 1))
                if valid(prv):
                    power(ssq, rsy, rsy_c, prv, 1.0 / D_INNER, sq_done, 3 * (prv.n + 1))
                if valid(group):
                    at_least(pool, silu_done, 4 * group.n + 3)
                    at_least(pool, y1_done, 3 * group.n)
                    v = lambda t: t.rearrange("p k (h e) -> p k h e", h=HEADS)
                    for k in range(GT):
                        ins = pool.tensor_tensor(
                            xD[:, k, :].rearrange("p (h e) -> p h e", h=HEADS),
                            xs[group.par][:, k, :].rearrange("p (h e) -> p h e", h=HEADS),
                            D_bc[:, :].unsqueeze(2).to_broadcast([P, HEADS, HEADDIM]), ALU.mult)
                    ins.then_inc(xD_done, 1)
                    at_least(pool, dec_done, group.n + 1)
                    at_least(pool, Gm_done, group.n + 1)
                    at_least(pool, y_mm, 3 * group.n)
                    form_M(pool, 2).then_inc(M_g, 1)
                if valid(prv):
                    power(mv2.rearrange("p (k s) -> p s k", s=2)[:, 1, :], rs2, ln2_p, prv, 1.0, ln2_c, 6 * (prv.n + 1))

            pool.wait_ge(emb_v, EMB_TILES + 1)
            pool.wait_ge(st_emb[0], 16 * 13)
            pool.wait_ge(st_emb[1], 16 * 12)
            pool.wait_ge(prep_v, PREP_V)
            pool.wait_ge(pad_zeroed, 16)
            pool.dma_start(W1a[:, :, :], W1[:, 0:DK0, :].rearrange("e p f -> p e f")).then_inc(ld_experts, 16)
            pool.dma_start(W1b[0:DK1, :, :], W1[:, DK0:D, :].rearrange("e p f -> p e f")).then_inc(ld_experts, 16)
            pool.dma_start(W1b[DK1:DK1 + 1, :, :], b1.rearrange("(a e) f -> a e f", a=1)).then_inc(ld_experts, 16)
            for e in range(EXPERTS):
                pool.dma_start(W2s[:, e], W2[e].rearrange("(c p) d -> p c d", p=P)).then_inc(ld_experts, 16)
            pool.dma_start(b2r[:, :, :], b2.rearrange("(a e) f -> a e f", a=1)).then_inc(ld_experts, 16)
            pipeline(pool, step)

            pool.wait_ge(st_rows[0], 16 * (GROUPS // 2))
            pool.wait_ge(st_rows[1], 16 * (GROUPS // 2))
            pool.iota(iota_q, [[1, P]], base=0, channel_multiplier=0, allow_small_or_imprecise_dtypes=True).then_inc(rt_g, 1)
            pool.iota(iota_i, [[1, SL]], base=0, channel_multiplier=0, allow_small_or_imprecise_dtypes=True).then_inc(rt_g, 1)
            pool.iota(row_p1, [[1, 1]], base=1, channel_multiplier=1, allow_small_or_imprecise_dtypes=True).then_inc(rt_g, 1)
            pool.memset(earlier_rows[:, :], 1.0).then_inc(rt_g, 1)
            pool.wait_ge(rt_g, 4)
            pool.affine_select(out=earlier_rows[:, :], in_=earlier_rows[:, :], compare_op=ALU.is_gt, fill=0.0, base=0,
                               pattern=[[1, P]], channel_multiplier=-1).then_inc(rt_g, 1)
            pool.wait_ge(rt_done, 1)

            def gather(t):
                at_least(pool, mix_done, t.n - 3)
                at_least(pool, f_out[t.r], 16 * t.j)
                settle(pool, settled_g)
                pool.tensor_copy(ids_in[:, t.r:t.r + 1], row_ids[:, bass.ds(t.n, 1)]).then_inc(f_ids, 1)
                pool.tensor_copy(ids_out[:, t.r:t.r + 1], out_ids[:, bass.ds(t.n, 1)]).then_inc(f_ids, 1)
                pool.wait_ge(f_ids, 2 * (t.n + 1))
                settle(pool, settled_g)
                pool.indirect_dma_start(tok_row[t.r], None, ffn_rows,
                                        bass.IndirectOffsetOnAxis(ap=ids_in[:, t.r:t.r + 1], axis=0),
                                        bounds_check=ROWS - 1, oob_is_err=False).then_inc(f_rows[t.r], 16)

            def scatter(t):
                pool.wait_ge(mix_done, t.n + 1)
                settle(pool, settled_g)
                pool.indirect_dma_start(out_rows, bass.IndirectOffsetOnAxis(ap=ids_out[:, t.r:t.r + 1], axis=0),
                                        mixed[t.par], None,
                                        bounds_check=TOKENS - 1, oob_is_err=False).then_inc(f_out[t.r], 16)

            def slot_step(t):
                if slot_valid(t.shift(-1)):
                    scatter(t.shift(-1))
                if slot_valid(t.shift(2)):
                    gather(t.shift(2))

            slot_pipeline(pool, slot_step)
        @block.scalar
        def _(act):
            act.wait_ge(ld_w, 16 * N_SMALL_LOADS)
            act.activation(neg_A[:, :], small_in[:, 0:6], ACT.Exp).then_inc(prep_a, 1)
            def move_pixels(bt):
                for u in range(2):
                    act.wait_ge(pix_T, bt * 2 + u + 1)
                    for q, (w0, nw_) in enumerate(WP_BANKS):
                        for c in range(3):
                            if q == 0:
                                dst, src = pix_move(u, q, w0, nw_, c, bt)
                                last = act.activation(dst, src, ACT.Copy)
                    last.then_inc(pix_ev_a, 1)

            with act.Fori(0, 8) as bt:
                move_pixels(bt)

            def step(group):
                nxt, prv, pp = group.shift(1), group.shift(-1), group.shift(-2)
                par = group.par

                def tanh(q):
                    at_least(act, proj_mm, 4 * group.n + q + 1)
                    b = pair(q)
                    if q < 3:
                        act.activation(zs[par][:, q, :], ps[:, b, 0:384], ACT.Tanh)
                        act.activation(xs[par][:, q, :], ps[:, b + 1, 0:384], ACT.Tanh).then_inc(th_done, 1)
                    else:
                        act.activation(Bs[par], ps[0:D_STATE, b, 0:384], ACT.Tanh)
                        act.activation(Cs[par], ps[0:D_STATE, b + 1, 0:384], ACT.Tanh).then_inc(th_done, 1)

                if valid(group):
                    at_least(act, y2_done, 3 * (group.n - 1))
                    at_least(act, y_mm, 3 * (group.n - 1))
                    at_least(act, G_mm, group.n - 1)
                    tanh(0)
                    tanh(1)
                if valid(pp):
                    at_least(act, t3_mm, pp.n + 1)
                    at_least(act, lg_mm, pp.n - 1)
                    act.activation(n2T0[par], ps[:, 0, 0:384], ACT.Copy).then_inc(t3_ev, 1)
                    act.activation(n2T1[par][0:DK1, :], ps[0:DK1, 1, 0:384], ACT.Copy).then_inc(t3_ev, 1)
                if valid(group):
                    tanh(2)
                    tanh(3)
                    at_least(act, dt_c, DT_LINKS * group.n + 1)
                    act.activation(u_, nabs, ACT.Exp).then_inc(u_done, 1)
                if valid(pp):
                    at_least(act, lg_read, pp.n + 1)
                    act.activation(le_, ld_, ACT.Exp).then_inc(sm_exp, 1)
                if valid(nxt):
                    at_least(act, t1_mm, nxt.n + 1)
                    at_least(act, proj_mm, 4 * (nxt.n - 1))
                    act.activation(xT0[nxt.par], ps[:, 0, 0:384], ACT.Copy).then_inc(t1_ev, 1)
                    act.activation(xT1[nxt.par][0:DK1, :], ps[0:DK1, 1, 0:384], ACT.Copy).then_inc(t1_ev, 1)
                if valid(prv):
                    for k in range(GT):
                        at_least(act, y2_done, 3 * prv.n + k + 1)
                        if k == 0:
                            at_least(act, rsy_c, 2 * prv.n)
                        at_least(act, sq_done, 3 * prv.n + k)
                        act.activation(sq, y[:, k, :], ACT.Square, accum_out=ssq[:, k:k + 1]).then_inc(sq_done, 1)
                        at_least(act, t2_mm, 3 * prv.n + k + 1)
                        at_least(act, o_mm, 3 * prv.n)
                        act.activation(yT[:, k, :], ps[:, T2_BANK[k], 0:384], ACT.Copy).then_inc(t2_ev, 1)
                if valid(group):
                    at_least(act, L_mm, group.n + 1)
                    at_least(act, M_v, 2 * group.n)
                    at_least(act, M_g, group.n)
                    act.activation(decay, ps[:, 6, 0:GT * HEADS * TIMES], ACT.Exp).then_inc(E_done, 1)

            pipeline(act, step)

            act.wait_ge(rt_slots, 1)
            act.activation(sums, ps[:, 0, 0:2 * SL], ACT.Copy).then_inc(rt_a, 1)

            def slot_step(t):
                if slot_valid(t):
                    at_least(act, own1_mm, t.n + 1)
                    at_least(act, gT_mm, t.n)
                    act.activation(g_tok.rearrange("p (b f) -> p b f", b=2), ps[:, 3:5, 0:384], ACT.Gelu).then_inc(own_gelu, 1)
                    at_least(act, com1_mm, t.n + 1)
                    at_least(act, two_mm, t.n - 1)
                    act.activation(g_common[t.par].rearrange("p (b c) t -> p b (c t)", b=2), ps[:, 1:3, 0:384], ACT.Gelu).then_inc(com_gelu, 1)

            slot_pipeline(act, slot_step)

        @block.vector
        def _(dve):
            ch = Chain(dve, prep_v, 0, 0)
            dve.memset(ones[:, :], 1.0)
            dve.wait_ge(ld_w, 16 * N_SMALL_LOADS)
            tap = conv_bc.rearrange("p (c k) -> p c k", k=4)[:, :, 3]
            for W, n in ((Wa, P), (Wb, DK1)):
                ch.step(dve.tensor_scalar(W[0:n, 0:384], W[0:n, 0:384], 0.5, None, ALU.mult))
                ch.step(dve.scalar_tensor_tensor(W[0:n, 384:768], W[0:n, 384:768], 0.5, tap[0:n, 0:384], ALU.mult, ALU.mult))
                ch.step(dve.scalar_tensor_tensor(W[0:n, PROJ:IN_W], W[0:n, PROJ:IN_W], 0.5, tap[0:n, 384:512], ALU.mult, ALU.mult))
            br = Wb[DK1:DK1 + 1, :]
            ch.step(dve.memset(br[:, 0:384], 0.0))
            ch.step(dve.tensor_scalar(br[:, 384:768], br[:, 384:768], 0.5, None, ALU.mult))
            ch.step(dve.tensor_scalar(br[:, PROJ:IN_W], br[:, PROJ:IN_W], 0.5, None, ALU.mult))
            for c in range(3):
                ch.step(dve.tensor_scalar(Wo[:, c, :], Wo[:, c, :], nw[:, c:c + 1], None, ALU.mult))
            dve.wait_ge(prep_a, 1)
            ch.step(dve.tensor_scalar(neg_A[:, :], neg_A[:, :], -1.0, None, ALU.mult))
            dve.wait_ge(prep_g, 11)
            ch.step(dve.tensor_reduce(causal16[:, :], causal[:, :].rearrange("p (n j) -> p j n", j=TIMES), AX.X, ALU.add))
            dve.wait_ge(prep_pe, 1)
            for i in range(2):
                for c in range(3):
                    ch.step(dve.tensor_copy(patch_WT[:, c, i, :], ps[:, c, i * D:(i + 1) * D]))
            assert ch.k == PREP_V, ch.k
            with dve.Fori(0, 8) as bt:
                for u in range(2):
                    dve.wait_ge(pix_T, bt * 2 + u + 1)
                    last = None
                    for q, (w0, nw_) in enumerate(WP_BANKS):
                        for c in range(3):
                            if q > 0:
                                dst, src = pix_move(u, q, w0, nw_, c, bt)
                                last = dve.tensor_copy(dst, src)
                    last.then_inc(pix_ev_v, 1)
            for t in range(EMB_TILES + 1):
                n = P if t < EMB_TILES else EMB_LAST
                dve.wait_ge(emb_mm, t + 1)
                if t >= 2:
                    dve.wait_ge(st_emb[t % 2], 16 * (t // 2))
                dve.tensor_tensor(hp[t % 2][0:n, :], ps[0:n, t % 8, 0:D], tok_b_bc[0:n, :], ALU.add).then_inc(emb_v, 1)
            for b in range(2):
                dve.memset(xT1[b][DK1:DK1 + 1, :], 1.0)
                last = dve.memset(n2T1[b][DK1:DK1 + 1, :], 1.0)
            last.then_inc(prep_v, 1)

            def step(group):
                nxt, prv, pp = group.shift(1), group.shift(-1), group.shift(-2)
                par = group.par

                def silu(q):
                    at_least(dve, th_done, 4 * group.n + q + 1)
                    b = pair(q)
                    if q < 3:
                        if q == 0:
                            at_least(dve, dec_in_done, group.n)
                            at_least(dve, dt_c, DT_LINKS * group.n)
                        dve.tensor_copy(dtv[:, q * HEADS:(q + 1) * HEADS], ps[:, b + 1, 384:390])
                        dve.scalar_tensor_tensor(zs[par][:, q, :], zs[par][:, q, :], 1.0, ps[:, b, 0:384], ALU.add, ALU.mult)
                        dve.scalar_tensor_tensor(xs[par][:, q, :], xs[par][:, q, :], 1.0, ps[:, b + 1, 0:384], ALU.add, ALU.mult).then_inc(silu_done, 1)
                    else:
                        dve.scalar_tensor_tensor(Bs[par], Bs[par], 1.0, ps[0:D_STATE, b, 0:384], ALU.add, ALU.mult)
                        dve.scalar_tensor_tensor(Cs[par], Cs[par], 1.0, ps[0:D_STATE, b + 1, 0:384], ALU.add, ALU.mult).then_inc(silu_done, 1)

                if valid(nxt):
                    c1 = Chain(dve, ln1_c, nxt.n, 6)
                    at_least(dve, ld_h[nxt.par], 16 * (nxt.j + 1))
                    at_least(dve, xn_done, 3 * nxt.n)
                    for k in range(GT):
                        c1.step(dve.bn_stats(st1[:, 6 * k:6 * k + 6], h_in[nxt.par][:, k, :]))
                    c1.sync()
                    settle(dve, settled_v)
                    for k in range(GT):
                        c1.step(dve.bn_aggr(mv1[:, 2 * k:2 * k + 2], st1[:, 6 * k:6 * k + 6]))
                    c1.done()
                if valid(group):
                    silu(0)
                if valid(nxt):
                    at_least(dve, ln1_p, 2 * (nxt.n + 1))
                    at_least(dve, t1_mm, nxt.n - 1)
                    c1.sync()
                    for k in range(GT):
                        dve.tensor_scalar(xn[nxt.par][:, k, :], h_in[nxt.par][:, k, :], mv1[:, 2 * k:2 * k + 1],
                                          rs1[:, k:k + 1], ALU.subtract, ALU.mult).then_inc(xn_done, 1)
                if valid(group):
                    silu(1)
                    silu(2)
                    cd = Chain(dve, dt_c, group.n, DT_LINKS)
                    at_least(dve, silu_done, 4 * group.n + 3)
                    cd.link(dve.scalar_tensor_tensor(nabs, dtv, -1.0, dtv, ALU.mult, ALU.min))
                    silu(3)
                if valid(pp):
                    cs = Chain(dve, sm_c, pp.n, SM_LINKS)
                    at_least(dve, lg_mm, pp.n + 1)
                    lg = ps[:, 6, 0:GT * EXPERTS].rearrange("p (k e) -> p k e", k=GT)
                    e3 = lambda t: t.rearrange("p (k e) -> p k e", k=GT)
                    bc = lambda t: t.unsqueeze(2).to_broadcast([P, GT, EXPERTS])
                    at_least(dve, row_done, pp.n)
                    cs.link(dve.tensor_reduce(lmax, lg, AX.X, ALU.max))
                    dve.tensor_tensor(e3(ld_), lg, bc(lmax), ALU.subtract).then_inc(lg_read, 1)

                def y_tile(k):
                    at_least(dve, y_mm, 3 * prv.n + k + 1)
                    if k == 0:
                        at_least(dve, xD_done, prv.n + 1)
                        at_least(dve, t2_mm, 3 * prv.n)
                        at_least(dve, sq_done, 3 * prv.n)
                    dve.tensor_tensor(y[:, k, :], ps[:, Y_BANK[k], 0:384], xD[:, k, :], ALU.add).then_inc(y1_done, 1)
                    at_least(dve, y1_done, 3 * prv.n + k + 1)
                    dve.tensor_tensor(y[:, k, :], y[:, k, :], zs[prv.par][:, k, :], ALU.mult).then_inc(y2_done, 1)

                if valid(prv):
                    y_tile(0)
                if valid(group):
                    at_least(dve, u_done, group.n + 1)
                    cd.link(dve.tensor_scalar(den, u_, 2.0, None, ALU.add))
                    cd.link(dve.reciprocal(rec, den))
                    cd.link(dve.tensor_tensor(s_, u_, rec, ALU.mult))
                    cd.link(dve.tensor_tensor(w_, s_, s_, ALU.mult))
                    cd.link(dve.tensor_scalar(ser, w_, 1.0 / (2 * LOG1P_TERMS - 1), None, ALU.mult))
                    for m in range(LOG1P_TERMS - 2, 0, -1):
                        cd.link(dve.scalar_tensor_tensor(ser, ser, 1.0 / (2 * m + 1), w_, ALU.add, ALU.mult))
                    cd.link(dve.scalar_tensor_tensor(ser, ser, 1.0, s_, ALU.add, ALU.mult))
                    cd.link(dve.tensor_scalar(relu, dtv, 0.0, None, ALU.max))
                    at_least(dve, dec_done, group.n)
                    cd.link(dve.scalar_tensor_tensor(dts, ser, 2.0, relu, ALU.mult, ALU.add))
                    cd.link(dve.tensor_tensor(a_.rearrange("p (k h) -> p k h", k=GT), dts.rearrange("p (k h) -> p k h", k=GT),
                                              neg_A[:, :].unsqueeze(1).to_broadcast([P, GT, HEADS]), ALU.mult))
                    cd.done()
                    at_least(dve, L_mm, group.n)
                    dve.tensor_tensor(decay_in.rearrange("p (s j) -> p s j", j=TIMES),
                                      a_.unsqueeze(2).to_broadcast([P, SH, TIMES]),
                                      causal16[:, :].unsqueeze(1).to_broadcast([P, SH, TIMES]), ALU.mult).then_inc(dec_in_done, 1)
                if valid(prv):
                    y_tile(1)
                if valid(pp):
                    at_least(dve, sm_exp, pp.n + 1)
                    cs.link(dve.tensor_reduce(rsum, e3(le_), AX.X, ALU.add))
                    cs.link(dve.reciprocal(rrec, rsum))
                    cs.link(dve.tensor_tensor(e3(pr_), e3(le_), bc(rrec), ALU.mult))
                    cs.link(dve.tensor_reduce(pmax, e3(pr_), AX.X, ALU.max))
                    cs.link(dve.tensor_tensor(e3(eq_), e3(pr_), bc(pmax), ALU.is_equal))
                    cs.link(dve.scalar_tensor_tensor(e3(cand), e3(eq_), -9.0, iota9p9[:, :].unsqueeze(1).to_broadcast([P, GT, EXPERTS]), ALU.mult, ALU.add))
                    r_now = routes[:, bass.ds(pp.n * GT, GT)]
                    cs.link(dve.tensor_reduce(r_now, e3(cand), AX.X, ALU.min))
                    cs.done()
                    dve.scalar_tensor_tensor(rows[pp.par][:, :, 2 * D:ROW_W].rearrange("p k a -> p (k a)"), r_now, 0.5, pmax,
                                             ALU.is_gt, ALU.mult).then_inc(row_done, 1)
                if valid(prv):
                    y_tile(2)
                if valid(group):
                    at_least(dve, E_done, group.n + 1)
                    dve.tensor_tensor(decay.rearrange("p (s j) -> p s j", j=TIMES), decay.rearrange("p (s j) -> p s j", j=TIMES),
                                      dts.unsqueeze(2).to_broadcast([P, SH, TIMES]), ALU.mult).then_inc(dec_done, 1)
                    at_least(dve, G_mm, group.n + 1)
                    at_least(dve, M_g, group.n)
                    dve.tensor_tensor(G_m, ps[:, 7, 0:384].rearrange("p (k t) -> p k t", k=GT),
                                      causal[:, :].unsqueeze(1).to_broadcast([P, GT, P]), ALU.mult).then_inc(Gm_done, 1)
                    at_least(dve, dec_done, group.n + 1)
                    at_least(dve, Gm_done, group.n + 1)
                    at_least(dve, y_mm, 3 * group.n)
                    for k in range(2):
                        form_M(dve, k).then_inc(M_v, 1)
                if valid(prv):
                    at_least(dve, rsy_c, 2 * (prv.n + 1))
                    at_least(dve, ld_res[prv.par], 16 * (prv.j + 1))
                    at_least(dve, st_rows[prv.par], 16 * prv.j)
                    for k in range(GT):
                        at_least(dve, o_mm, 3 * prv.n + max(k + 1, 2))
                        dve.scalar_tensor_tensor(rows[prv.par][:, k, D:2 * D], ps[:, O_BANK[k], O_COL[k]:O_COL[k] + D], rsy[:, k:k + 1],
                                                 h_res[prv.par][:, k, :], ALU.mult, ALU.add).then_inc(h2_done, 1)
                    c2 = Chain(dve, ln2_c, prv.n, 6)
                    at_least(dve, n2_done, 3 * prv.n)
                    for k in range(GT):
                        at_least(dve, h2_done, 3 * prv.n + k + 1)
                        c2.step(dve.bn_stats(st2[:, 6 * k:6 * k + 6], rows[prv.par][:, k, D:2 * D]))
                    c2.sync()
                    settle(dve, settled_v)
                    for k in range(GT):
                        c2.step(dve.bn_aggr(mv2[:, 2 * k:2 * k + 2], st2[:, 6 * k:6 * k + 6]))
                    c2.sync()
                    c2.done()
                    at_least(dve, ln2_p, 2 * (prv.n + 1))
                    for k in range(GT):
                        dve.tensor_scalar(rows[prv.par][:, k, 0:D], rows[prv.par][:, k, D:2 * D], mv2[:, 2 * k:2 * k + 1],
                                          rs2[:, k:k + 1], ALU.subtract, ALU.mult).then_inc(n2_done, 1)

            pipeline(dve, step)

            dve.wait_ge(st_rows[0], 16 * (GROUPS // 2))
            dve.wait_ge(st_rows[1], 16 * (GROUPS // 2))
            rc = Chain(dve, rt_v, 0, 0)
            full = TOKENS // P
            rc.step(dve.memset(routes[TOKENS - full * P:P, full:full + 1], float(EXPERTS)))
            rc.step(dve.memset(routes[:, full + 1:TILES], float(EXPERTS)))
            rc.link(dve.memset(no_add, 0.0))
            for e in range(EXPERTS):
                rc.step(dve.tensor_scalar(onehot[:, e, :], routes[:, :], float(e), None, ALU.is_equal))
            rc.sync()
            flat = onehot.rearrange("p e k -> p (e k)")
            rc.link(dve.tensor_tensor_scan(running, flat, no_add, 0.0, ALU.add, ALU.add))
            r3 = running.rearrange("p (e k) -> p e k", e=EXPERTS)
            rc.link(dve.tensor_tensor(to_slot, r3, onehot, ALU.subtract))
            rc.link(dve.tensor_copy(seg0, to_slot[:, :, 0]))
            rc.link(dve.tensor_tensor(count, r3[:, :, TILES - 1], seg0, ALU.subtract))
            assert rc.k == RT_COUNT, rc.k
            dve.wait_ge(rt_count, 1)
            rc.step(dve.tensor_copy(before, ps[:, 1, 0:EXPERTS]))
            rc.link(dve.tensor_scalar(total_e, ps[:, 2, 0:EXPERTS], float(P - 1), None, ALU.add))
            rc.link(dve.tensor_copy(cnt_i, total_e))
            rc.link(dve.tensor_scalar(cnt_i, cnt_i, 7, None, ALU.logical_shift_right))
            rc.link(dve.tensor_copy(tiles_e, cnt_i))
            rc.link(dve.tensor_tensor_scan(tile_end, tiles_e, no_add[:, 0:EXPERTS], 0.0, ALU.add, ALU.add))
            rc.link(dve.tensor_tensor(slot0, tile_end, tiles_e, ALU.subtract))
            rc.link(dve.scalar_tensor_tensor(slot0, slot0, float(P), before, ALU.mult, ALU.add))
            rc.link(dve.tensor_tensor(slot0, slot0, seg0, ALU.subtract))
            rc.link(dve.tensor_tensor(to_slot, to_slot, slot0.unsqueeze(2).to_broadcast([P, EXPERTS, TILES]), ALU.add))
            rc.link(dve.tensor_tensor(to_slot, to_slot, onehot, ALU.mult))
            rc.link(dve.tensor_reduce(slot, to_slot.rearrange("p e k -> p k e"), AX.X, ALU.add))
            rc.link(dve.tensor_scalar(is_pad, routes[:, :], EXPERTS - 0.5, float(2 * SL * P), ALU.is_gt, ALU.mult))
            rc.link(dve.tensor_tensor(slot, slot, is_pad, ALU.add))
            rc.link(dve.tensor_copy(ints[0], slot))
            rc.step(dve.tensor_scalar(ints[1], ints[0], P - 1, None, ALU.bitwise_and))
            rc.link(dve.tensor_scalar(ints[2], ints[0], 7, None, ALU.logical_shift_right))
            rc.step(dve.tensor_copy(slot_q, ints[1]))
            rc.link(dve.tensor_copy(slot_i, ints[2]))
            assert rc.k == RT_SLOT, rc.k
            dve.wait_ge(rt_g, 3)
            rc.step(dve.tensor_tensor(at_q, iota_q.unsqueeze(1).to_broadcast([P, TILES, P]),
                                      slot_q.unsqueeze(2).to_broadcast([P, TILES, P]), ALU.is_equal))
            eq_i = at_i[:, :, 1, :]
            rc.link(dve.tensor_tensor(eq_i, iota_i.unsqueeze(1).to_broadcast([P, TILES, SL]),
                                      slot_i.unsqueeze(2).to_broadcast([P, TILES, SL]), ALU.is_equal))
            rc.link(dve.tensor_tensor(at_i[:, :, 0, :], eq_i, iota_i[:, 0:TILES].unsqueeze(2).to_broadcast([P, TILES, SL]), ALU.mult))
            rc.link(dve.tensor_scalar(eq_i, eq_i, row_p1, None, ALU.mult))
            assert rc.k == RT_HOT, rc.k
            rc.link(dve.tensor_tensor(past, iota_i.unsqueeze(2).to_broadcast([P, SL, EXPERTS]),
                                      tile_end.unsqueeze(1).to_broadcast([P, SL, EXPERTS]), ALU.is_ge))
            rc.link(dve.tensor_reduce(expert_f, past, AX.X, ALU.add))
            rc.link(dve.tensor_scalar(expert_f, expert_f, float(EXPERTS - 1), None, ALU.min))
            rc.link(dve.tensor_copy(expert_ids, expert_f))
            dve.wait_ge(rt_a, 1)
            rc.link(dve.tensor_scalar(empty, sums[:, SL:2 * SL], 0.5, float(ROWS), ALU.is_lt, ALU.mult))
            rc.link(dve.scalar_tensor_tensor(row_f, sums[:, 0:SL], float(P), sums[:, SL:2 * SL], ALU.mult, ALU.add))
            rc.link(dve.scalar_tensor_tensor(row_f, row_f, -1.0, empty, ALU.add, ALU.add))
            rc.link(dve.tensor_copy(row_ids, row_f))
            rc.link(dve.tensor_scalar(row_tmp, row_ids, TIMES - 1, None, ALU.bitwise_and))
            rc.link(dve.tensor_copy(time_f, row_tmp))
            rc.link(dve.tensor_scalar(row_tmp, row_ids, 4, None, ALU.logical_shift_right))
            rc.link(dve.tensor_copy(row_f, row_tmp))
            rc.link(dve.scalar_tensor_tensor(row_f, time_f, float(POSITIONS), row_f, ALU.mult, ALU.add))
            dve.tensor_copy(out_ids, row_f).then_inc(rt_done, 1)
            dve.wait_ge(rt_done, 1)
            for b in range(2):
                last = dve.memset(fT1[b][DK1:DK1 + 1, :], 1.0)
            last.then_inc(rt_done, 1)

            def slot_step(t):
                nxt, prv = t.shift(1), t.shift(-1)
                if slot_valid(nxt):
                    at_least(dve, fx_mm, nxt.n + 1)
                    at_least(dve, com1_mm, nxt.n - 1)
                    dve.tensor_copy(fT0[nxt.par], ps[:, 0, 0:P])
                    dve.tensor_copy(fT1[nxt.par][0:DK1, :], ps[0:DK1, 0, P:2 * P]).then_inc(fx_ev, 1)
                if slot_valid(prv):
                    w = tok_row[prv.r][:, 2 * D:ROW_W]
                    cm = Chain(dve, mix_c, prv.n, 2)
                    cm.step(dve.tensor_scalar(one_minus_w[:, 0:1], w, -1.0, 1.0, ALU.mult, ALU.add))
                    at_least(dve, two_mm, prv.n + 1)
                    at_least(dve, f_out[prv.shift(-2).r], 16 * prv.shift(2).j)
                    cm.sync()
                    cm.link(dve.scalar_tensor_tensor(mixed[prv.par], ps[:, 7, 0:D], one_minus_w[:, 0:1], tok_row[prv.r][:, D:2 * D], ALU.mult, ALU.add))
                    cm.done()
                    dve.scalar_tensor_tensor(mixed[prv.par], ps[:, 7, D:2 * D], w, mixed[prv.par], ALU.mult, ALU.add).then_inc(mix_done, 1)
                if slot_valid(t):
                    at_least(dve, gT_mm, t.n + 1)
                    at_least(dve, two_mm, t.n - 1)
                    dve.tensor_copy(g_own[t.par].rearrange("p (b c) t -> p b (c t)", b=2), ps[:, 5:7, 0:384]).then_inc(gT_ev, 1)

            slot_pipeline(dve, slot_step)

        @block.tensor
        def _(pe):
            pe.wait_ge(prep_g, 3)
            pe.wait_ge(ld_w, 16 * N_SMALL_LOADS)
            pw = patch_W.rearrange("p a (i q c) -> p a i q c", i=2, c=3)
            for i in range(2):
                for c in range(3):
                    for a in range(2):
                        last = nc.tensor.transpose(ps[:, c, i * D + a * 96:i * D + (a + 1) * 96], pw[:, a, i, :, c], ident[0:96, 0:96])
            last.then_inc(prep_pe, 1)
            pe.wait_ge(prep_v, PREP_V)
            def transpose_pixels(bt):
                for u in range(2):
                    pe.wait_ge(pix_cut, bt * 2 + u + 1)
                    at_least(pe, pix_ev_a, bt * 2 + u - 1)
                    at_least(pe, pix_ev_v, bt * 2 + u - 1)
                    for q, (w0, nw_) in enumerate(WP_BANKS):
                        for w in range(nw_):
                            last = nc.tensor.transpose(ps[:, 1 + 3 * u + q, w * RB:(w + 1) * RB], pix_by_patch[u][:, (w0 + w) * P:(w0 + w + 1) * P], ident[0:RB, 0:RB])
                    last.then_inc(pix_T, 1)

            transpose_pixels(0)
            with pe.Fori(1, 8) as bt:
                transpose_pixels(bt)
            pe.wait_ge(pix_ev_a, 16)
            pe.wait_ge(pix_ev_v, 16)
            for t in range(EMB_TILES + 1):
                n = P if t < EMB_TILES else EMB_LAST
                if t >= 8:
                    pe.wait_ge(emb_v, t - 7)
                for m in range(6):
                    c, i = m // 2, m % 2
                    lhs = XT[:, i, c, t * POS_TILE:t * POS_TILE + n // TIMES, :].rearrange("p q b -> p (q b)")
                    last = nc.tensor.matmul(ps[0:n, t % 8, 0:D], lhs, patch_WT[:, c, i, :], start=(m == 0), stop=(m == 5))
                last.then_inc(emb_mm, 1)
            pe.wait_ge(prep_v, PREP_V + 1)
            pe.wait_ge(emb_v, EMB_TILES + 1)

            def step(group):
                nxt, prv, pp = group.shift(1), group.shift(-1), group.shift(-2)
                par = group.par

                def transpose_rows(src, sem_):
                    for k in range(GT):
                        nc.tensor.transpose(ps[:, 0, k * P:(k + 1) * P], src[:, k, 0:DK0], ident[:, :])
                        last = nc.tensor.transpose(ps[0:DK1, 1, k * P:(k + 1) * P], src[:, k, DK0:D], ident[:, :])
                    last.then_inc(sem_, 1)

                def proj(q):
                    b = pair(q)
                    if q == 0:
                        at_least(pe, t1_ev, 2 * (group.n + 1))
                    at_least(pe, silu_done, 4 * group.n + q - 1)
                    if q < 3:
                        for W, T, s in ((Wa, xT0[par], 0), (Wb, xT1[par], 1)):
                            nc.tensor.matmul(ps[:, b, 0:384], T[:, q * P:(q + 1) * P], W[:, 0:384], start=s == 0, stop=s == 1)
                            last = nc.tensor.matmul(ps[:, b + 1, 0:390], T[:, q * P:(q + 1) * P], W[:, 384:PROJ], start=s == 0, stop=s == 1)
                    else:
                        for W, T, s in ((Wa, xT0[par], 0), (Wb, xT1[par], 1)):
                            nc.tensor.matmul(ps[0:D_STATE, b, 0:384], W[:, PROJ:PROJ + D_STATE], T, start=s == 0, stop=s == 1)
                            last = nc.tensor.matmul(ps[0:D_STATE, b + 1, 0:384], W[:, PROJ + D_STATE:IN_W], T, start=s == 0, stop=s == 1)
                    last.then_inc(proj_mm, 1)

                def y_tile(k):
                    if k == 0:
                        at_least(pe, M_v, 2 * (prv.n + 1))
                        at_least(pe, M_g, prv.n + 1)
                        at_least(pe, silu_done, 4 * prv.n + 3)
                        at_least(pe, Gm_done, prv.n + 1)
                    if k == 1:
                        at_least(pe, E_done, prv.n + 1)
                        if valid(pp):
                            at_least(pe, lg_read, pp.n + 1)
                    if k == 2:
                        at_least(pe, y1_done, 3 * prv.n + 1)
                    for h in range(HEADS):
                        last = nc.tensor.matmul(ps[:, Y_BANK[k], h * HEADDIM:(h + 1) * HEADDIM], M_all[:, k, h, :],
                                                xs[prv.par][:, k, h * HEADDIM:(h + 1) * HEADDIM], start=True, stop=True)
                    last.then_inc(y_mm, 1)

                if valid(group):
                    proj(0)
                    proj(1)
                if valid(pp):
                    at_least(pe, n2_done, 3 * (pp.n + 1))
                    at_least(pe, h2_done, 3 * (pp.n + 1))
                    transpose_rows(rows[pp.par], t3_mm)
                if valid(group):
                    proj(2)
                    proj(3)
                if valid(pp):
                    at_least(pe, t3_ev, 2 * (pp.n + 1))
                    at_least(pe, E_done, pp.n + 2 if valid(prv) else pp.n + 1)
                    for k in range(GT):
                        o = ps[:, 6, k * EXPERTS:(k + 1) * EXPERTS]
                        nc.tensor.matmul(o, n2T0[pp.par][:, k * P:(k + 1) * P], Wsa[:, :], start=True, stop=False)
                        last = nc.tensor.matmul(o, n2T1[pp.par][:, k * P:(k + 1) * P], Wsb[:, :], start=False, stop=True)
                    last.then_inc(lg_mm, 1)
                if valid(prv):
                    y_tile(0)
                    y_tile(1)
                if valid(nxt):
                    at_least(pe, xn_done, 3 * (nxt.n + 1))
                    if valid(pp):
                        at_least(pe, t3_ev, 2 * (pp.n + 1))
                    transpose_rows(xn[nxt.par], t1_mm)
                if valid(prv):
                    y_tile(2)
                    for k in range(GT):
                        at_least(pe, y2_done, 3 * prv.n + k + 1)
                        if k < 2:
                            if valid(nxt):
                                at_least(pe, t1_ev, 2 * (nxt.n + 1))
                            elif valid(pp):
                                at_least(pe, t3_ev, 2 * (pp.n + 1))
                        else:
                            at_least(pe, t2_ev, 3 * prv.n + 1)
                        for c in range(3):
                            last = nc.tensor.transpose(ps[:, T2_BANK[k], c * P:(c + 1) * P], y[:, k, c * P:(c + 1) * P], ident[:, :])
                        last.then_inc(t2_mm, 1)
                if valid(group):
                    at_least(pe, dec_in_done, group.n + 1)
                    if valid(prv):
                        at_least(pe, y1_done, 3 * prv.n + 3)
                    nc.tensor.matmul(ps[:, 6, 0:GT * HEADS * TIMES], later[:, :], decay_in, start=True, stop=True).then_inc(L_mm, 1)
                    at_least(pe, silu_done, 4 * (group.n + 1))
                    for k in range(GT):
                        last = nc.tensor.matmul(ps[:, 7, k * P:(k + 1) * P], Bs[par][:, k * P:(k + 1) * P], Cs[par][:, k * P:(k + 1) * P],
                                                start=True, stop=True)
                    last.then_inc(G_mm, 1)
                if valid(prv):
                    for k in range(GT):
                        at_least(pe, t2_ev, 3 * prv.n + 3)
                        for c in range(3):
                            last = nc.tensor.matmul(ps[:, O_BANK[k], O_COL[k]:O_COL[k] + D], yT[:, k, c * P:(c + 1) * P], Wo[:, c, :],
                                                    start=c == 0, stop=c == 2)
                        last.then_inc(o_mm, 1)

            pipeline(pe, step)

            pe.wait_ge(rt_v, RT_COUNT)
            pe.wait_ge(rt_g, 5)
            nc.tensor.matmul(ps[:, 1, 0:EXPERTS], earlier_rows[:, :], count, start=True, stop=True)
            nc.tensor.matmul(ps[:, 2, 0:EXPERTS], ones[:, :], count, start=True, stop=True).then_inc(rt_count, 1)
            pe.wait_ge(rt_v, RT_HOT)

            def add_tile(k, start, stop):
                return nc.tensor.matmul(ps[:, 0, 0:2 * SL], at_q[:, bass.ds(k, 1), :], at_i[:, bass.ds(k, 1), :, :], start=start, stop=stop)

            add_tile(0, True, False)
            with pe.Fori(1, TILES - 1) as k:
                add_tile(k, False, False)
            add_tile(TILES - 1, False, True).then_inc(rt_slots, 1)
            pe.wait_ge(ld_experts, 16 * (EXPERTS + 4))
            pe.wait_ge(rt_done, 2)

            def load_expert(t):
                return pe.value_load(expert_ids[0:1, bass.ds(t.n, 1)], min_val=0, max_val=EXPERTS - 1)

            def slot_step(t):
                nxt, prv = t.shift(1), t.shift(-1)
                if slot_valid(t):
                    e = load_expert(t)
                    at_least(pe, fx_ev, t.n + 1)
                    at_least(pe, own_gelu, t.n)
                    for T, W, s in ((fT0[t.par], W1a, 0), (fT1[t.par], W1b, 1)):
                        for b in range(2):
                            last = nc.tensor.matmul(ps[:, 3 + b, 0:384], T, W[:, bass.ds(e, 1), b * 384:(b + 1) * 384], start=s == 0, stop=s == 1)
                    last.then_inc(own1_mm, 1)
                    at_least(pe, com_gelu, t.n)
                    for c in range(FCH):
                        o = ps[:, 1 + c // 3, (c % 3) * P:(c % 3 + 1) * P]
                        nc.tensor.matmul(o, W1a[:, 0, c * P:(c + 1) * P], fT0[t.par], start=True, stop=False)
                        last = nc.tensor.matmul(o, W1b[:, 0, c * P:(c + 1) * P], fT1[t.par], start=False, stop=True)
                    last.then_inc(com1_mm, 1)
                if slot_valid(nxt):
                    pe.wait_ge(f_rows[nxt.r], 16 * (nxt.j + 1))
                    at_least(pe, fx_ev, nxt.n)
                    nc.tensor.transpose(ps[:, 0, 0:P], tok_row[nxt.r][:, 0:DK0], ident[:, :])
                    nc.tensor.transpose(ps[0:DK1, 0, P:2 * P], tok_row[nxt.r][:, DK0:D], ident[:, :]).then_inc(fx_mm, 1)
                if slot_valid(prv):
                    ep = load_expert(prv)
                    at_least(pe, gT_ev, prv.n + 1)
                    at_least(pe, com_gelu, prv.n + 1)
                    at_least(pe, mix_done, prv.n)
                    for c in range(FCH):
                        nc.tensor.matmul(ps[:, 7, 0:D], g_common[prv.par][:, c, :], W2s[:, 0, c, :], start=c == 0, stop=False)
                    nc.tensor.matmul(ps[:, 7, 0:D], ones[0:1, :], b2r[:, 0, :], start=False, stop=True)
                    for c in range(FCH):
                        nc.tensor.matmul(ps[:, 7, D:2 * D], g_own[prv.par][:, c, :], W2s[:, bass.ds(ep, 1), c, :], start=c == 0, stop=False)
                    nc.tensor.matmul(ps[:, 7, D:2 * D], ones[0:1, :], b2r[:, bass.ds(ep, 1), :], start=False, stop=True).then_inc(two_mm, 1)
                if slot_valid(t):
                    at_least(pe, own_gelu, t.n + 1)
                    at_least(pe, gT_ev, t.n)
                    for c in range(FCH):
                        last = nc.tensor.transpose(ps[:, 5 + c // 3, (c % 3) * P:(c % 3 + 1) * P], g_tok[:, c * P:(c + 1) * P], ident[:, :])
                    last.then_inc(gT_mm, 1)

            slot_pipeline(pe, slot_step)


_INS = ['x', 'txt', 'L0_tok_W', 'L0_tok_b', 'L0_attn_W_in', 'L0_attn_conv_w', 'L0_attn_conv_b', 'L0_attn_dt_bias',
        'L0_attn_A_log', 'L0_attn_D', 'L0_attn_norm_w', 'L0_attn_W_out', 'L0_ffn_Ws', 'L0_ffn_bs', 'L0_ffn_W1',
        'L0_ffn_b1', 'L0_ffn_W2', 'L0_ffn_b2']
_OUTS = [((TIMES, POSITIONS, D), 'float32')]


def kernel(**inputs):
    import numpy as _np
    import concourse.bacc as _bacc
    from concourse import mybir as _mybir
    from concourse.bass_utils import run_bass_kernel_spmd as _run

    nc = _bacc.Bacc("TRN2", target_bir_lowering=False, num_devices=1)
    arrays, args = {}, []
    for name in _INS:
        a = _np.ascontiguousarray(inputs[name])
        arrays[f"in_{name}_dram"] = a
        args.append(nc.dram_tensor(f"in_{name}_dram", a.shape, _mybir.dt.from_np(a.dtype), kind="ExternalInput").ap())
    for i, (shape, dtype) in enumerate(_OUTS):
        dt = _mybir.dt.from_np(_np.dtype(dtype))
        args.append(nc.dram_tensor(f"out_{i}_dram", shape, dt, kind="ExternalOutput").ap())
    build_kernel(nc, *args)
    r = _run(nc, [arrays], core_ids=[0])
    return r.results[0]["out_0_dram"]
```

```python
import numpy as np
from contextlib import ExitStack

import concourse.bass as bass
from concourse import mybir

TIMES = 16
N_PATCH = 196
N_TEXT = 512
POSITIONS = N_PATCH + N_TEXT
D = 192
DK0 = 128
DK1 = D - DK0
P = 128
POS_TILE = P // TIMES
GT = 3
GROUPS = -(-POSITIONS // (POS_TILE * GT))
TILES = GROUPS * GT
TOKENS = POSITIONS * TIMES
ROWS = TILES * P
D_INNER = 384
HEADS = 6
HEADDIM = 64
D_STATE = 64
PIX = 768
EXPERTS = 9
D_FF = 768
FCH = D_FF // P
SLOT_TILES = TOKENS // P + EXPERTS
ROW_W = 2 * D + 1
EPS = 1e-5
LOG1P_TERMS = 8
X_SCALE = 2.0 ** 10
PK = 2 * D
E_ROWS = DK1 + 2


class Group:

    def __init__(self, j, r, cycle=2):
        self.j, self.r, self.cycle = j, r, cycle
        self.par = r % 2

    @property
    def n(self):
        return self.j * self.cycle + self.r

    def shift(self, d):
        q = self.r + d
        return Group(self.j + q // self.cycle, q % self.cycle, self.cycle)


def at_least(eng, sem, value):
    if isinstance(value, int) and value <= 0:
        return
    eng.wait_ge(sem, value)


def settle(eng, always):
    eng.sem_inc(always, 1)


class Chain:

    def __init__(self, eng, sem, n, per):
        self.eng, self.sem, self.n, self.per, self.k = eng, sem, n, per, 0

    def step(self, ins):
        self.k += 1
        ins.then_inc(self.sem, 1)

    def sync(self):
        at_least(self.eng, self.sem, self.n * self.per + self.k)

    def link(self, ins):
        self.step(ins)
        self.sync()

    def done(self):
        assert self.k == self.per, (self.k, self.per)


def build_kernel(nc, x, txt, tok_W, tok_b, W_in, conv_w, conv_b, dt_bias, A_log, D_skip, norm_w, W_out,
                 Ws, bs, W1, b1, W2, b2, out):
    f32, bf16, f16, i32 = mybir.dt.float32, mybir.dt.bfloat16, mybir.dt.float16, mybir.dt.int32
    ALU, ACT, AX = mybir.AluOpType, mybir.ActivationFunctionType, mybir.AxisListType

    h_rows = nc.dram_tensor("h_rows", (ROWS, D), f32).ap()
    ffn_rows = nc.dram_tensor("ffn_rows", (ROWS, ROW_W), f32).ap()
    b1_rows = nc.dram_tensor("b1_rows", (2, EXPERTS * D_FF), f16).ap()
    b2_rows = nc.dram_tensor("b2_rows", (2, EXPERTS * D), f16).ap()

    ctx = ExitStack()
    with ctx:
        def sb(name, shape, dt=f32):
            return ctx.enter_context(nc.sbuf_tensor(name, shape, dt))

        def sem(name):
            return ctx.enter_context(nc.semaphore(name))

        def sems(name, n):
            return [sem(f"{name}{i}") for i in range(n)]

        ident = sb("ident", [P, P])
        later = sb("later", [P, P])
        causal = sb("causal", [P, P])
        causal16 = sb("causal16", [P, TIMES])
        ones = sb("ones", [P, P])
        earlier_rows = sb("earlier_rows", [P, P])
        minus_half = sb("minus_half", [P, 4])
        iota9p9 = sb("iota9p9", [P, EXPERTS])
        tok_b_bc = sb("tok_b_bc", [P, D])
        neg_A = sb("neg_A", [P, HEADS])
        D_bc = sb("D_bc", [P, HEADS])
        small_in = sb("small_in", [P, 16])
        ident_h = sb("ident_h", [P, P], f16)
        magnitude, magnitude_all, bits, scale, inverse = [sb(n, [P, 3]) for n in
                                                          ("magnitude", "magnitude_all", "bits", "scale", "inverse")]
        inv_h, inv_out, g_scale, neg_inv_out, inv_logit = [sb(n, [P, 1]) for n in
                                                           ("inv_h", "inv_out", "g_scale", "neg_inv_out", "inv_logit")]
        sizes, sizes2 = sb("sizes", [P, EXPERTS + 1]), sb("sizes2", [P, EXPERTS + 1])
        g_scale_row = sb("g_scale_row", [2, P], f16)
        PROJ = 2 * D_INNER + HEADS
        IN_W = PROJ + 2 * D_STATE
        Wa = sb("Wa", [P, IN_W])
        Wb = sb("Wb", [DK1 + 1, IN_W])
        Wo = sb("Wo", [P, 3, D])
        ws_in = sb("ws_in", [P, 2 * EXPERTS])
        bs_in = sb("bs_in", [1, EXPERTS])
        bs_h = sb("bs_h", [1, 2 * EXPERTS], f16)
        WsA, WsB, WsD, WsE = [sb(n, [P, EXPERTS], f16) for n in ("WsA", "WsB", "WsD", "WsE")]
        routes = sb("routes", [P, TILES])
        E1W = EXPERTS * D_FF
        E2W = EXPERTS * FCH * D
        w_all = sb("w_all", [P, 2 * E1W + E2W])
        w_h = w_all[:, :].bitcast(f16)
        W1A, W1B, W1D, W1E = [w_h[:, i * E1W:(i + 1) * E1W].rearrange("p (e f) -> p e f", e=EXPERTS) for i in range(4)]
        W2hi, W2lo = [w_h[:, 4 * E1W + i * E2W:4 * E1W + (i + 1) * E2W].rearrange("p (e c d) -> p e c d", e=EXPERTS, c=FCH)
                      for i in range(2)]
        b2h = sb("b2h", [2, EXPERTS, D], f16)
        B1C, B2R = E1W // P, 16
        b1_in, b1_hi, b1_lo = sb("b1_in", [P, B1C]), sb("b1_hi", [P, B1C], f16), sb("b1_lo", [P, B1C], f16)
        B2P = EXPERTS * D // B2R
        b2_in, b2_hi, b2_lo = sb("b2_in", [B2P, B2R]), sb("b2_hi", [B2P, B2R], f16), sb("b2_lo", [B2P, B2R], f16)
        HALF = 8 * 224
        RB = 2 * 3 * 14
        ET = N_PATCH // 2
        pix = [w_all[0:RB, u * HALF:(u + 1) * HALF] for u in range(2)]
        pix_by_patch = [w_all[0:RB, (2 + u) * HALF:(3 + u) * HALF] for u in range(2)]
        o = 4 * HALF
        hp = [w_all[0:ET, o + u * 2 * D:o + (u + 1) * 2 * D].rearrange("p (f d) -> p f d", f=2) for u in range(2)]
        zeros = w_all[:, o + 4 * D:o + 6 * D]
        patch_W = w_all[0:96, o + 6 * D:o + 6 * D + 2 * PIX].rearrange("p (a k) -> p a k", a=2)
        o += 6 * D + 2 * PIX
        conv_bc = w_all[:, o:o + 2048]
        nw = w_all[:, o + 2048:o + 2051]
        STAGE = 2 * D_FF + FCH * D
        ARENA = STAGE + 21260
        arena = sb("arena", [P, ARENA])
        stage = arena[:, 0:STAGE]
        XTW = RB * 14
        XT = [[arena[:, STAGE + (2 * r + u) * XTW:STAGE + (2 * r + u + 1) * XTW] for u in range(2)] for r in range(2)]
        patch_WT = arena[:, STAGE + 4 * XTW:STAGE + 4 * XTW + 6 * D].rearrange("p (c i d) -> p c i d", c=3, i=2)

        class Area:
            def __init__(self, at=0):
                self.at = at

            def take(self, size, parts=P):
                a = arena[0:parts, self.at:self.at + size]
                self.at += size
                assert self.at <= ARENA, self.at
                return a

        ar = Area(STAGE)
        k3 = lambda ap, w: ap.rearrange("p (k w) -> p k w", w=w)
        h_in = [k3(ar.take(GT * D), D) for _ in range(2)]
        xn = [k3(ar.take(GT * D), D) for _ in range(2)]
        xT0 = [ar.take(GT * P) for _ in range(2)]
        xT1 = [ar.take(GT * P, DK1 + 1) for _ in range(2)]
        zs = [k3(ar.take(GT * D_INNER), D_INNER) for _ in range(2)]
        xs = [k3(ar.take(GT * D_INNER), D_INNER) for _ in range(2)]
        Bs = [ar.take(GT * P, D_STATE) for _ in range(2)]
        Cs = [ar.take(GT * P, D_STATE) for _ in range(2)]
        rows_flat = [ar.take(GT * ROW_W) for _ in range(2)]
        rows = [k3(r, ROW_W) for r in rows_flat]
        rows_h = [k3(r.bitcast(f16), 2 * ROW_W) for r in rows_flat]
        n2 = k3(ar.take(GT * D), D)
        nAC = ar.take(GT * P).bitcast(f16).rearrange("p (a k t) -> p a k t", a=2, k=GT)
        nD = ar.take(GT * P // 2).bitcast(f16).rearrange("p (k t) -> p k t", k=GT)
        nE = ar.take(GT * P // 2).bitcast(f16).rearrange("p (k t) -> p k t", k=GT)
        decay_in = ar.take(GT * HEADS * TIMES)
        decay = ar.take(GT * HEADS * TIMES)
        G_m = k3(ar.take(GT * P), P)
        M_all = ar.take(GT * HEADS * P).rearrange("p (k h t) -> p k h t", k=GT, h=HEADS)
        xD = k3(ar.take(GT * D_INNER), D_INNER)
        y = k3(ar.take(GT * D_INNER), D_INNER)
        yT = k3(ar.take(GT * D_INNER), D_INNER)
        sq = ar.take(D_INNER)
        st1 = ar.take(GT * 6)
        mv1 = ar.take(GT * 2)
        var1 = ar.take(GT)
        rs1 = ar.take(GT)
        st2 = ar.take(GT * 6)
        mv2 = ar.take(GT * 2)
        var2 = ar.take(GT)
        rs2 = ar.take(GT)
        ssq = ar.take(GT)
        ms = ar.take(GT)
        rsy = ar.take(GT)
        SH = GT * HEADS
        dtv, nabs, u_, den, rec, s_, w_, ser, relu, dts, a_ = [ar.take(SH) for _ in range(11)]
        lmax, rsum, rrec, pmax = [ar.take(GT) for _ in range(4)]
        ld_, le_, pr_, eq_, cand = [ar.take(GT * EXPERTS) for _ in range(5)]

        rt = Area()
        onehot = rt.take(EXPERTS * TILES).rearrange("p (e k) -> p e k", e=EXPERTS)
        running = rt.take(EXPERTS * TILES)
        no_add = rt.take(EXPERTS * TILES)
        to_slot = rt.take(EXPERTS * TILES).rearrange("p (e k) -> p e k", e=EXPERTS)
        iota_q = rt.take(P)
        iota_i = rt.take(SLOT_TILES)
        row_p1 = rt.take(1)
        seg0, count, before, total_e, tiles_e, tile_end, slot0 = [rt.take(EXPERTS) for _ in range(7)]
        slot, slot_q, slot_i, is_pad = [rt.take(TILES) for _ in range(4)]
        at_q = rt.take(TILES * P // 2).bitcast(bf16).rearrange("p (k q) -> p k q", q=P)
        at_i = rt.take(TILES * SLOT_TILES).bitcast(bf16).rearrange("p (k t i) -> p k t i", t=2, i=SLOT_TILES)
        SL = SLOT_TILES
        sums, = [rt.take(2 * SL)]
        row_f, empty, time_f, past = rt.take(SL), rt.take(SL), rt.take(SL), rt.take(SL * EXPERTS).rearrange("p (i e) -> p i e", e=EXPERTS)
        expert_f = rt.take(SL)
        ints = [rt.take(TILES).bitcast(i32) for _ in range(3)]
        cnt_i = rt.take(EXPERTS).bitcast(i32)
        row_ids = rt.take(SL).bitcast(i32)
        row_tmp = rt.take(SL).bitcast(i32)
        out_ids = rt.take(SL).bitcast(i32)
        expert_ids = rt.take(SL).bitcast(i32)
        ex = Area()
        tok_row = [ex.take(ROW_W) for _ in range(4)]
        tok_h = [t.bitcast(f16) for t in tok_row]
        fT = [ex.take(3 * P // 2).bitcast(f16) for _ in range(2)]
        fE = [ex.take(P // 2).bitcast(f16) for _ in range(2)]
        g32 = [ex.take(D_FF) for _ in range(2)]
        g_hi, g_lo = [[[ex.take(D_FF // 2).bitcast(f16) for _ in range(2)] for _ in range(2)] for _ in range(2)]
        mixed = [ex.take(D) for _ in range(2)]
        w_common, w_own = [[ex.take(1) for _ in range(2)] for _ in range(2)]
        ids_in = ex.take(4).bitcast(i32)
        ids_out = ex.take(4).bitcast(i32)
        assert ex.at < TILES * EXPERTS * 4 + P + 600 + TILES * (P + SL) // 2

        ps = ctx.enter_context(nc.psum_tensor("ps", [P, 8, 512], f32))

        ld_w = sem("ld_w")
        ld_pw = sem("ld_pw")
        ld_tb = sem("ld_tb")
        st_b = sem("st_b")
        ld_stage = sem("ld_stage")
        ld_b = sem("ld_b")
        mx_v = sem("mx_v")
        mx_done = sem("mx_done")
        sc_v = sem("sc_v")
        sc_g = sem("sc_g")
        cv_hi = sem("cv_hi")
        cv_lo = sem("cv_lo")
        bias_v = sem("bias_v")
        ld_pix = sems("ld_pix", 2)
        txt_copied = sem("txt_copied")
        pad_zeroed = sem("pad_zeroed")
        ld_experts = sem("ld_experts")
        settled_v, settled_g = sem("settled_v"), sem("settled_g")
        prep_v = sem("prep_v")
        prep_g = sem("prep_g")
        prep_a = sem("prep_a")
        prep_pe = sem("prep_pe")
        pix_cut = sem("pix_cut")
        pix_T = sem("pix_T")
        pix_ev_a = sem("pix_ev_a")
        pix_ev_v = sem("pix_ev_v")
        emb_mm = sem("emb_mm")
        emb_v = sem("emb_v")
        st_emb = sems("st_emb", 2)

        ld_h = sems("ld_h", 2)
        ld_res = sems("ld_res", 2)
        ln1_c = sem("ln1_c")
        ln1_p = sem("ln1_p")
        xn_done = sem("xn_done")
        t1_mm = sem("t1_mm")
        t1_ev = sem("t1_ev")
        proj_mm = sem("proj_mm")
        th_done = sem("th_done")
        silu_done = sem("silu_done")
        dt_c = sem("dt_c")
        u_done = sem("u_done")
        dts_done = sem("dts_done")
        dec_in_done = sem("dec_in_done")
        L_mm = sem("L_mm")
        E_done = sem("E_done")
        dec_done = sem("dec_done")
        G_mm = sem("G_mm")
        Gm_done = sem("Gm_done")
        M_v = sem("M_v")
        M_g = sem("M_g")
        xD_done = sem("xD_done")
        y_mm = sem("y_mm")
        y1_done = sem("y1_done")
        y2_done = sem("y2_done")
        sq_done = sem("sq_done")
        t2_mm = sem("t2_mm")
        t2_ev = sem("t2_ev")
        rsy_c = sem("rsy_c")
        o_mm = sem("o_mm")
        h2_done = sem("h2_done")
        ln2_c = sem("ln2_c")
        ln2_p = sem("ln2_p")
        n2_done = sem("n2_done")
        t3_mm = sem("t3_mm")
        t3_ev = sem("t3_ev")
        n2_c = sem("n2_c")
        lg_mm = sem("lg_mm")
        lg_read = sem("lg_read")
        sm_exp = sem("sm_exp")
        sm_c = sem("sm_c")
        row_done = sem("row_done")
        st_rows = sems("st_rows", 2)

        rt_g = sem("rt_g")
        rt_v = sem("rt_v")
        rt_a = sem("rt_a")
        rt_count = sem("rt_count")
        rt_slots = sem("rt_slots")
        rt_done = sem("rt_done")
        f_ids = sem("f_ids")
        f_oids = sem("f_oids")
        f_rows = sems("f_rows", 4)
        f_out = sems("f_out", 4)
        fx_mm = sem("fx_mm")
        fx_ev = sem("fx_ev")
        hid_mm = sem("hid_mm")
        gelu_done = sems("gelu_done", 2)
        hi_done = sems("hi_done", 2)
        lo_done = sems("lo_done", 2)
        two_mm = sem("two_mm")
        mix_c = sem("mix_c")
        mix_done = sem("mix_done")

        block = ctx.enter_context(nc.Block())

        def pair(q):
            return 2 + 2 * (q % 2)

        x_blocks = x.rearrange("b c (h i) w -> (b c h) (i w)", i=16)
        emb_rows = h_rows[0:N_PATCH * TIMES, :].rearrange("(f p b) d -> p b f d", f=2, b=TIMES)
        out_rows = out.rearrange("b n d -> (b n) d")

        N_SMALL_LOADS = 18
        PREP_V = 17
        MX_V = 8
        SC_ROUTER, SC_ALL = 10, 21
        DT_LINKS = 9 + LOG1P_TERMS - 1
        RT_COUNT, RT_SLOT, RT_HOT = 16, 35, 39
        SM_LINKS = 8
        WP_BANKS = ((0, 5), (5, 5), (10, 4))
        T2_BANK = (0, 1, 0)
        Y_BANK = (7, 6, 7)
        O_BANK, O_COL = (1, 1, 0), (0, D, 0)

        def pix_move(group, u, q, w0, nw_):
            src = ps[:, 1 + 3 * u + q, 0:nw_ * RB].rearrange("p (w r) -> p w r", r=RB)
            dst = XT[group.par][u].rearrange("p (r w) -> p w r", w=14)[:, w0:w0 + nw_]
            return dst, src

        def valid(group, total=GROUPS):
            n = group.n
            return not isinstance(n, int) or 0 <= n < total

        LOOP0, LOOP1 = 4, 28
        SLOT_LOOP0, SLOT_LOOP1 = 4, 92

        def pipeline(eng, step, first=-1, loop0=LOOP0, loop1=LOOP1, last=GROUPS + 2, cycle=2):
            for n in range(first, loop0):
                step(Group(n // cycle, n % cycle, cycle))
            with eng.Fori(loop0 // cycle, loop1 // cycle) as j:
                for r in range(cycle):
                    step(Group(j, r, cycle))
            for n in range(loop1, last):
                step(Group(n // cycle, n % cycle, cycle))

        def patch_pipeline(eng, step, between=None):
            step(Group(0, 0))
            step(Group(0, 1))
            if between:
                between()
            with eng.Fori(1, 3) as j:
                step(Group(j, 0))
                step(Group(j, 1))
            for n in range(6, 9):
                step(Group(n // 2, n % 2))

        SPLIT_AT = [-1, 0, 1, 2, 3, LOOP1, LOOP1 + 1, LOOP1 + 2, LOOP1 + 3]

        def split_of(group):
            return SPLIT_AT.index(group.n) if isinstance(group.n, int) else None

        def slot_pipeline(eng, step):
            pipeline(eng, step, -2, SLOT_LOOP0, SLOT_LOOP1, SLOT_TILES + 1, 4)

        def slot_valid(group):
            return valid(group, SLOT_TILES)

        def form_M(eng, k):
            g = G_m[:, k, :].rearrange("p (n j) -> p n j", j=TIMES).unsqueeze(1).to_broadcast([P, HEADS, POS_TILE, TIMES])
            d = decay.rearrange("p (k h j) -> p k h j", k=GT, h=HEADS)[:, k].unsqueeze(2).to_broadcast([P, HEADS, POS_TILE, TIMES])
            return eng.tensor_tensor(M_all[:, k].rearrange("p h (n j) -> p h n j", j=TIMES), g, d, ALU.mult)

        @block.sync
        def _(sp):
            sp.dma_start(patch_W, tok_W.rearrange("(a p) k -> p a k", a=2)).then_inc(ld_pw, 16)
            sp.dma_start(pix[0], x_blocks[0:RB, 0:HALF]).then_inc(ld_pix[0], 16)
            sp.dma_start(pix[1], x_blocks[0:RB, HALF:2 * HALF]).then_inc(ld_pix[1], 16)

            def load_pix(group):
                for u in range(2):
                    row0 = group.n * RB
                    if not isinstance(row0, int):
                        row0 = sp.snap(row0)
                    at_least(sp, pix_cut, group.n * 2 + u - 1)
                    sp.dma_start(pix[u], x_blocks[bass.ds(row0, RB), u * HALF:(u + 1) * HALF]).then_inc(ld_pix[u], 16)

            def load_stage(e):
                one = lambda ap: ap[bass.ds(e, 1)].rearrange("a p f -> p (a f)") if len(ap.shape) == 3 else ap[bass.ds(e, 1)]
                sp.dma_start(stage[:, 0:D_FF], one(W1[:, 0:DK0, :])).then_inc(ld_stage, 16)
                for i in range(2):
                    sp.dma_start(stage[i * DK1:(i + 1) * DK1, D_FF:2 * D_FF], one(W1[:, DK0:D, :])).then_inc(ld_stage, 16)
                sp.dma_start(stage[:, 2 * D_FF:STAGE].rearrange("p (a c d) -> p a c d", a=1, d=D),
                             W2.rearrange("e (c p) d -> p e c d", p=P)[:, bass.ds(e, 1)]).then_inc(ld_stage, 16)

            load_stage(0)
            load_pix(Group(0, 1))

            def patch_step(s):
                nxt, prv = s.shift(2), s.shift(-1)
                if valid(nxt, 8):
                    load_pix(nxt)
                if valid(prv, 8):
                    for b in range(2):
                        entry = prv.n * 2 + b
                        if not isinstance(entry, int):
                            entry = sp.snap(entry)
                        at_least(sp, emb_v, 2 * prv.n + b + 1)
                        sp.dma_start(emb_rows[:, bass.ds(entry, 1)], hp[b].unsqueeze(1)).then_inc(st_emb[b], 16)
                e = s.shift(1).n
                if not isinstance(e, int):
                    e = sp.snap(e)
                at_least(sp, mx_done, s.n + 1)
                load_stage(e if not isinstance(e, int) or e < EXPERTS else 0)

            patch_pipeline(sp, patch_step)
            sp.wait_ge(pad_zeroed, 16)
            sp.wait_ge(st_emb[0], 16 * 8)
            sp.wait_ge(st_emb[1], 16 * 8)
            sp.wait_ge(txt_copied, 16)

            def load_rows(dst, group, s):
                row0 = group.n * (GT * P)
                if not isinstance(row0, int):
                    row0 = sp.snap(row0)
                return dst, row0, s

            def load_h(group):
                dst, row0, s = load_rows(h_in[group.par], group, ld_h)
                at_least(sp, xn_done, 3 * (group.n - 1))
                sp.dma_start(dst, h_rows[bass.ds(row0, GT * P), :].rearrange("(k p) d -> p k d", p=P)).then_inc(ld_h[group.par], 16)

            def load_res(group):
                dst, row0, s = load_rows(rows[group.par][:, :, D:2 * D], group, ld_res)
                at_least(sp, st_rows[group.par], 16 * group.j)
                sp.dma_start(dst, h_rows[bass.ds(row0, GT * P), :].rearrange("(k p) d -> p k d", p=P)).then_inc(ld_res[group.par], 16)

            def store_rows(group):
                row0 = group.n * (GT * P)
                if not isinstance(row0, int):
                    row0 = sp.snap(row0)
                at_least(sp, row_done, group.n + 1)
                sp.dma_start(ffn_rows[bass.ds(row0, GT * P), :].rearrange("(k p) d -> p k d", p=P), rows[group.par]).then_inc(st_rows[group.par], 16)

            def step(group):
                if valid(group.shift(2)):
                    load_h(group.shift(2))
                if valid(group.shift(-2)):
                    store_rows(group.shift(-2))
                if valid(group):
                    load_res(group)
                e = split_of(group)
                if e is not None:
                    if e + 1 < EXPERTS:
                        sp.wait_ge(cv_hi, e + 1)
                        sp.wait_ge(cv_lo, e + 1)
                        load_stage(e + 1)
                if e == 1:
                    sp.wait_ge(bias_v, 4)
                    for r, (one, two) in enumerate(((b1_hi, b2_hi), (b1_lo, b2_lo))):
                        sp.dma_start(b1_rows[r].rearrange("(p c) -> p c", c=B1C), one[:, :]).then_inc(st_b, 16)
                        sp.dma_start(b2_rows[r].rearrange("(p c) -> p c", c=B2R), two[:, :]).then_inc(st_b, 16)
                    sp.wait_ge(st_b, 64)
                    sp.dma_start(W1E[DK1:E_ROWS, :, :].rearrange("a e f -> a (e f)"), b1_rows).then_inc(ld_experts, 16)
                    sp.dma_start(b2h[:, :, :].rearrange("a e f -> a (e f)"), b2_rows).then_inc(ld_experts, 16)

            load_h(Group(0, 0))
            pipeline(sp, step)

            for r in range(4):
                sp.wait_ge(f_out[r], 16 * ((SLOT_TILES - r + 3) // 4))

        @block.gpsimd
        def _(pool):
            pool.memset(zeros, 0.0).then_inc(prep_g, 1)
            pool.memset(ident[:, :], 0.0).then_inc(prep_g, 1)
            pool.wait_ge(prep_g, 2)
            pool.affine_select(out=ident[:, :], in_=ident[:, :], compare_op=ALU.not_equal, fill=1.0, base=0,
                               pattern=[[-1, P]], channel_multiplier=1).then_inc(prep_g, 1)
            pool.memset(later[:, :], 1.0).then_inc(prep_g, 1)
            pool.memset(causal[:, :], 1.0).then_inc(prep_g, 1)
            pool.memset(minus_half[:, :], -0.5).then_inc(prep_g, 1)
            pool.wait_ge(prep_g, 6)
            pool.tensor_copy(ident_h[:, :], ident[:, :]).then_inc(prep_g, 1)
            pool.dma_start(h_rows[TOKENS:ROWS, :].rearrange("(p a) d -> p (a d)", p=96),
                           zeros[0:96, :]).then_inc(pad_zeroed, 16)
            blocks = [[-TIMES, POS_TILE], [0, TIMES]]
            up_blocks = [[TIMES, POS_TILE], [0, TIMES]]
            pool.affine_select(out=later[:, :], in_=later[:, :], compare_op=ALU.is_gt, fill=0.0, base=0,
                               pattern=[[-1, P]], channel_multiplier=1).then_inc(prep_g, 1)
            pool.affine_select(out=causal[:, :], in_=causal[:, :], compare_op=ALU.is_ge, fill=0.0, base=0,
                               pattern=[[1, P]], channel_multiplier=-1).then_inc(prep_g, 1)
            pool.wait_ge(prep_g, 9)
            pool.affine_select(out=later[:, :], in_=later[:, :], compare_op=ALU.is_ge, fill=0.0, base=TIMES - 1,
                               pattern=up_blocks, channel_multiplier=-1).then_inc(prep_g, 1)
            pool.affine_select(out=causal[:, :], in_=causal[:, :], compare_op=ALU.is_ge, fill=0.0, base=0,
                               pattern=blocks, channel_multiplier=1).then_inc(prep_g, 1)
            pool.iota(iota9p9[:, :], [[1, EXPERTS]], base=9, channel_multiplier=0,
                      allow_small_or_imprecise_dtypes=True).then_inc(prep_g, 1)

            pool.wait_ge(ld_pix[1], 16)
            pool.dma_start(h_rows[N_PATCH * TIMES:TOKENS, :].rearrange("(n b) d -> n b d", b=TIMES),
                           txt.rearrange("b n d -> n b d")).then_inc(txt_copied, 16)
            RMAX = bass.bass_isa.ReduceOp.max
            pool.wait_ge(mx_v, 3)
            pool.partition_all_reduce(magnitude_all[:, 0:1], magnitude[:, 0:1], P, RMAX).then_inc(sc_g, 1)
            pool.wait_ge(mx_v, MX_V)
            pool.partition_all_reduce(magnitude_all[:, 1:3], magnitude[:, 1:3], P, RMAX).then_inc(sc_g, 1)

            def power(src, dst, sem_, group, scale, ready, count, times=1.0):
                ch = Chain(pool, sem_, group.n, 2)
                at_least(pool, ready, count)
                settle(pool, settled_g)
                tmp = {id(rs1): var1, id(rs2): var2, id(rsy): ms}[id(dst)]
                ch.link(pool.tensor_scalar(tmp, src, scale / times ** 2, EPS / times ** 2, ALU.mult, ALU.add))
                ch.step(pool.tensor_tensor(dst, tmp, minus_half[:, 0:GT], ALU.pow))
                ch.done()

            def step(group):
                nxt, prv = group.shift(1), group.shift(-1)
                if valid(nxt):
                    power(mv1.rearrange("p (k s) -> p s k", s=2)[:, 1, :], rs1, ln1_p, nxt, 1.0, ln1_c, 6 * (nxt.n + 1))
                if valid(prv):
                    power(ssq, rsy, rsy_c, prv, 1.0 / D_INNER, sq_done, 3 * (prv.n + 1))
                if valid(group):
                    at_least(pool, silu_done, 4 * group.n + 3)
                    at_least(pool, y1_done, 3 * group.n)
                    v = lambda t: t.rearrange("p k (h e) -> p k h e", h=HEADS)
                    for k in range(GT):
                        ins = pool.tensor_tensor(
                            xD[:, k, :].rearrange("p (h e) -> p h e", h=HEADS),
                            xs[group.par][:, k, :].rearrange("p (h e) -> p h e", h=HEADS),
                            D_bc[:, :].unsqueeze(2).to_broadcast([P, HEADS, HEADDIM]), ALU.mult)
                    ins.then_inc(xD_done, 1)
                    at_least(pool, dec_done, group.n + 1)
                    at_least(pool, Gm_done, group.n + 1)
                    at_least(pool, y_mm, 3 * group.n)
                    form_M(pool, 2).then_inc(M_g, 1)
                if valid(prv):
                    power(mv2.rearrange("p (k s) -> p s k", s=2)[:, 1, :], rs2, ln2_p, prv, 1.0, ln2_c, 6 * (prv.n + 1), X_SCALE)

            pipeline(pool, step)

            pool.wait_ge(st_rows[0], 16 * (GROUPS // 2))
            pool.wait_ge(st_rows[1], 16 * (GROUPS // 2))
            pool.iota(iota_q, [[1, P]], base=0, channel_multiplier=0, allow_small_or_imprecise_dtypes=True).then_inc(rt_g, 1)
            pool.iota(iota_i, [[1, SL]], base=0, channel_multiplier=0, allow_small_or_imprecise_dtypes=True).then_inc(rt_g, 1)
            pool.iota(row_p1, [[1, 1]], base=1, channel_multiplier=1, allow_small_or_imprecise_dtypes=True).then_inc(rt_g, 1)
            pool.memset(earlier_rows[:, :], 1.0).then_inc(rt_g, 1)
            pool.wait_ge(rt_g, 4)
            pool.affine_select(out=earlier_rows[:, :], in_=earlier_rows[:, :], compare_op=ALU.is_gt, fill=0.0, base=0,
                               pattern=[[1, P]], channel_multiplier=-1).then_inc(rt_g, 1)
            pool.wait_ge(rt_done, 1)

            def gather(t):
                at_least(pool, mix_done, t.n - 3)
                settle(pool, settled_g)
                pool.tensor_copy(ids_in[:, t.r:t.r + 1], row_ids[:, bass.ds(t.n, 1)]).then_inc(f_ids, 1)
                pool.wait_ge(f_ids, t.n + 1)
                settle(pool, settled_g)
                pool.indirect_dma_start(tok_row[t.r], None, ffn_rows,
                                        bass.IndirectOffsetOnAxis(ap=ids_in[:, t.r:t.r + 1], axis=0),
                                        bounds_check=ROWS - 1, oob_is_err=False).then_inc(f_rows[t.r], 16)

            def scatter(t):
                at_least(pool, f_out[t.r], 16 * t.j)
                settle(pool, settled_g)
                pool.tensor_copy(ids_out[:, t.r:t.r + 1], out_ids[:, bass.ds(t.n, 1)]).then_inc(f_oids, 1)
                pool.wait_ge(f_oids, t.n + 1)
                pool.wait_ge(mix_done, t.n + 1)
                settle(pool, settled_g)
                pool.indirect_dma_start(out_rows, bass.IndirectOffsetOnAxis(ap=ids_out[:, t.r:t.r + 1], axis=0),
                                        mixed[t.par], None,
                                        bounds_check=TOKENS - 1, oob_is_err=False).then_inc(f_out[t.r], 16)

            def slot_step(t):
                if slot_valid(t.shift(2)):
                    gather(t.shift(2))
                if slot_valid(t.shift(-1)):
                    scatter(t.shift(-1))

            slot_pipeline(pool, slot_step)
        @block.scalar
        def _(act):
            act.dma_start(tok_b_bc[:, :], tok_b.rearrange("(a d) -> a d", a=1).to_broadcast([P, D])).then_inc(ld_tb, 16)
            act.dma_start(conv_bc, conv_w.rearrange("(a c) k -> a (c k)", a=1).to_broadcast([P, 2048])).then_inc(ld_w, 16)
            for dst, rows_ in ((Wa[:, :], W_in[0:DK0, :]), (Wb[0:DK1, :], W_in[DK0:D, :])):
                act.dma_start(dst[:, 0:768], rows_[:, 0:768]).then_inc(ld_w, 16)
                act.dma_start(dst[:, PROJ:IN_W], rows_[:, 768:896]).then_inc(ld_w, 16)
                act.dma_start(dst[:, 768:PROJ], rows_[:, 896:902]).then_inc(ld_w, 16)
            cb = conv_b.rearrange("(a c) -> a c", a=1)
            act.dma_start(Wb[DK1:DK1 + 1, 384:768], cb[:, 0:384]).then_inc(ld_w, 16)
            act.dma_start(Wb[DK1:DK1 + 1, PROJ:IN_W], cb[:, 384:512]).then_inc(ld_w, 16)
            act.dma_start(Wb[DK1:DK1 + 1, 768:PROJ], dt_bias.rearrange("(a c) -> a c", a=1)).then_inc(ld_w, 16)
            act.dma_start(small_in[:, 0:6], A_log.rearrange("(a c) -> a c", a=1).to_broadcast([P, 6])).then_inc(ld_w, 16)
            act.dma_start(D_bc[:, :], D_skip.rearrange("(a c) -> a c", a=1).to_broadcast([P, 6])).then_inc(ld_w, 16)
            act.dma_start(Wo[:, :, :], W_out.rearrange("(c p) d -> p c d", p=P)).then_inc(ld_w, 16)
            act.dma_start(ws_in[:, 0:EXPERTS], Ws[0:DK0, :]).then_inc(ld_w, 16)
            for i in range(2):
                act.dma_start(ws_in[i * DK1:(i + 1) * DK1, EXPERTS:2 * EXPERTS], Ws[DK0:D, :]).then_inc(ld_w, 16)
            act.dma_start(bs_in[:, :], bs.rearrange("(a c) -> a c", a=1)).then_inc(ld_w, 16)
            act.dma_start(nw, norm_w.rearrange("(c p) -> p c", p=P), allow_slow_non_contiguous=True).then_inc(ld_w, 16)
            act.dma_start(b1_in[:, :], b1.rearrange("e f -> (e f)").rearrange("(p c) -> p c", c=B1C)).then_inc(ld_b, 16)
            act.dma_start(b2_in[:, :], b2.rearrange("e f -> (e f)").rearrange("(p c) -> p c", c=B2R)).then_inc(ld_b, 16)

            def between():
                act.wait_ge(ld_w, 16 * N_SMALL_LOADS)
                act.activation(neg_A[:, :], small_in[:, 0:6], ACT.Exp).then_inc(prep_a, 1)
                act.wait_ge(bias_v, 2)
                for r in range(2):
                    act.dma_start(WsE[DK1 + r:DK1 + r + 1, :], bs_h[:, r * EXPERTS:(r + 1) * EXPERTS]).then_inc(ld_w, 16)

            def patch_step(s):
                if valid(s, 8):
                    for u in range(2):
                        act.wait_ge(pix_T, s.n * 2 + u + 1)
                        at_least(act, emb_mm, 2 * (s.n - 1))
                        act.activation(*pix_move(s, u, 0, *WP_BANKS[0]), ACT.Copy).then_inc(pix_ev_a, 1)

            patch_pipeline(act, patch_step, between)

            def step(group):
                nxt, prv, pp = group.shift(1), group.shift(-1), group.shift(-2)
                par = group.par

                def tanh(q):
                    at_least(act, proj_mm, 4 * group.n + q + 1)
                    b = pair(q)
                    if q < 3:
                        act.activation(zs[par][:, q, :], ps[:, b, 0:384], ACT.Tanh)
                        act.activation(xs[par][:, q, :], ps[:, b + 1, 0:384], ACT.Tanh).then_inc(th_done, 1)
                    else:
                        act.activation(Bs[par], ps[0:D_STATE, b, 0:384], ACT.Tanh)
                        act.activation(Cs[par], ps[0:D_STATE, b + 1, 0:384], ACT.Tanh).then_inc(th_done, 1)

                if valid(group):
                    at_least(act, y2_done, 3 * (group.n - 1))
                    at_least(act, y_mm, 3 * (group.n - 1))
                    at_least(act, G_mm, group.n - 1)
                    tanh(0)
                    tanh(1)
                if valid(pp):
                    at_least(act, t3_mm, pp.n + 1)
                    at_least(act, lg_mm, pp.n)
                    act.activation(nAC, ps[:, 0, 0:384].bitcast(f16).rearrange("p (a k t) -> p a k t", a=2, k=GT), ACT.Copy).then_inc(t3_ev, 1)
                    nDp = ps[:, 1, 0:192].bitcast(f16).rearrange("p (k t) -> p k t", k=GT)
                    act.activation(nD, nDp, ACT.Copy).then_inc(t3_ev, 1)
                    act.activation(nE[0:DK1], nDp[0:DK1], ACT.Copy).then_inc(t3_ev, 1)
                if valid(group):
                    tanh(2)
                    tanh(3)
                    at_least(act, dt_c, DT_LINKS * group.n + 1)
                    act.activation(u_, nabs, ACT.Exp).then_inc(u_done, 1)
                if valid(pp):
                    at_least(act, lg_read, pp.n + 1)
                    act.activation(le_, ld_, ACT.Exp, scale=inv_logit[:, 0:1]).then_inc(sm_exp, 1)
                if valid(nxt):
                    at_least(act, t1_mm, nxt.n + 1)
                    at_least(act, proj_mm, 4 * (nxt.n - 1))
                    act.activation(xT0[nxt.par], ps[:, 0, 0:384], ACT.Copy).then_inc(t1_ev, 1)
                    act.activation(xT1[nxt.par][0:DK1, :], ps[0:DK1, 1, 0:384], ACT.Copy).then_inc(t1_ev, 1)
                if valid(prv):
                    for k in range(GT):
                        at_least(act, y2_done, 3 * prv.n + k + 1)
                        if k == 0:
                            at_least(act, rsy_c, 2 * prv.n)
                        at_least(act, sq_done, 3 * prv.n + k)
                        act.activation(sq, y[:, k, :], ACT.Square, accum_out=ssq[:, k:k + 1]).then_inc(sq_done, 1)
                        at_least(act, t2_mm, 3 * prv.n + k + 1)
                        at_least(act, o_mm, 3 * prv.n)
                        act.activation(yT[:, k, :], ps[:, T2_BANK[k], 0:384], ACT.Copy).then_inc(t2_ev, 1)
                if valid(group):
                    at_least(act, L_mm, group.n + 1)
                    at_least(act, M_v, 2 * group.n)
                    at_least(act, M_g, group.n)
                    act.activation(decay, ps[:, 6, 0:GT * HEADS * TIMES], ACT.Exp).then_inc(E_done, 1)
                e = split_of(group)
                if e is not None:
                    act.wait_ge(ld_stage, 64 * (EXPERTS + e + 1))
                    act.wait_ge(sc_v, SC_ALL)
                    act.activation(W1A[:, e, :], stage[:, 0:D_FF], ACT.Identity, scale=scale[:, 1:2])
                    act.activation(W1D[:, e, :], stage[:, D_FF:2 * D_FF], ACT.Identity, scale=scale[:, 1:2])
                    act.activation(W2hi[:, e].rearrange("p c d -> p (c d)"), stage[:, 2 * D_FF:STAGE], ACT.Identity, scale=scale[:, 2:3]).then_inc(cv_hi, 1)

            pipeline(act, step)

            act.wait_ge(rt_slots, 1)
            act.activation(sums, ps[:, 0, 0:2 * SL], ACT.Copy).then_inc(rt_a, 1)

            def slot_step(t):
                if slot_valid(t):
                    at_least(act, hid_mm, t.n + 1)
                    for i, bank in enumerate((3, 1)):
                        at_least(act, lo_done[i], t.n)
                        act.activation(g32[i].rearrange("p (b f) -> p b f", b=2), ps[:, bank:bank + 2, 0:384], ACT.Gelu, scale=inv_h[:, 0:1]).then_inc(gelu_done[i], 1)
                        at_least(act, gelu_done[i], t.n + 1)
                        at_least(act, two_mm, t.n - 1)
                        act.activation(g_hi[i][t.par], g32[i], ACT.Identity, scale=g_scale[:, 0:1]).then_inc(hi_done[i], 1)

            slot_pipeline(act, slot_step)

        @block.vector
        def _(dve):
            def cut(group):
                for u in range(2):
                    at_least(dve, ld_pix[u], 16 * (group.n + 1))
                    at_least(dve, pix_T, 2 * group.n + u - 1)
                    dve.tensor_copy(pix_by_patch[u].rearrange("p (w i j) -> p w i j", i=8, j=16),
                                    pix[u].rearrange("p (i w j) -> p w i j", i=8, j=16)).then_inc(pix_cut, 1)
                    if not isinstance(group.n, int) or group.n > 0:
                        move_pixels(group.shift(-1), u)

            def move_pixels(group, u):
                at_least(dve, pix_T, group.n * 2 + u + 1)
                at_least(dve, emb_mm, 2 * (group.n - 1))
                for q in (1, 2):
                    last = dve.tensor_copy(*pix_move(group, u, q, *WP_BANKS[q]))
                last.then_inc(pix_ev_v, 1)

            ch = Chain(dve, prep_v, 0, 0)
            cut(Group(0, 0))
            dve.wait_ge(prep_pe, 1)
            for n, bank in enumerate((0, 7, 4)):
                dve.tensor_copy(patch_WT[:, n], ps[:, bank, 0:2 * D].rearrange("p (i d) -> p i d", i=2)).then_inc(prep_v, 1)
            ch.k = 3

            def set_scales(cols, links):
                c = Chain(dve, sc_v, 0, 0)
                c.k = links
                c.link(dve.tensor_scalar(magnitude_all[:, cols], magnitude_all[:, cols], 2.0 ** -20, 2.0 ** 60, ALU.max, ALU.min))
                c.link(dve.tensor_scalar(bits[:, cols].bitcast(i32), magnitude_all[:, cols].bitcast(i32), 0x7f800000, None, ALU.bitwise_and))
                c.step(dve.tensor_scalar(scale[:, cols].bitcast(i32), bits[:, cols].bitcast(i32), -1.0, float(268 << 23), ALU.mult, ALU.add))
                c.link(dve.tensor_scalar(inverse[:, cols], bits[:, cols], 2.0 ** -14, None, ALU.mult))
                return c

            def between():
                dve.memset(ones[:, :], 1.0)
                dve.wait_ge(ld_w, 16 * N_SMALL_LOADS)
                tap = conv_bc.rearrange("p (c k) -> p c k", k=4)[:, :, 3]
                for W, n in ((Wa, P), (Wb, DK1)):
                    ch.step(dve.tensor_scalar(W[0:n, 0:384], W[0:n, 0:384], 0.5, None, ALU.mult))
                    ch.step(dve.scalar_tensor_tensor(W[0:n, 384:768], W[0:n, 384:768], 0.5, tap[0:n, 0:384], ALU.mult, ALU.mult))
                    ch.step(dve.scalar_tensor_tensor(W[0:n, PROJ:IN_W], W[0:n, PROJ:IN_W], 0.5, tap[0:n, 384:512], ALU.mult, ALU.mult))
                br = Wb[DK1:DK1 + 1, :]
                ch.step(dve.memset(br[:, 0:384], 0.0))
                ch.step(dve.tensor_scalar(br[:, 384:768], br[:, 384:768], 0.5, None, ALU.mult))
                ch.step(dve.tensor_scalar(br[:, PROJ:IN_W], br[:, PROJ:IN_W], 0.5, None, ALU.mult))
                for c in range(3):
                    ch.step(dve.tensor_scalar(Wo[:, c, :], Wo[:, c, :], nw[:, c:c + 1], None, ALU.mult))
                dve.wait_ge(prep_a, 1)
                ch.step(dve.tensor_scalar(neg_A[:, :], neg_A[:, :], -1.0, None, ALU.mult))
                dve.wait_ge(prep_g, 12)
                ch.step(dve.tensor_reduce(causal16[:, :], causal[:, :].rearrange("p (n j) -> p j n", j=TIMES), AX.X, ALU.add))
                mx = Chain(dve, mx_v, 0, 0)
                mx.link(dve.tensor_reduce(magnitude[:, 0:1], ws_in[:, :], AX.X, ALU.max, apply_absolute_value=True))
                mx.link(dve.tensor_reduce(sizes[0:1, 0:1], bs_in[:, :], AX.X, ALU.max, apply_absolute_value=True))
                mx.step(dve.tensor_tensor(magnitude[0:1, 0:1], magnitude[0:1, 0:1], sizes[0:1, 0:1], ALU.max))
                dve.wait_ge(sc_g, 1)
                sc = set_scales(slice(0, 1), 0)
                s0 = scale[:, 0:1]
                sc.step(dve.tensor_scalar(inv_logit[:, :], inverse[:, 0:1], 1.0 / X_SCALE, None, ALU.mult))
                sc.step(dve.tensor_scalar(WsA[:, :], ws_in[:, 0:EXPERTS], s0, None, ALU.mult))
                sc.step(dve.tensor_scalar(WsD[:, :], ws_in[:, EXPERTS:2 * EXPERTS], s0, None, ALU.mult))
                sc.link(dve.tensor_scalar(bs_h[:, 0:EXPERTS], bs_in[:, :], s0[0:1], None, ALU.mult))
                sc.step(dve.scalar_tensor_tensor(WsB[:, :], ws_in[:, 0:EXPERTS], s0, WsA[:, :], ALU.mult, ALU.subtract))
                sc.step(dve.scalar_tensor_tensor(WsE[0:DK1, :], ws_in[0:DK1, EXPERTS:2 * EXPERTS], s0[0:DK1], WsD[0:DK1, :], ALU.mult, ALU.subtract))
                dve.scalar_tensor_tensor(bs_h[:, EXPERTS:2 * EXPERTS], bs_in[:, :], s0[0:1], bs_h[:, 0:EXPERTS], ALU.mult, ALU.subtract).then_inc(bias_v, 2)
                assert sc.k == SC_ROUTER, sc.k

            def patch_step(s):
                nxt, prv = s.shift(1), s.shift(-1)
                if valid(nxt, 8):
                    cut(nxt)
                elif valid(s, 8):
                    for u in range(2):
                        move_pixels(s, u)
                if valid(prv, 8):
                    if not valid(prv.shift(-1)):
                        dve.wait_ge(ld_tb, 16)
                    for b in range(2):
                        at_least(dve, emb_mm, 2 * prv.n + b + 1)
                        at_least(dve, st_emb[b], 16 * prv.n)
                        dve.tensor_tensor(hp[b], ps[0:ET, 7 * b, 0:2 * D].rearrange("p (f d) -> p f d", f=2),
                                          tok_b_bc[0:ET, :].unsqueeze(1).to_broadcast([ET, 2, D]), ALU.add).then_inc(emb_v, 1)
                at_least(dve, ld_stage, 64 * (s.n + 1))
                dve.tensor_reduce(sizes[:, bass.ds(s.n, 1)], stage[:, 0:2 * D_FF], AX.X, ALU.max, apply_absolute_value=True)
                dve.tensor_reduce(sizes2[:, bass.ds(s.n, 1)], stage[:, 2 * D_FF:STAGE], AX.X, ALU.max, apply_absolute_value=True).then_inc(mx_done, 1)

            patch_pipeline(dve, patch_step, between)
            dve.wait_ge(ld_b, 32)
            dve.wait_ge(mx_done, EXPERTS)
            mx = Chain(dve, mx_v, 0, 0)
            mx.k = 3
            mx.step(dve.memset(sizes2[:, EXPERTS:EXPERTS + 1], 0.0))
            mx.link(dve.tensor_reduce(sizes[:, EXPERTS:EXPERTS + 1], b1_in[:, :], AX.X, ALU.max, apply_absolute_value=True))
            mx.link(dve.tensor_reduce(sizes2[0:B2P, EXPERTS:EXPERTS + 1], b2_in[:, :], AX.X, ALU.max, apply_absolute_value=True))
            mx.step(dve.tensor_reduce(magnitude[:, 1:2], sizes[:, :], AX.X, ALU.max))
            mx.step(dve.tensor_reduce(magnitude[:, 2:3], sizes2[:, :], AX.X, ALU.max))
            assert mx.k == MX_V, mx.k
            dve.wait_ge(sc_g, 2)
            sc = set_scales(slice(1, 3), SC_ROUTER)
            sc.step(dve.tensor_scalar(inv_h[:, :], inverse[:, 1:2], 1.0 / X_SCALE, None, ALU.mult))
            sc.link(dve.tensor_scalar(g_scale[:, :], scale[:, 1:2], 2.0 ** -7, 2.0 ** 15, ALU.mult, ALU.min))
            sc.link(dve.tensor_scalar(g_scale[:, :], g_scale[:, :], 2.0 ** -14, None, ALU.max))
            sc.step(dve.tensor_scalar(g_scale_row[:, :], ones[0:2, :], g_scale[0:2, :], None, ALU.mult))
            sc.link(dve.reciprocal(inv_out[:, :], g_scale[:, :]))
            sc.link(dve.tensor_scalar(inv_out[:, :], inv_out[:, :], inverse[:, 2:3], None, ALU.mult))
            sc.step(dve.tensor_scalar(neg_inv_out[:, :], inv_out[:, :], -1.0, None, ALU.mult))
            assert sc.k == SC_ALL, sc.k
            for src, hi, lo, by, n in ((b1_in, b1_hi, b1_lo, scale[:, 1:2], P), (b2_in, b2_hi, b2_lo, scale[:, 2:3], B2P)):
                sc.link(dve.tensor_scalar(hi[:, :], src[:, :], by[0:n], None, ALU.mult))
                dve.scalar_tensor_tensor(lo[:, :], src[:, :], by[0:n], hi[:, :], ALU.mult, ALU.subtract).then_inc(bias_v, 1)
            for b in range(2):
                dve.memset(xT1[b][DK1:DK1 + 1, :], 1.0)
            dve.memset(nE[DK1:E_ROWS], X_SCALE).then_inc(prep_v, 1)

            def step(group):
                nxt, prv, pp = group.shift(1), group.shift(-1), group.shift(-2)
                par = group.par

                def silu(q):
                    at_least(dve, th_done, 4 * group.n + q + 1)
                    b = pair(q)
                    if q < 3:
                        if q == 0:
                            at_least(dve, dec_in_done, group.n)
                            at_least(dve, dt_c, DT_LINKS * group.n)
                        dve.tensor_copy(dtv[:, q * HEADS:(q + 1) * HEADS], ps[:, b + 1, 384:390])
                        dve.scalar_tensor_tensor(zs[par][:, q, :], zs[par][:, q, :], 1.0, ps[:, b, 0:384], ALU.add, ALU.mult)
                        dve.scalar_tensor_tensor(xs[par][:, q, :], xs[par][:, q, :], 1.0, ps[:, b + 1, 0:384], ALU.add, ALU.mult).then_inc(silu_done, 1)
                    else:
                        dve.scalar_tensor_tensor(Bs[par], Bs[par], 1.0, ps[0:D_STATE, b, 0:384], ALU.add, ALU.mult)
                        dve.scalar_tensor_tensor(Cs[par], Cs[par], 1.0, ps[0:D_STATE, b + 1, 0:384], ALU.add, ALU.mult).then_inc(silu_done, 1)

                if valid(nxt):
                    c1 = Chain(dve, ln1_c, nxt.n, 6)
                    at_least(dve, ld_h[nxt.par], 16 * (nxt.j + 1))
                    at_least(dve, xn_done, 3 * nxt.n)
                    for k in range(GT):
                        c1.step(dve.bn_stats(st1[:, 6 * k:6 * k + 6], h_in[nxt.par][:, k, :]))
                    c1.sync()
                    settle(dve, settled_v)
                    for k in range(GT):
                        c1.step(dve.bn_aggr(mv1[:, 2 * k:2 * k + 2], st1[:, 6 * k:6 * k + 6]))
                    c1.done()
                if valid(group):
                    silu(0)
                if valid(nxt):
                    at_least(dve, ln1_p, 2 * (nxt.n + 1))
                    at_least(dve, t1_mm, nxt.n - 1)
                    c1.sync()
                    for k in range(GT):
                        dve.tensor_scalar(xn[nxt.par][:, k, :], h_in[nxt.par][:, k, :], mv1[:, 2 * k:2 * k + 1],
                                          rs1[:, k:k + 1], ALU.subtract, ALU.mult).then_inc(xn_done, 1)
                if valid(group):
                    silu(1)
                    silu(2)
                    cd = Chain(dve, dt_c, group.n, DT_LINKS)
                    at_least(dve, silu_done, 4 * group.n + 3)
                    cd.link(dve.scalar_tensor_tensor(nabs, dtv, -1.0, dtv, ALU.mult, ALU.min))
                    silu(3)
                if valid(pp):
                    cs = Chain(dve, sm_c, pp.n, SM_LINKS)
                    at_least(dve, lg_mm, pp.n + 1)
                    lg = ps[:, 6, 0:GT * EXPERTS].rearrange("p (k e) -> p k e", k=GT)
                    e3 = lambda t: t.rearrange("p (k e) -> p k e", k=GT)
                    bc = lambda t: t.unsqueeze(2).to_broadcast([P, GT, EXPERTS])
                    at_least(dve, row_done, pp.n)
                    cs.link(dve.tensor_reduce(lmax, lg, AX.X, ALU.max))
                    dve.tensor_tensor(e3(ld_), lg, bc(lmax), ALU.subtract).then_inc(lg_read, 1)

                def y_tile(k):
                    at_least(dve, y_mm, 3 * prv.n + k + 1)
                    if k == 0:
                        at_least(dve, xD_done, prv.n + 1)
                        at_least(dve, t2_mm, 3 * prv.n)
                        at_least(dve, sq_done, 3 * prv.n)
                    dve.tensor_tensor(y[:, k, :], ps[:, Y_BANK[k], 0:384], xD[:, k, :], ALU.add).then_inc(y1_done, 1)
                    at_least(dve, y1_done, 3 * prv.n + k + 1)
                    dve.tensor_tensor(y[:, k, :], y[:, k, :], zs[prv.par][:, k, :], ALU.mult).then_inc(y2_done, 1)

                if valid(prv):
                    y_tile(0)
                if valid(group):
                    at_least(dve, u_done, group.n + 1)
                    cd.link(dve.tensor_scalar(den, u_, 2.0, None, ALU.add))
                    cd.link(dve.reciprocal(rec, den))
                    cd.link(dve.tensor_tensor(s_, u_, rec, ALU.mult))
                    cd.link(dve.tensor_tensor(w_, s_, s_, ALU.mult))
                    cd.link(dve.tensor_scalar(ser, w_, 1.0 / (2 * LOG1P_TERMS - 1), None, ALU.mult))
                    for m in range(LOG1P_TERMS - 2, 0, -1):
                        cd.link(dve.scalar_tensor_tensor(ser, ser, 1.0 / (2 * m + 1), w_, ALU.add, ALU.mult))
                    cd.link(dve.scalar_tensor_tensor(ser, ser, 1.0, s_, ALU.add, ALU.mult))
                    cd.link(dve.tensor_scalar(relu, dtv, 0.0, None, ALU.max))
                    at_least(dve, dec_done, group.n)
                    cd.link(dve.scalar_tensor_tensor(dts, ser, 2.0, relu, ALU.mult, ALU.add))
                    cd.link(dve.tensor_tensor(a_.rearrange("p (k h) -> p k h", k=GT), dts.rearrange("p (k h) -> p k h", k=GT),
                                              neg_A[:, :].unsqueeze(1).to_broadcast([P, GT, HEADS]), ALU.mult))
                    cd.done()
                    at_least(dve, L_mm, group.n)
                    dve.tensor_tensor(decay_in.rearrange("p (s j) -> p s j", j=TIMES),
                                      a_.unsqueeze(2).to_broadcast([P, SH, TIMES]),
                                      causal16[:, :].unsqueeze(1).to_broadcast([P, SH, TIMES]), ALU.mult).then_inc(dec_in_done, 1)
                if valid(prv):
                    y_tile(1)
                if valid(pp):
                    at_least(dve, sm_exp, pp.n + 1)
                    cs.link(dve.tensor_reduce(rsum, e3(le_), AX.X, ALU.add))
                    cs.link(dve.reciprocal(rrec, rsum))
                    cs.link(dve.tensor_tensor(e3(pr_), e3(le_), bc(rrec), ALU.mult))
                    cs.link(dve.tensor_reduce(pmax, e3(pr_), AX.X, ALU.max))
                    cs.link(dve.tensor_tensor(e3(eq_), e3(pr_), bc(pmax), ALU.is_equal))
                    cs.link(dve.scalar_tensor_tensor(e3(cand), e3(eq_), -9.0, iota9p9[:, :].unsqueeze(1).to_broadcast([P, GT, EXPERTS]), ALU.mult, ALU.add))
                    r_now = routes[:, bass.ds(pp.n * GT, GT)]
                    cs.link(dve.tensor_reduce(r_now, e3(cand), AX.X, ALU.min))
                    cs.done()
                    dve.scalar_tensor_tensor(rows[pp.par][:, :, 2 * D:ROW_W].rearrange("p k a -> p (k a)"), r_now, 0.5, pmax,
                                             ALU.is_gt, ALU.mult).then_inc(row_done, 1)
                if valid(prv):
                    y_tile(2)
                if valid(group):
                    at_least(dve, E_done, group.n + 1)
                    dve.tensor_tensor(decay.rearrange("p (s j) -> p s j", j=TIMES), decay.rearrange("p (s j) -> p s j", j=TIMES),
                                      dts.unsqueeze(2).to_broadcast([P, SH, TIMES]), ALU.mult).then_inc(dec_done, 1)
                    at_least(dve, G_mm, group.n + 1)
                    at_least(dve, M_g, group.n)
                    dve.tensor_tensor(G_m, ps[:, 7, 0:384].rearrange("p (k t) -> p k t", k=GT),
                                      causal[:, :].unsqueeze(1).to_broadcast([P, GT, P]), ALU.mult).then_inc(Gm_done, 1)
                    at_least(dve, dec_done, group.n + 1)
                    at_least(dve, Gm_done, group.n + 1)
                    at_least(dve, y_mm, 3 * group.n)
                    for k in range(2):
                        form_M(dve, k).then_inc(M_v, 1)
                if valid(prv):
                    at_least(dve, rsy_c, 2 * (prv.n + 1))
                    at_least(dve, ld_res[prv.par], 16 * (prv.j + 1))
                    for k in range(GT):
                        at_least(dve, o_mm, 3 * prv.n + max(k + 1, 2))
                        dve.scalar_tensor_tensor(rows[prv.par][:, k, D:2 * D], ps[:, O_BANK[k], O_COL[k]:O_COL[k] + D], rsy[:, k:k + 1],
                                                 rows[prv.par][:, k, D:2 * D], ALU.mult, ALU.add).then_inc(h2_done, 1)
                    c2 = Chain(dve, ln2_c, prv.n, 6)
                    at_least(dve, n2_done, 3 * prv.n)
                    for k in range(GT):
                        at_least(dve, h2_done, 3 * prv.n + k + 1)
                        c2.step(dve.bn_stats(st2[:, 6 * k:6 * k + 6], rows[prv.par][:, k, D:2 * D]))
                    c2.sync()
                    settle(dve, settled_v)
                    for k in range(GT):
                        c2.step(dve.bn_aggr(mv2[:, 2 * k:2 * k + 2], st2[:, 6 * k:6 * k + 6]))
                    c2.sync()
                    c2.done()
                    at_least(dve, ln2_p, 2 * (prv.n + 1))
                    for k in range(GT):
                        last = dve.tensor_scalar(n2[:, k, :], rows[prv.par][:, k, D:2 * D], mv2[:, 2 * k:2 * k + 1],
                                                 rs2[:, k:k + 1], ALU.subtract, ALU.mult)
                    last.then_inc(n2_c, 1)
                    at_least(dve, n2_c, prv.n + 1)
                    pk = rows_h[prv.par]
                    dve.tensor_copy(pk[:, :, 0:D], n2).then_inc(n2_done, 1)
                    at_least(dve, n2_done, 3 * prv.n + 1)
                    dve.tensor_tensor(pk[:, :, D:D + DK1], n2[:, :, DK0:D], pk[:, :, DK0:D], ALU.subtract).then_inc(n2_done, 1)
                    dve.tensor_tensor(pk[:, :, D + DK1:PK], n2[:, :, 0:DK0], pk[:, :, 0:DK0], ALU.subtract).then_inc(n2_done, 1)
                e = split_of(group)
                if e is not None:
                    dve.wait_ge(cv_hi, e + 1)
                    s1, s2 = scale[:, 1:2], scale[:, 2:3]
                    dve.scalar_tensor_tensor(W1B[:, e, :], stage[:, 0:D_FF], s1, W1A[:, e, :], ALU.mult, ALU.subtract)
                    dve.scalar_tensor_tensor(W1E[0:DK1, e, :], stage[0:DK1, D_FF:2 * D_FF], s1[0:DK1], W1D[0:DK1, e, :], ALU.mult, ALU.subtract)
                    dve.scalar_tensor_tensor(W2lo[:, e].rearrange("p c d -> p (c d)"), stage[:, 2 * D_FF:STAGE], s2,
                                             W2hi[:, e].rearrange("p c d -> p (c d)"), ALU.mult, ALU.subtract).then_inc(cv_lo, 1)

            pipeline(dve, step)

            dve.wait_ge(st_rows[0], 16 * (GROUPS // 2))
            dve.wait_ge(st_rows[1], 16 * (GROUPS // 2))
            dve.wait_ge(cv_lo, EXPERTS)
            rc = Chain(dve, rt_v, 0, 0)
            full = TOKENS // P
            rc.step(dve.memset(routes[TOKENS - full * P:P, full:full + 1], float(EXPERTS)))
            rc.step(dve.memset(routes[:, full + 1:TILES], float(EXPERTS)))
            rc.link(dve.memset(no_add, 0.0))
            for e in range(EXPERTS):
                rc.step(dve.tensor_scalar(onehot[:, e, :], routes[:, :], float(e), None, ALU.is_equal))
            rc.sync()
            flat = onehot.rearrange("p e k -> p (e k)")
            rc.link(dve.tensor_tensor_scan(running, flat, no_add, 0.0, ALU.add, ALU.add))
            r3 = running.rearrange("p (e k) -> p e k", e=EXPERTS)
            rc.link(dve.tensor_tensor(to_slot, r3, onehot, ALU.subtract))
            rc.link(dve.tensor_copy(seg0, to_slot[:, :, 0]))
            rc.link(dve.tensor_tensor(count, r3[:, :, TILES - 1], seg0, ALU.subtract))
            assert rc.k == RT_COUNT, rc.k
            dve.wait_ge(rt_count, 1)
            rc.step(dve.tensor_copy(before, ps[:, 1, 0:EXPERTS]))
            rc.link(dve.tensor_scalar(total_e, ps[:, 2, 0:EXPERTS], float(P - 1), None, ALU.add))
            rc.link(dve.tensor_copy(cnt_i, total_e))
            rc.link(dve.tensor_scalar(cnt_i, cnt_i, 7, None, ALU.logical_shift_right))
            rc.link(dve.tensor_copy(tiles_e, cnt_i))
            rc.link(dve.tensor_tensor_scan(tile_end, tiles_e, no_add[:, 0:EXPERTS], 0.0, ALU.add, ALU.add))
            rc.link(dve.tensor_tensor(slot0, tile_end, tiles_e, ALU.subtract))
            rc.link(dve.scalar_tensor_tensor(slot0, slot0, float(P), before, ALU.mult, ALU.add))
            rc.link(dve.tensor_tensor(slot0, slot0, seg0, ALU.subtract))
            rc.link(dve.tensor_tensor(to_slot, to_slot, slot0.unsqueeze(2).to_broadcast([P, EXPERTS, TILES]), ALU.add))
            rc.link(dve.tensor_tensor(to_slot, to_slot, onehot, ALU.mult))
            rc.link(dve.tensor_reduce(slot, to_slot.rearrange("p e k -> p k e"), AX.X, ALU.add))
            rc.link(dve.tensor_scalar(is_pad, routes[:, :], EXPERTS - 0.5, float(2 * SL * P), ALU.is_gt, ALU.mult))
            rc.link(dve.tensor_tensor(slot, slot, is_pad, ALU.add))
            rc.link(dve.tensor_copy(ints[0], slot))
            rc.step(dve.tensor_scalar(ints[1], ints[0], P - 1, None, ALU.bitwise_and))
            rc.link(dve.tensor_scalar(ints[2], ints[0], 7, None, ALU.logical_shift_right))
            rc.step(dve.tensor_copy(slot_q, ints[1]))
            rc.link(dve.tensor_copy(slot_i, ints[2]))
            assert rc.k == RT_SLOT, rc.k
            dve.wait_ge(rt_g, 3)
            rc.step(dve.tensor_tensor(at_q, iota_q.unsqueeze(1).to_broadcast([P, TILES, P]),
                                      slot_q.unsqueeze(2).to_broadcast([P, TILES, P]), ALU.is_equal))
            eq_i = at_i[:, :, 1, :]
            rc.link(dve.tensor_tensor(eq_i, iota_i.unsqueeze(1).to_broadcast([P, TILES, SL]),
                                      slot_i.unsqueeze(2).to_broadcast([P, TILES, SL]), ALU.is_equal))
            rc.link(dve.tensor_tensor(at_i[:, :, 0, :], eq_i, iota_i[:, 0:TILES].unsqueeze(2).to_broadcast([P, TILES, SL]), ALU.mult))
            rc.link(dve.tensor_scalar(eq_i, eq_i, row_p1, None, ALU.mult))
            assert rc.k == RT_HOT, rc.k
            rc.link(dve.tensor_tensor(past, iota_i.unsqueeze(2).to_broadcast([P, SL, EXPERTS]),
                                      tile_end.unsqueeze(1).to_broadcast([P, SL, EXPERTS]), ALU.is_ge))
            rc.link(dve.tensor_reduce(expert_f, past, AX.X, ALU.add))
            rc.link(dve.tensor_scalar(expert_f, expert_f, float(EXPERTS - 1), None, ALU.min))
            rc.link(dve.tensor_copy(expert_ids, expert_f))
            dve.wait_ge(rt_a, 1)
            rc.link(dve.tensor_scalar(empty, sums[:, SL:2 * SL], 0.5, float(ROWS), ALU.is_lt, ALU.mult))
            rc.link(dve.scalar_tensor_tensor(row_f, sums[:, 0:SL], float(P), sums[:, SL:2 * SL], ALU.mult, ALU.add))
            rc.link(dve.scalar_tensor_tensor(row_f, row_f, -1.0, empty, ALU.add, ALU.add))
            rc.link(dve.tensor_copy(row_ids, row_f))
            rc.link(dve.tensor_scalar(row_tmp, row_ids, TIMES - 1, None, ALU.bitwise_and))
            rc.link(dve.tensor_copy(time_f, row_tmp))
            rc.link(dve.tensor_scalar(row_tmp, row_ids, 4, None, ALU.logical_shift_right))
            rc.link(dve.tensor_copy(row_f, row_tmp))
            rc.link(dve.scalar_tensor_tensor(row_f, time_f, float(POSITIONS), row_f, ALU.mult, ALU.add))
            dve.tensor_copy(out_ids, row_f).then_inc(rt_done, 1)
            dve.wait_ge(rt_done, 1)
            for b in range(2):
                last = dve.memset(fE[b][DK1:E_ROWS, :], X_SCALE)
            last.then_inc(rt_done, 1)

            def slot_step(t):
                nxt, prv = t.shift(1), t.shift(-1)
                if slot_valid(nxt):
                    at_least(dve, fx_mm, nxt.n + 1)
                    at_least(dve, hid_mm, nxt.n - 1)
                    fx = ps[:, 0, 0:3 * P // 2].bitcast(f16)
                    dve.tensor_copy(fT[nxt.par], fx)
                    dve.tensor_copy(fE[nxt.par][0:DK1, :], fx[0:DK1, 2 * P:3 * P]).then_inc(fx_ev, 1)
                if slot_valid(prv):
                    w = tok_row[prv.r][:, 2 * D:ROW_W]
                    cm = Chain(dve, mix_c, prv.n, 3)
                    at_least(dve, mix_done, prv.n - 1)
                    wc, wo = w_common[prv.par], w_own[prv.par]
                    cm.step(dve.tensor_scalar(wc, w, neg_inv_out[:, 0:1], inv_out[:, 0:1], ALU.mult, ALU.add))
                    cm.step(dve.tensor_scalar(wo, w, inv_out[:, 0:1], None, ALU.mult))
                    at_least(dve, two_mm, prv.n + 1)
                    at_least(dve, f_out[prv.shift(-2).r], 16 * prv.shift(2).j)
                    cm.sync()
                    o = ps[:, 6 + prv.par, :]
                    cm.link(dve.scalar_tensor_tensor(mixed[prv.par], o[:, 0:D], wc, tok_row[prv.r][:, D:2 * D], ALU.mult, ALU.add))
                    cm.done()
                    dve.scalar_tensor_tensor(mixed[prv.par], o[:, D:2 * D], wo, mixed[prv.par], ALU.mult, ALU.add).then_inc(mix_done, 1)
                if slot_valid(t):
                    for i in range(2):
                        at_least(dve, hi_done[i], t.n + 1)
                        at_least(dve, two_mm, t.n - 1)
                        dve.scalar_tensor_tensor(g_lo[i][t.par], g32[i], g_scale[:, 0:1], g_hi[i][t.par], ALU.mult, ALU.subtract).then_inc(lo_done[i], 1)

            slot_pipeline(dve, slot_step)

        @block.tensor
        def _(pe):
            pe.wait_ge(prep_g, 3)
            pe.wait_ge(ld_pw, 16)
            pw = patch_W.rearrange("p a (i q c) -> p a i q c", i=2, c=3)
            for c, bank in enumerate((0, 7, 4)):
                for i in range(2):
                    for a in range(2):
                        last = nc.tensor.transpose(ps[:, bank, i * D + a * 96:i * D + (a + 1) * 96], pw[:, a, i, :, c], ident[0:96, 0:96])
            last.then_inc(prep_pe, 1)

            def patch_step(s):
                prv = s.shift(-1)
                if valid(s, 8):
                    for u in range(2):
                        at_least(pe, pix_cut, s.n * 2 + u + 1)
                        at_least(pe, pix_ev_a, s.n * 2 + u - 1)
                        at_least(pe, pix_ev_v, s.n * 2 + u - 1)
                        if isinstance(s.n, int) and s.n == 0 and u == 1:
                            pe.wait_ge(prep_v, 3)
                        for q, (w0, nw_) in enumerate(WP_BANKS):
                            for w in range(nw_):
                                last = nc.tensor.transpose(ps[:, 1 + 3 * u + q, w * RB:(w + 1) * RB], pix_by_patch[u][:, (w0 + w) * P:(w0 + w + 1) * P], ident[0:RB, 0:RB])
                        last.then_inc(pix_T, 1)
                if valid(prv, 8):
                    at_least(pe, pix_ev_a, 2 * (prv.n + 1))
                    at_least(pe, pix_ev_v, 2 * (prv.n + 1))
                    for b in range(2):
                        at_least(pe, emb_v, 2 * (prv.n - 1) + b + 1)
                        for f in range(2):
                            for m in range(6):
                                c, u = m // 2, m % 2
                                col = (b * 3 + c) * N_PATCH + f * ET
                                last = nc.tensor.matmul(ps[0:ET, 7 * b, f * D:(f + 1) * D], XT[prv.par][u][:, col:col + ET], patch_WT[:, c, u, :],
                                                        start=(m == 0), stop=(m == 5))
                        last.then_inc(emb_mm, 1)

            patch_pipeline(pe, patch_step)
            pe.wait_ge(prep_v, PREP_V + 1)
            pe.wait_ge(emb_v, 2 * 8)
            pe.wait_ge(ld_w, 16 * (N_SMALL_LOADS + 2))

            def step(group):
                nxt, prv, pp = group.shift(1), group.shift(-1), group.shift(-2)
                par = group.par

                def transpose_rows(src, sem_):
                    for k in range(GT):
                        nc.tensor.transpose(ps[:, 0, k * P:(k + 1) * P], src[:, k, 0:DK0], ident[:, :])
                        last = nc.tensor.transpose(ps[0:DK1, 1, k * P:(k + 1) * P], src[:, k, DK0:D], ident[:, :])
                    last.then_inc(sem_, 1)

                def split_T(src, sem_):
                    AC, Dd = ps[:, 0, :].bitcast(f16), ps[:, 1, :].bitcast(f16)
                    for k in range(GT):
                        nc.tensor.transpose(AC[:, k * P:(k + 1) * P], src[:, k, 0:DK0], ident_h[:, :])
                        nc.tensor.transpose(AC[:, (GT + k) * P:(GT + k + 1) * P], src[:, k, D + DK1:PK], ident_h[:, :])
                        last = nc.tensor.transpose(Dd[:, k * P:(k + 1) * P], src[:, k, DK0:D + DK1], ident_h[:, :])
                    last.then_inc(sem_, 1)

                def proj(q):
                    b = pair(q)
                    if q == 0:
                        at_least(pe, t1_ev, 2 * (group.n + 1))
                    at_least(pe, silu_done, 4 * group.n + q - 1)
                    if q < 3:
                        for W, T, s in ((Wa, xT0[par], 0), (Wb, xT1[par], 1)):
                            nc.tensor.matmul(ps[:, b, 0:384], T[:, q * P:(q + 1) * P], W[:, 0:384], start=s == 0, stop=s == 1)
                            last = nc.tensor.matmul(ps[:, b + 1, 0:390], T[:, q * P:(q + 1) * P], W[:, 384:PROJ], start=s == 0, stop=s == 1)
                    else:
                        for W, T, s in ((Wa, xT0[par], 0), (Wb, xT1[par], 1)):
                            nc.tensor.matmul(ps[0:D_STATE, b, 0:384], W[:, PROJ:PROJ + D_STATE], T, start=s == 0, stop=s == 1)
                            last = nc.tensor.matmul(ps[0:D_STATE, b + 1, 0:384], W[:, PROJ + D_STATE:IN_W], T, start=s == 0, stop=s == 1)
                    last.then_inc(proj_mm, 1)

                def y_tile(k):
                    if k == 0:
                        at_least(pe, M_v, 2 * (prv.n + 1))
                        at_least(pe, M_g, prv.n + 1)
                        at_least(pe, silu_done, 4 * prv.n + 3)
                        at_least(pe, Gm_done, prv.n + 1)
                    if k == 1:
                        at_least(pe, E_done, prv.n + 1)
                        if valid(pp):
                            at_least(pe, lg_read, pp.n + 1)
                    if k == 2:
                        at_least(pe, y1_done, 3 * prv.n + 1)
                    for h in range(HEADS):
                        last = nc.tensor.matmul(ps[:, Y_BANK[k], h * HEADDIM:(h + 1) * HEADDIM], M_all[:, k, h, :],
                                                xs[prv.par][:, k, h * HEADDIM:(h + 1) * HEADDIM], start=True, stop=True)
                    last.then_inc(y_mm, 1)

                if valid(group):
                    proj(0)
                    proj(1)
                if valid(pp):
                    at_least(pe, n2_done, 3 * (pp.n + 1))
                    at_least(pe, h2_done, 3 * (pp.n + 1))
                    split_T(rows_h[pp.par], t3_mm)
                if valid(group):
                    proj(2)
                    proj(3)
                if valid(pp):
                    at_least(pe, t3_ev, 3 * (pp.n + 1))
                    at_least(pe, E_done, pp.n + 2 if valid(prv) else pp.n + 1)
                    for k in range(GT):
                        o = ps[:, 6, k * EXPERTS:(k + 1) * EXPERTS]
                        for m, (T, W) in enumerate(((nAC[:, 0, k], WsA[:, :]), (nAC[:, 0, k], WsB[:, :]), (nAC[:, 1, k], WsA[:, :]),
                                                    (nD[:, k], WsD[:, :]), (nE[0:E_ROWS, k], WsE[0:E_ROWS, :]))):
                            last = nc.tensor.matmul(o, T, W, start=m == 0, stop=m == 4)
                    last.then_inc(lg_mm, 1)
                if valid(prv):
                    y_tile(0)
                    y_tile(1)
                if valid(nxt):
                    at_least(pe, xn_done, 3 * (nxt.n + 1))
                    if valid(pp):
                        at_least(pe, t3_ev, 3 * (pp.n + 1))
                    transpose_rows(xn[nxt.par], t1_mm)
                if valid(prv):
                    y_tile(2)
                    for k in range(GT):
                        at_least(pe, y2_done, 3 * prv.n + k + 1)
                        if k < 2:
                            if valid(nxt):
                                at_least(pe, t1_ev, 2 * (nxt.n + 1))
                            elif valid(pp):
                                at_least(pe, t3_ev, 3 * (pp.n + 1))
                        else:
                            at_least(pe, t2_ev, 3 * prv.n + 1)
                        for c in range(3):
                            last = nc.tensor.transpose(ps[:, T2_BANK[k], c * P:(c + 1) * P], y[:, k, c * P:(c + 1) * P], ident[:, :])
                        last.then_inc(t2_mm, 1)
                if valid(group):
                    at_least(pe, dec_in_done, group.n + 1)
                    if valid(prv):
                        at_least(pe, y1_done, 3 * prv.n + 3)
                    nc.tensor.matmul(ps[:, 6, 0:GT * HEADS * TIMES], later[:, :], decay_in, start=True, stop=True).then_inc(L_mm, 1)
                    at_least(pe, silu_done, 4 * (group.n + 1))
                    for k in range(GT):
                        last = nc.tensor.matmul(ps[:, 7, k * P:(k + 1) * P], Bs[par][:, k * P:(k + 1) * P], Cs[par][:, k * P:(k + 1) * P],
                                                start=True, stop=True)
                    last.then_inc(G_mm, 1)
                if valid(prv):
                    for k in range(GT):
                        at_least(pe, t2_ev, 3 * prv.n + 3)
                        for c in range(3):
                            last = nc.tensor.matmul(ps[:, O_BANK[k], O_COL[k]:O_COL[k] + D], yT[:, k, c * P:(c + 1) * P], Wo[:, c, :],
                                                    start=c == 0, stop=c == 2)
                        last.then_inc(o_mm, 1)

            pipeline(pe, step)

            pe.wait_ge(rt_v, RT_COUNT)
            pe.wait_ge(rt_g, 5)
            nc.tensor.matmul(ps[:, 1, 0:EXPERTS], earlier_rows[:, :], count, start=True, stop=True)
            nc.tensor.matmul(ps[:, 2, 0:EXPERTS], ones[:, :], count, start=True, stop=True).then_inc(rt_count, 1)
            pe.wait_ge(rt_v, RT_HOT)

            def add_tile(k, start, stop):
                return nc.tensor.matmul(ps[:, 0, 0:2 * SL], at_q[:, bass.ds(k, 1), :], at_i[:, bass.ds(k, 1), :, :], start=start, stop=stop)

            add_tile(0, True, False)
            with pe.Fori(1, TILES - 1) as k:
                add_tile(k, False, False)
            add_tile(TILES - 1, False, True).then_inc(rt_slots, 1)
            pe.wait_ge(ld_experts, 16 * 2)
            pe.wait_ge(cv_hi, EXPERTS)
            pe.wait_ge(cv_lo, EXPERTS)
            pe.wait_ge(rt_done, 2)

            def load_expert(t):
                return pe.value_load(expert_ids[0:1, bass.ds(t.n, 1)], min_val=0, max_val=EXPERTS - 1)

            def slot_step(t):
                nxt, prv = t.shift(1), t.shift(-1)
                if slot_valid(t):
                    e = load_expert(t)
                    at_least(pe, fx_ev, t.n + 1)
                    T = fT[t.par]
                    at_least(pe, gelu_done[0], t.n)
                    at_least(pe, gelu_done[1], t.n)
                    for c in range(FCH):
                        for m, (W, n, r) in enumerate(((W1A, P, T[:, 0:P]), (W1A, P, T[:, P:2 * P]), (W1B, P, T[:, 0:P]),
                                                       (W1D, P, T[:, 2 * P:3 * P]), (W1E, E_ROWS, fE[t.par][0:E_ROWS, :]))):
                            for i, bank in ((1, 1), (0, 3)):
                                o = ps[:, bank + c // 3, (c % 3) * P:(c % 3 + 1) * P]
                                lhs = W[0:n, 0, c * P:(c + 1) * P] if i else W[0:n, bass.ds(e, 1), c * P:(c + 1) * P]
                                last = nc.tensor.matmul(o, lhs, r, start=m == 0, stop=m == 4)
                    last.then_inc(hid_mm, 1)
                if slot_valid(prv):
                    ep = load_expert(prv)
                if slot_valid(nxt):
                    pe.wait_ge(f_rows[nxt.r], 16 * (nxt.j + 1))
                    at_least(pe, fx_ev, nxt.n)
                    fx = ps[:, 0, 0:3 * P // 2].bitcast(f16)
                    for i, col in enumerate((0, D + DK1, DK0)):
                        last = nc.tensor.transpose(fx[:, i * P:(i + 1) * P], tok_h[nxt.r][:, col:col + P], ident_h[:, :])
                    last.then_inc(fx_mm, 1)
                if slot_valid(prv):
                    at_least(pe, mix_done, prv.n - 1)
                    for i in (1, 0):
                        at_least(pe, hi_done[i], prv.n + 1)
                        at_least(pe, lo_done[i], prv.n + 1)
                        o = ps[:, 6 + prv.par, (1 - i) * D:(2 - i) * D]
                        for c in range(FCH):
                            hi, lo = g_hi[i][prv.par][:, c * P:(c + 1) * P], g_lo[i][prv.par][:, c * P:(c + 1) * P]
                            wc = lambda W: W[:, 0, c, :] if i else W[:, bass.ds(ep, 1), c, :]
                            nc.tensor.matmul(o, hi, wc(W2hi), start=c == 0, stop=False)
                            nc.tensor.matmul(o, hi, wc(W2lo), start=False, stop=False)
                            nc.tensor.matmul(o, lo, wc(W2hi), start=False, stop=False)
                        last = nc.tensor.matmul(o, g_scale_row[:, :], b2h[:, 0, :] if i else b2h[:, bass.ds(ep, 1), :], start=False, stop=True)
                    last.then_inc(two_mm, 1)

            slot_pipeline(pe, slot_step)


_INS = ['x', 'txt', 'L0_tok_W', 'L0_tok_b', 'L0_attn_W_in', 'L0_attn_conv_w', 'L0_attn_conv_b', 'L0_attn_dt_bias',
        'L0_attn_A_log', 'L0_attn_D', 'L0_attn_norm_w', 'L0_attn_W_out', 'L0_ffn_Ws', 'L0_ffn_bs', 'L0_ffn_W1',
        'L0_ffn_b1', 'L0_ffn_W2', 'L0_ffn_b2']
_OUTS = [((TIMES, POSITIONS, D), 'float32')]


def kernel(**inputs):
    import numpy as _np
    import concourse.bacc as _bacc
    from concourse import mybir as _mybir
    from concourse.bass_utils import run_bass_kernel_spmd as _run

    nc = _bacc.Bacc("TRN2", target_bir_lowering=False, num_devices=1)
    arrays, args = {}, []
    for name in _INS:
        a = _np.ascontiguousarray(inputs[name])
        arrays[f"in_{name}_dram"] = a
        args.append(nc.dram_tensor(f"in_{name}_dram", a.shape, _mybir.dt.from_np(a.dtype), kind="ExternalInput").ap())
    for i, (shape, dtype) in enumerate(_OUTS):
        dt = _mybir.dt.from_np(_np.dtype(dtype))
        args.append(nc.dram_tensor(f"out_{i}_dram", shape, dt, kind="ExternalOutput").ap())
    build_kernel(nc, *args)
    r = _run(nc, [arrays], core_ids=[0])
    return r.results[0]["out_0_dram"]
```

```python
import numpy as np
from contextlib import ExitStack

import concourse.bass as bass
from concourse import mybir

TIMES = 16
N_PATCH = 196
N_TEXT = 512
POSITIONS = N_PATCH + N_TEXT
D = 192
DK0 = 128
DK1 = D - DK0
P = 128
POS_TILE = P // TIMES
GT = 3
GROUPS = -(-POSITIONS // (POS_TILE * GT))
TILES = GROUPS * GT
TOKENS = POSITIONS * TIMES
ROWS = TILES * P
D_INNER = 384
HEADS = 6
HEADDIM = 64
D_STATE = 64
PIX = 768
EXPERTS = 9
D_FF = 768
FCH = D_FF // P
SLOT_TILES = TOKENS // P + EXPERTS
ROW_W = 2 * D + 1
EPS = 1e-5
LOG1P_TERMS = 7
X_SCALE = 2.0 ** 10
PK = 2 * D
E_ROWS = DK1 + 2


class Group:

    def __init__(self, j, r, cycle=2):
        self.j, self.r, self.cycle = j, r, cycle
        self.par = r % 2

    @property
    def n(self):
        return self.j * self.cycle + self.r

    def shift(self, d):
        q = self.r + d
        return Group(self.j + q // self.cycle, q % self.cycle, self.cycle)


def at_least(eng, sem, value):
    if isinstance(value, int) and value <= 0:
        return
    eng.wait_ge(sem, value)


def settle(eng, always):
    eng.sem_inc(always, 1)


class Chain:

    def __init__(self, eng, sem, n, per):
        self.eng, self.sem, self.n, self.per, self.k = eng, sem, n, per, 0

    def step(self, ins):
        self.k += 1
        ins.then_inc(self.sem, 1)

    def sync(self):
        at_least(self.eng, self.sem, self.n * self.per + self.k)

    def link(self, ins):
        self.step(ins)
        self.sync()

    def done(self):
        assert self.k == self.per, (self.k, self.per)


def build_kernel(nc, x, txt, tok_W, tok_b, W_in, conv_w, conv_b, dt_bias, A_log, D_skip, norm_w, W_out,
                 Ws, bs, W1, b1, W2, b2, out):
    f32, bf16, f16, i32 = mybir.dt.float32, mybir.dt.bfloat16, mybir.dt.float16, mybir.dt.int32
    ALU, ACT, AX = mybir.AluOpType, mybir.ActivationFunctionType, mybir.AxisListType

    h_rows = nc.dram_tensor("h_rows", (ROWS, D), f32).ap()
    ffn_rows = nc.dram_tensor("ffn_rows", (ROWS, ROW_W), f32).ap()
    b1_rows = nc.dram_tensor("b1_rows", (2, EXPERTS * D_FF), f16).ap()
    b2_rows = nc.dram_tensor("b2_rows", (2, EXPERTS * D), f16).ap()

    ctx = ExitStack()
    with ctx:
        def sb(name, shape, dt=f32):
            return ctx.enter_context(nc.sbuf_tensor(name, shape, dt))

        def sem(name):
            return ctx.enter_context(nc.semaphore(name))

        def sems(name, n):
            return [sem(f"{name}{i}") for i in range(n)]

        ident = sb("ident", [P, P])
        later = sb("later", [P, P])
        causal_s = sb("causal_s", [P, P])
        causal = sb("causal", [P, P])
        causal16 = sb("causal16", [P, TIMES])
        ones = sb("ones", [P, P])
        earlier_rows = sb("earlier_rows", [P, P])
        minus_half = sb("minus_half", [P, 4])
        iota9p9 = sb("iota9p9", [P, EXPERTS])
        tok_b_bc = sb("tok_b_bc", [P, D])
        neg_A = sb("neg_A", [P, HEADS])
        D_bc = sb("D_bc", [P, HEADS])
        small_in = sb("small_in", [P, 16])
        ident_h = sb("ident_h", [P, P], f16)
        magnitude, magnitude_all, bits, scale, inverse = [sb(n, [P, 4]) for n in
                                                          ("magnitude", "magnitude_all", "bits", "scale", "inverse")]
        inv_h, inv_out, g_scale, neg_inv_out, inv_logit, inv_in, inv_in2 = [
            sb(n, [P, 1]) for n in ("inv_h", "inv_out", "g_scale", "neg_inv_out", "inv_logit", "inv_in", "inv_in2")]
        sizes, sizes2 = sb("sizes", [P, EXPERTS + 1]), sb("sizes2", [P, EXPERTS + 1])
        g_scale_row = sb("g_scale_row", [2, P], f16)
        PROJ = 2 * D_INNER + HEADS
        IN_W = PROJ + 2 * D_STATE
        WiA, WiB, WiD, WiE = [sb(n, [P, IN_W], f16) for n in ("WiA", "WiB", "WiD", "WiE")]
        Wo = sb("Wo", [P, 3, D])
        ws_in = sb("ws_in", [P, 2 * EXPERTS])
        bs_in = sb("bs_in", [1, EXPERTS])
        bs_h = sb("bs_h", [1, 2 * EXPERTS], f16)
        WsA, WsB, WsD, WsE = [sb(n, [P, EXPERTS], f16) for n in ("WsA", "WsB", "WsD", "WsE")]
        routes = sb("routes", [P, TILES])
        E1W = EXPERTS * D_FF
        E2W = EXPERTS * FCH * D
        w_all = sb("w_all", [P, 2 * E1W + E2W])
        w_h = w_all[:, :].bitcast(f16)
        W1A, W1B, W1D, W1E = [w_h[:, i * E1W:(i + 1) * E1W].rearrange("p (e f) -> p e f", e=EXPERTS) for i in range(4)]
        W2hi, W2lo = [w_h[:, 4 * E1W + i * E2W:4 * E1W + (i + 1) * E2W].rearrange("p (e c d) -> p e c d", e=EXPERTS, c=FCH)
                      for i in range(2)]
        b2h = sb("b2h", [2, EXPERTS, D], f16)
        B1C, B2R = E1W // P, 16
        b1_in, b1_hi, b1_lo = sb("b1_in", [P, B1C]), sb("b1_hi", [P, B1C], f16), sb("b1_lo", [P, B1C], f16)
        B2P = EXPERTS * D // B2R
        b2_in, b2_hi, b2_lo = sb("b2_in", [B2P, B2R]), sb("b2_hi", [B2P, B2R], f16), sb("b2_lo", [B2P, B2R], f16)
        HALF = 8 * 224
        RB = 2 * 3 * 14
        ET = N_PATCH // 2
        pix = [w_all[0:RB, u * HALF:(u + 1) * HALF] for u in range(2)]
        pix_by_patch = [w_all[0:RB, (2 + u) * HALF:(3 + u) * HALF] for u in range(2)]
        o = 4 * HALF
        hp = [w_all[0:ET, o + u * 2 * D:o + (u + 1) * 2 * D].rearrange("p (f d) -> p f d", f=2) for u in range(2)]
        zeros = w_all[:, o + 4 * D:o + 6 * D]
        patch_W = w_all[0:96, o + 6 * D:o + 6 * D + 2 * PIX].rearrange("p (a k) -> p a k", a=2)
        o += 6 * D + 2 * PIX
        conv_bc = w_all[:, o:o + 2048]
        nw = w_all[:, o + 2048:o + 2051]
        o += 2052
        Wa, Wb = w_all[:, o:o + IN_W], w_all[:, o + IN_W:o + 2 * IN_W]
        in_bias = w_all[0:1, o + 2 * IN_W:o + 3 * IN_W]
        in_bias_h = w_all[0:1, o + 3 * IN_W:o + 4 * IN_W].bitcast(f16).rearrange("p (a c) -> p a c", a=2)
        STAGE = 2 * D_FF + FCH * D
        ARENA = STAGE + 21260
        arena = sb("arena", [P, ARENA])
        stage = arena[:, 0:STAGE]
        XTW = RB * 14
        XT = [[arena[:, STAGE + (2 * r + u) * XTW:STAGE + (2 * r + u + 1) * XTW] for u in range(2)] for r in range(2)]
        patch_WT = arena[:, STAGE + 4 * XTW:STAGE + 4 * XTW + 6 * D].rearrange("p (c i d) -> p c i d", c=3, i=2)

        class Area:
            def __init__(self, at=0):
                self.at = at

            def take(self, size, parts=P):
                a = arena[0:parts, self.at:self.at + size]
                self.at += size
                assert self.at <= ARENA, self.at
                return a

        ar = Area(STAGE)
        k3 = lambda ap, w: ap.rearrange("p (k w) -> p k w", w=w)
        zs = [k3(ar.take(GT * D_INNER), D_INNER) for _ in range(2)]
        xs = [k3(ar.take(GT * D_INNER), D_INNER) for _ in range(2)]
        Bs = [ar.take(GT * P, D_STATE) for _ in range(2)]
        Cs = [ar.take(GT * P, D_STATE) for _ in range(2)]
        h_in = [k3(ar.take(GT * D), D) for _ in range(2)]
        xn32 = k3(ar.take(GT * D), D)
        xn_h = k3(ar.take(GT * D).bitcast(f16), PK)
        xAC = ar.take(GT * P).bitcast(f16).rearrange("p (a k t) -> p a k t", a=2, k=GT)
        xDD = ar.take(GT * P // 2).bitcast(f16).rearrange("p (k t) -> p k t", k=GT)
        xE = ar.take(GT * P // 2).bitcast(f16).rearrange("p (k t) -> p k t", k=GT)
        rows_flat = [ar.take(GT * ROW_W) for _ in range(2)]
        rows = [k3(r, ROW_W) for r in rows_flat]
        rows_h = [k3(r.bitcast(f16), 2 * ROW_W) for r in rows_flat]
        n32 = k3(ar.take(GT * D), D)
        nAC = ar.take(GT * P).bitcast(f16).rearrange("p (a k t) -> p a k t", a=2, k=GT)
        nD = ar.take(GT * P // 2).bitcast(f16).rearrange("p (k t) -> p k t", k=GT)
        nE = ar.take(GT * P // 2).bitcast(f16).rearrange("p (k t) -> p k t", k=GT)
        decay_in = ar.take(GT * HEADS * TIMES)
        decay = ar.take(GT * HEADS * TIMES)
        G_m = k3(ar.take(GT * P), P)
        M_all = ar.take(GT * HEADS * P).rearrange("p (k h t) -> p k h t", k=GT, h=HEADS)
        xD = k3(ar.take(GT * D_INNER), D_INNER)
        y = k3(ar.take(GT * D_INNER), D_INNER)
        yT = k3(ar.take(GT * D_INNER), D_INNER)
        sq = ar.take(D_INNER)
        st1 = ar.take(GT * 6)
        mv1 = ar.take(GT * 2)
        var1 = ar.take(GT)
        rs1 = ar.take(GT)
        neg1, shift1, neg2, shift2 = [ar.take(GT) for _ in range(4)]
        st2 = ar.take(GT * 6)
        mv2 = ar.take(GT * 2)
        var2 = ar.take(GT)
        rs2 = ar.take(GT)
        ssq = ar.take(GT)
        ms = ar.take(GT)
        rsy = ar.take(GT)
        SH = GT * HEADS
        dtv, nabs, u_, den, rec, s_, w_, ser, relu, dts, a_ = [ar.take(SH) for _ in range(11)]
        lmax, rsum, rrec, pmax = [ar.take(GT) for _ in range(4)]
        ld_, le_, pr_, eq_, cand = [ar.take(GT * EXPERTS) for _ in range(5)]

        rt = Area()
        onehot = rt.take(EXPERTS * TILES).rearrange("p (e k) -> p e k", e=EXPERTS)
        running = rt.take(EXPERTS * TILES)
        no_add = rt.take(EXPERTS * TILES)
        to_slot = rt.take(EXPERTS * TILES).rearrange("p (e k) -> p e k", e=EXPERTS)
        HOT = 10
        iota_q = rt.take(P // 2).bitcast(bf16)
        iota_i16 = rt.take((SLOT_TILES + 1) // 2).bitcast(bf16)[:, 0:SLOT_TILES]
        iota_i = rt.take(SLOT_TILES)
        row_p1 = rt.take(1)
        seg0, count, before, total_e, tiles_e, tile_end, slot0 = [rt.take(EXPERTS) for _ in range(7)]
        slot, is_pad = [rt.take(TILES) for _ in range(2)]
        slot_q, slot_i = [rt.take(TILES // 2).bitcast(bf16) for _ in range(2)]
        at_q = rt.take(TILES * P // 2).bitcast(bf16).rearrange("p (k q) -> p k q", q=P)
        at_i = rt.take(TILES * SLOT_TILES).bitcast(bf16).rearrange("p (k t i) -> p k t i", t=2, i=SLOT_TILES)
        SL = SLOT_TILES
        sums, = [rt.take(2 * SL)]
        row_f, empty, time_f, past = rt.take(SL), rt.take(SL), rt.take(SL), rt.take(SL * EXPERTS).rearrange("p (i e) -> p i e", e=EXPERTS)
        expert_f = rt.take(SL)
        ints = [rt.take(TILES).bitcast(i32) for _ in range(3)]
        cnt_i = rt.take(EXPERTS).bitcast(i32)
        row_ids = rt.take(SL).bitcast(i32)
        row_tmp = rt.take(SL).bitcast(i32)
        out_ids = rt.take(SL).bitcast(i32)
        expert_ids = rt.take(SL).bitcast(i32)
        ex = Area()
        tok_row = [ex.take(ROW_W) for _ in range(4)]
        tok_h = [t.bitcast(f16) for t in tok_row]
        fT = [ex.take(3 * P // 2).bitcast(f16) for _ in range(2)]
        fE = [ex.take(P // 2).bitcast(f16) for _ in range(2)]
        g32 = [ex.take(D_FF) for _ in range(2)]
        g_hi, g_lo = [[[ex.take(D_FF // 2).bitcast(f16) for _ in range(2)] for _ in range(2)] for _ in range(2)]
        mixed = [ex.take(D) for _ in range(2)]
        w_common, w_own = [[ex.take(1) for _ in range(2)] for _ in range(2)]
        ids_in = ex.take(4).bitcast(i32)
        ids_out = ex.take(4).bitcast(i32)
        assert ex.at < TILES * EXPERTS * 4 + P + 600 + TILES * (P + SL) // 2

        ps = ctx.enter_context(nc.psum_tensor("ps", [P, 8, 512], f32))

        ld_w = sem("ld_w")
        ld_pw = sem("ld_pw")
        ld_tb = sem("ld_tb")
        st_b = sem("st_b")
        ld_stage = sem("ld_stage")
        ld_b = sem("ld_b")
        mx_v = sem("mx_v")
        mx_done = sem("mx_done")
        sc_v = sem("sc_v")
        sc_g = sem("sc_g")
        cv_hi = sem("cv_hi")
        cv_lo = sem("cv_lo")
        bias_v = sem("bias_v")
        ld_pix = sems("ld_pix", 2)
        txt_copied = sem("txt_copied")
        pad_zeroed = sem("pad_zeroed")
        ld_experts = sem("ld_experts")
        settled_v, settled_g = sem("settled_v"), sem("settled_g")
        prep_v = sem("prep_v")
        prep_g = sem("prep_g")
        prep_a = sem("prep_a")
        prep_pe = sem("prep_pe")
        pix_cut = sem("pix_cut")
        pix_T = sem("pix_T")
        pix_ev_a = sem("pix_ev_a")
        pix_ev_v = sem("pix_ev_v")
        emb_mm = sem("emb_mm")
        emb_v = sem("emb_v")
        st_emb = sems("st_emb", 2)

        ld_h = sems("ld_h", 2)
        ld_res = sems("ld_res", 2)
        ln1_c = sem("ln1_c")
        ln1_p = sem("ln1_p")
        x32_done = sem("x32_done")
        xhi_done = sem("xhi_done")
        xlo_done = sem("xlo_done")
        t1_mm = sem("t1_mm")
        t1_ev = sem("t1_ev")
        proj_mm = sem("proj_mm")
        th_done = sem("th_done")
        silu_done = sem("silu_done")
        dt_c = sem("dt_c")
        u_done = sem("u_done")
        dec_in_done = sem("dec_in_done")
        L_mm = sem("L_mm")
        E_done = sem("E_done")
        dec_done = sem("dec_done")
        G_mm = sem("G_mm")
        Gm_done = sem("Gm_done")
        M_v = sem("M_v")
        M_g = sem("M_g")
        xD_done = sem("xD_done")
        y_mm = sem("y_mm")
        y1_done = sem("y1_done")
        y2_done = sem("y2_done")
        sq_done = sem("sq_done")
        t2_mm = sem("t2_mm")
        t2_ev = sem("t2_ev")
        rsy_c = sem("rsy_c")
        o_mm = sem("o_mm")
        h2_done = sem("h2_done")
        ln2_c = sem("ln2_c")
        ln2_p = sem("ln2_p")
        n32_done = sem("n32_done")
        nhi_done = sem("nhi_done")
        nlo_done = sem("nlo_done")
        t3_mm = sem("t3_mm")
        t3_ev = sem("t3_ev")
        lg_mm = sem("lg_mm")
        lg_read = sem("lg_read")
        sm_exp = sem("sm_exp")
        sm_c = sem("sm_c")
        row_done = sem("row_done")
        st_rows = sems("st_rows", 2)

        rt_g = sem("rt_g")
        rt_v = sem("rt_v")
        rt_a = sem("rt_a")
        hot_i, hot_q = sem("hot_i"), sem("hot_q")
        hot_k = sem("hot_k")
        hot_p = sem("hot_p")
        rt_count = sem("rt_count")
        rt_slots = sem("rt_slots")
        rt_done = sem("rt_done")
        f_ids = sem("f_ids")
        f_oids = sem("f_oids")
        f_rows = sems("f_rows", 4)
        f_out = sems("f_out", 4)
        fx_mm = sem("fx_mm")
        fx_ev = sem("fx_ev")
        hid_mm = sem("hid_mm")
        gelu_done = sems("gelu_done", 2)
        hi_done = sems("hi_done", 2)
        lo_done = sems("lo_done", 2)
        two_mm = sem("two_mm")
        mix_c = sem("mix_c")
        mix_done = sem("mix_done")

        block = ctx.enter_context(nc.Block())

        def pair(q):
            return 2 + 2 * (q % 2)

        x_blocks = x.rearrange("b c (h i) w -> (b c h) (i w)", i=16)
        emb_rows = h_rows[N_TEXT * TIMES:TOKENS, :].rearrange("(f p b) d -> p b f d", f=2, b=TIMES)
        out_rows = out.rearrange("b n d -> (b n) d")

        N_SMALL_LOADS = 21
        PREP_V = 17
        MX_FIRST, MX_V = 8, 13
        SC_ROUTER, SC_ALL = 18, 29
        DT_LINKS = 9 + LOG1P_TERMS - 1
        RT_COUNT, RT_SLOT = 16, 35
        SM_LINKS = 8
        WP_BANKS = ((0, 5), (5, 5), (10, 4))
        T2_BANK = (2, 3, 4)
        Y_BANK = (7, 6, 7)
        O_BANK, O_COL = (1, 1, 0), (0, D, 0)

        def pix_move(group, u, q, w0, nw_):
            src = ps[:, 1 + 3 * u + q, 0:nw_ * RB].rearrange("p (w r) -> p w r", r=RB)
            dst = XT[group.par][u].rearrange("p (r w) -> p w r", w=14)[:, w0:w0 + nw_]
            return dst, src

        def valid(group, total=GROUPS):
            n = group.n
            return not isinstance(n, int) or 0 <= n < total

        LOOP0, LOOP1 = 8, 28
        SLOT_LOOP0, SLOT_LOOP1 = 8, 92

        def pipeline(eng, step, first=-1, loop0=LOOP0, loop1=LOOP1, last=GROUPS + 3, cycle=2):
            for n in range(first, loop0):
                step(Group(n // cycle, n % cycle, cycle))
            with eng.Fori(loop0 // cycle, loop1 // cycle) as j:
                for r in range(cycle):
                    step(Group(j, r, cycle))
            for n in range(loop1, last):
                step(Group(n // cycle, n % cycle, cycle))

        def patch_pipeline(eng, step, between=None, later_on=None):
            step(Group(0, 0))
            step(Group(0, 1))
            if between:
                between()
            with eng.Fori(1, 3) as j:
                step(Group(j, 0))
                step(Group(j, 1))
            step(Group(3, 0))
            if later_on:
                later_on()
            step(Group(3, 1))
            step(Group(4, 0))

        SPLIT_AT = [0, 1, 2, 3, 4, 5, LOOP1, LOOP1 + 1, LOOP1 + 2]

        def split_of(group):
            return SPLIT_AT.index(group.n) if isinstance(group.n, int) and group.n in SPLIT_AT else None

        def slot_pipeline(eng, step):
            pipeline(eng, step, -2, SLOT_LOOP0, SLOT_LOOP1, SLOT_TILES + 1, 4)

        def slot_valid(group):
            return valid(group, SLOT_TILES)

        def form_M(eng, k):
            g = G_m[:, k, :].rearrange("p (n j) -> p n j", j=TIMES).unsqueeze(1).to_broadcast([P, HEADS, POS_TILE, TIMES])
            d = decay.rearrange("p (k h j) -> p k h j", k=GT, h=HEADS)[:, k].unsqueeze(2).to_broadcast([P, HEADS, POS_TILE, TIMES])
            return eng.tensor_tensor(M_all[:, k].rearrange("p h (n j) -> p h n j", j=TIMES), g, d, ALU.mult)

        @block.sync
        def _(sp):
            sp.dma_start(patch_W, tok_W.rearrange("(a p) k -> p a k", a=2)).then_inc(ld_pw, 16)
            sp.dma_start(pix[0], x_blocks[0:RB, 0:HALF]).then_inc(ld_pix[0], 16)
            sp.dma_start(pix[1], x_blocks[0:RB, HALF:2 * HALF]).then_inc(ld_pix[1], 16)

            def load_pix(group):
                for u in range(2):
                    row0 = group.n * RB
                    if not isinstance(row0, int):
                        row0 = sp.snap(row0)
                    at_least(sp, pix_cut, group.n * 2 + u - 1)
                    sp.dma_start(pix[u], x_blocks[bass.ds(row0, RB), u * HALF:(u + 1) * HALF]).then_inc(ld_pix[u], 16)

            def load_stage(e):
                one = lambda ap: ap[bass.ds(e, 1)].rearrange("a p f -> p (a f)") if len(ap.shape) == 3 else ap[bass.ds(e, 1)]
                sp.dma_start(stage[:, 0:D_FF], one(W1[:, 0:DK0, :])).then_inc(ld_stage, 16)
                for i in range(2):
                    sp.dma_start(stage[i * DK1:(i + 1) * DK1, D_FF:2 * D_FF], one(W1[:, DK0:D, :])).then_inc(ld_stage, 16)
                sp.dma_start(stage[:, 2 * D_FF:STAGE].rearrange("p (a c d) -> p a c d", a=1, d=D),
                             W2.rearrange("e (c p) d -> p e c d", p=P)[:, bass.ds(e, 1)]).then_inc(ld_stage, 16)

            load_stage(0)
            load_pix(Group(0, 1))

            def patch_step(s):
                nxt, prv = s.shift(2), s.shift(-1)
                if valid(nxt, 8):
                    load_pix(nxt)
                if valid(prv, 8):
                    for b in range(2):
                        entry = prv.n * 2 + b
                        if not isinstance(entry, int):
                            entry = sp.snap(entry)
                        at_least(sp, emb_v, 2 * prv.n + b + 1)
                        sp.dma_start(emb_rows[:, bass.ds(entry, 1)], hp[b].unsqueeze(1)).then_inc(st_emb[b], 16)
                e = s.shift(1).n
                if not isinstance(e, int):
                    e = sp.snap(e)
                at_least(sp, mx_done, s.n + 1)
                load_stage(e if not isinstance(e, int) or e < EXPERTS else 0)

            def load_rows(dst, group, s):
                row0 = group.n * (GT * P)
                if not isinstance(row0, int):
                    row0 = sp.snap(row0)
                return dst, row0, s

            def load_h(group):
                dst, row0, s = load_rows(h_in[group.par], group, ld_h)
                at_least(sp, x32_done, group.n - 1)
                sp.dma_start(dst, h_rows[bass.ds(row0, GT * P), :].rearrange("(k p) d -> p k d", p=P)).then_inc(ld_h[group.par], 16)

            def load_res(group):
                dst, row0, s = load_rows(rows[group.par][:, :, D:2 * D], group, ld_res)
                at_least(sp, st_rows[group.par], 16 * group.j)
                sp.dma_start(dst, h_rows[bass.ds(row0, GT * P), :].rearrange("(k p) d -> p k d", p=P)).then_inc(ld_res[group.par], 16)

            def store_rows(group):
                row0 = group.n * (GT * P)
                if not isinstance(row0, int):
                    row0 = sp.snap(row0)
                at_least(sp, row_done, group.n + 1)
                sp.dma_start(ffn_rows[bass.ds(row0, GT * P), :].rearrange("(k p) d -> p k d", p=P), rows[group.par]).then_inc(st_rows[group.par], 16)

            def step(group):
                if valid(group.shift(2)):
                    load_h(group.shift(2))
                if valid(group.shift(-3)):
                    store_rows(group.shift(-3))
                if valid(group.shift(-1)):
                    load_res(group.shift(-1))
                e = split_of(group)
                if e is not None:
                    if e + 1 < EXPERTS:
                        sp.wait_ge(cv_hi, e + 1)
                        sp.wait_ge(cv_lo, e + 1)
                        load_stage(e + 1)
                if e == 1:
                    sp.wait_ge(bias_v, 4)
                    for r, (one, two) in enumerate(((b1_hi, b2_hi), (b1_lo, b2_lo))):
                        sp.dma_start(b1_rows[r].rearrange("(p c) -> p c", c=B1C), one[:, :]).then_inc(st_b, 16)
                        sp.dma_start(b2_rows[r].rearrange("(p c) -> p c", c=B2R), two[:, :]).then_inc(st_b, 16)
                    sp.wait_ge(st_b, 64)
                    sp.dma_start(W1E[DK1:E_ROWS, :, :].rearrange("a e f -> a (e f)"), b1_rows).then_inc(ld_experts, 16)
                    sp.dma_start(b2h[:, :, :].rearrange("a e f -> a (e f)"), b2_rows).then_inc(ld_experts, 16)

            def first_rows():
                sp.wait_ge(txt_copied, 16)
                load_h(Group(0, 0))

            patch_pipeline(sp, patch_step, None, first_rows)
            sp.wait_ge(pad_zeroed, 16)
            sp.wait_ge(st_emb[0], 16 * 8)
            sp.wait_ge(st_emb[1], 16 * 8)
            pipeline(sp, step)

            for r in range(4):
                sp.wait_ge(f_out[r], 16 * ((SLOT_TILES - r + 3) // 4))

        @block.gpsimd
        def _(pool):
            pool.memset(zeros, 0.0).then_inc(prep_g, 1)
            pool.memset(ident[:, :], 0.0).then_inc(prep_g, 1)
            pool.wait_ge(prep_g, 2)
            pool.affine_select(out=ident[:, :], in_=ident[:, :], compare_op=ALU.not_equal, fill=1.0, base=0,
                               pattern=[[-1, P]], channel_multiplier=1).then_inc(prep_g, 1)
            pool.memset(later[:, :], 1.0).then_inc(prep_g, 1)
            pool.memset(causal[:, :], 1.0).then_inc(prep_g, 1)
            pool.memset(minus_half[:, :], -0.5).then_inc(prep_g, 1)
            pool.wait_ge(prep_g, 6)
            pool.tensor_copy(ident_h[:, :], ident[:, :]).then_inc(prep_g, 1)
            pool.dma_start(h_rows[TOKENS:ROWS, :].rearrange("(p a) d -> p (a d)", p=96),
                           zeros[0:96, :]).then_inc(pad_zeroed, 16)
            blocks = [[-TIMES, POS_TILE], [0, TIMES]]
            up_blocks = [[TIMES, POS_TILE], [0, TIMES]]
            pool.affine_select(out=later[:, :], in_=later[:, :], compare_op=ALU.is_gt, fill=0.0, base=0,
                               pattern=[[-1, P]], channel_multiplier=1).then_inc(prep_g, 1)
            pool.affine_select(out=causal[:, :], in_=causal[:, :], compare_op=ALU.is_ge, fill=0.0, base=0,
                               pattern=[[1, P]], channel_multiplier=-1).then_inc(prep_g, 1)
            pool.wait_ge(prep_g, 9)
            pool.affine_select(out=later[:, :], in_=later[:, :], compare_op=ALU.is_ge, fill=0.0, base=TIMES - 1,
                               pattern=up_blocks, channel_multiplier=-1).then_inc(prep_g, 1)
            pool.affine_select(out=causal[:, :], in_=causal[:, :], compare_op=ALU.is_ge, fill=0.0, base=0,
                               pattern=blocks, channel_multiplier=1).then_inc(prep_g, 1)
            pool.iota(iota9p9[:, :], [[1, EXPERTS]], base=9, channel_multiplier=0,
                      allow_small_or_imprecise_dtypes=True).then_inc(prep_g, 1)

            pool.wait_ge(ld_pix[1], 16 * 3)
            pool.dma_start(h_rows[0:N_TEXT * TIMES, :].rearrange("(n b) d -> n b d", b=TIMES),
                           txt.rearrange("b n d -> n b d")).then_inc(txt_copied, 16)
            RMAX = bass.bass_isa.ReduceOp.max
            pool.wait_ge(mx_v, MX_FIRST)
            pool.partition_all_reduce(magnitude_all[:, 0:2], magnitude[:, 0:2], P, RMAX).then_inc(sc_g, 1)

            def power(src, dst, sem_, group, scale, ready, count, times=1.0):
                ch = Chain(pool, sem_, group.n, 2 if dst is rsy else 4)
                at_least(pool, ready, count)
                settle(pool, settled_g)
                neg, shift, mean = {id(rs1): (neg1, shift1, mv1), id(rs2): (neg2, shift2, mv2), id(rsy): (None, None, None)}[id(dst)]
                tmp = {id(rs1): var1, id(rs2): var2, id(rsy): ms}[id(dst)]
                ch.link(pool.tensor_scalar(tmp, src, scale / times ** 2, EPS / times ** 2, ALU.mult, ALU.add))
                ch.step(pool.tensor_tensor(dst, tmp, minus_half[:, 0:GT], ALU.pow))
                if neg is not None:
                    ch.sync()
                    settle(pool, settled_g)
                    ch.link(pool.tensor_scalar(neg, dst, -1.0, None, ALU.mult))
                    ch.step(pool.tensor_tensor(shift, neg, mean.rearrange("p (k s) -> p s k", s=2)[:, 0, :], ALU.mult))
                ch.done()

            def lo_parts(dst, src):
                pool.tensor_tensor(dst[:, :, D:D + DK1], src[:, :, DK0:D], dst[:, :, DK0:D], ALU.subtract)
                return pool.tensor_tensor(dst[:, :, D + DK1:PK], src[:, :, 0:DK0], dst[:, :, 0:DK0], ALU.subtract)

            def step(group):
                nxt, prv, pp = group.shift(1), group.shift(-1), group.shift(-2)
                if valid(nxt):
                    at_least(pool, x32_done, nxt.n)
                if valid(nxt):
                    power(mv1.rearrange("p (k s) -> p s k", s=2)[:, 1, :], rs1, ln1_p, nxt, 1.0, ln1_c, 6 * (nxt.n + 1), X_SCALE)
                if valid(prv):
                    at_least(pool, dec_done, prv.n + 1)
                    at_least(pool, Gm_done, prv.n + 1)
                    at_least(pool, y_mm, 3 * prv.n)
                    form_M(pool, 1).then_inc(M_g, 1)
                if valid(prv):
                    form_M(pool, 2).then_inc(M_g, 1)
                if valid(nxt):
                    at_least(pool, xhi_done, nxt.n + 1)
                    lo_parts(xn_h, xn32).then_inc(xlo_done, 1)
                if valid(pp):
                    at_least(pool, n32_done, pp.n)
                if valid(pp):
                    power(mv2.rearrange("p (k s) -> p s k", s=2)[:, 1, :], rs2, ln2_p, pp, 1.0, ln2_c, 6 * (pp.n + 1), X_SCALE)
                if valid(pp):
                    at_least(pool, nhi_done, pp.n + 1)
                    lo_parts(rows_h[pp.par], n32).then_inc(nlo_done, 1)
                if valid(prv):
                    power(ssq, rsy, rsy_c, prv, 1.0 / D_INNER, sq_done, 3 * (prv.n + 1))
                if valid(group):
                    at_least(pool, silu_done, 4 * group.n + 3)
                    at_least(pool, y1_done, 3 * group.n)
                    for k in range(GT):
                        ins = pool.tensor_tensor(
                            xD[:, k, :].rearrange("p (h e) -> p h e", h=HEADS),
                            xs[group.par][:, k, :].rearrange("p (h e) -> p h e", h=HEADS),
                            D_bc[:, :].unsqueeze(2).to_broadcast([P, HEADS, HEADDIM]), ALU.mult)
                    ins.then_inc(xD_done, 1)
                if isinstance(group.n, int) and group.n == -1:
                    pool.wait_ge(mx_v, MX_V)
                    pool.partition_all_reduce(magnitude_all[:, 2:4], magnitude[:, 2:4], P, RMAX).then_inc(sc_g, 1)

            pipeline(pool, step)

            pool.wait_ge(st_rows[0], 16 * (GROUPS // 2))
            pool.wait_ge(st_rows[1], 16 * (GROUPS // 2))
            pool.iota(iota_q, [[1, P]], base=0, channel_multiplier=0, allow_small_or_imprecise_dtypes=True).then_inc(rt_g, 1)
            pool.iota(iota_i, [[1, SL]], base=0, channel_multiplier=0, allow_small_or_imprecise_dtypes=True).then_inc(rt_g, 1)
            pool.iota(iota_i16, [[1, SL]], base=0, channel_multiplier=0, allow_small_or_imprecise_dtypes=True).then_inc(rt_g, 1)
            pool.iota(row_p1, [[1, 1]], base=1, channel_multiplier=1, allow_small_or_imprecise_dtypes=True).then_inc(rt_g, 1)
            pool.memset(earlier_rows[:, :], 1.0).then_inc(rt_g, 1)
            pool.wait_ge(rt_g, 5)
            pool.affine_select(out=earlier_rows[:, :], in_=earlier_rows[:, :], compare_op=ALU.is_gt, fill=0.0, base=0,
                               pattern=[[1, P]], channel_multiplier=-1).then_inc(rt_g, 1)
            with pool.Fori(0, TILES // HOT) as j:
                k0 = pool.snap(j * HOT)
                ks = bass.ds(k0, HOT)
                pool.wait_ge(hot_i, j + 1)
                pool.tensor_tensor(at_i[:, ks, 0, :], at_i[:, ks, 1, :], iota_i16[:, ks].unsqueeze(2).to_broadcast([P, HOT, SL]), ALU.mult).then_inc(hot_k, 1)
            pool.wait_ge(rt_done, 1)

            def gather(t):
                at_least(pool, mix_done, t.n - 3)
                settle(pool, settled_g)
                pool.tensor_copy(ids_in[:, t.r:t.r + 1], row_ids[:, bass.ds(t.n, 1)]).then_inc(f_ids, 1)
                pool.wait_ge(f_ids, t.n + 1)
                settle(pool, settled_g)
                pool.indirect_dma_start(tok_row[t.r], None, ffn_rows,
                                        bass.IndirectOffsetOnAxis(ap=ids_in[:, t.r:t.r + 1], axis=0),
                                        bounds_check=ROWS - 1, oob_is_err=False).then_inc(f_rows[t.r], 16)

            def scatter(t):
                at_least(pool, f_out[t.r], 16 * t.j)
                settle(pool, settled_g)
                pool.tensor_copy(ids_out[:, t.r:t.r + 1], out_ids[:, bass.ds(t.n, 1)]).then_inc(f_oids, 1)
                pool.wait_ge(f_oids, t.n + 1)
                pool.wait_ge(mix_done, t.n + 1)
                settle(pool, settled_g)
                pool.indirect_dma_start(out_rows, bass.IndirectOffsetOnAxis(ap=ids_out[:, t.r:t.r + 1], axis=0),
                                        mixed[t.par], None,
                                        bounds_check=TOKENS - 1, oob_is_err=False).then_inc(f_out[t.r], 16)

            def slot_step(t):
                if slot_valid(t.shift(2)):
                    gather(t.shift(2))
                if slot_valid(t.shift(-1)):
                    scatter(t.shift(-1))

            slot_pipeline(pool, slot_step)
        @block.scalar
        def _(act):
            act.dma_start(tok_b_bc[:, :], tok_b.rearrange("(a d) -> a d", a=1).to_broadcast([P, D])).then_inc(ld_tb, 16)
            act.dma_start(conv_bc, conv_w.rearrange("(a c) k -> a (c k)", a=1).to_broadcast([P, 2048])).then_inc(ld_w, 16)
            for dst, rows_ in ((Wa, W_in[0:DK0, :]), (Wb[0:DK1], W_in[DK0:D, :]), (Wb[DK1:P], W_in[DK0:D, :])):
                act.dma_start(dst[:, 0:768], rows_[:, 0:768]).then_inc(ld_w, 16)
                act.dma_start(dst[:, PROJ:IN_W], rows_[:, 768:896]).then_inc(ld_w, 16)
                act.dma_start(dst[:, 768:PROJ], rows_[:, 896:902]).then_inc(ld_w, 16)
            cb = conv_b.rearrange("(a c) -> a c", a=1)
            act.dma_start(in_bias[:, 384:768], cb[:, 0:384]).then_inc(ld_w, 16)
            act.dma_start(in_bias[:, PROJ:IN_W], cb[:, 384:512]).then_inc(ld_w, 16)
            act.dma_start(in_bias[:, 768:PROJ], dt_bias.rearrange("(a c) -> a c", a=1)).then_inc(ld_w, 16)
            act.dma_start(small_in[:, 0:6], A_log.rearrange("(a c) -> a c", a=1).to_broadcast([P, 6])).then_inc(ld_w, 16)
            act.dma_start(D_bc[:, :], D_skip.rearrange("(a c) -> a c", a=1).to_broadcast([P, 6])).then_inc(ld_w, 16)
            act.dma_start(Wo[:, :, :], W_out.rearrange("(c p) d -> p c d", p=P)).then_inc(ld_w, 16)
            act.dma_start(ws_in[:, 0:EXPERTS], Ws[0:DK0, :]).then_inc(ld_w, 16)
            for i in range(2):
                act.dma_start(ws_in[i * DK1:(i + 1) * DK1, EXPERTS:2 * EXPERTS], Ws[DK0:D, :]).then_inc(ld_w, 16)
            act.dma_start(bs_in[:, :], bs.rearrange("(a c) -> a c", a=1)).then_inc(ld_w, 16)
            act.dma_start(nw, norm_w.rearrange("(c p) -> p c", p=P), allow_slow_non_contiguous=True).then_inc(ld_w, 16)
            act.dma_start(b1_in[:, :], b1.rearrange("e f -> (e f)").rearrange("(p c) -> p c", c=B1C)).then_inc(ld_b, 16)
            act.dma_start(b2_in[:, :], b2.rearrange("e f -> (e f)").rearrange("(p c) -> p c", c=B2R)).then_inc(ld_b, 16)

            def between():
                act.wait_ge(ld_w, 16 * N_SMALL_LOADS)
                act.activation(neg_A[:, :], small_in[:, 0:6], ACT.Exp).then_inc(prep_a, 1)

            def later_on():
                act.wait_ge(bias_v, 2)
                for r in range(2):
                    act.dma_start(WiE[DK1 + r:DK1 + r + 1, :], in_bias_h[:, r, :]).then_inc(ld_w, 16)
                    act.dma_start(WsE[DK1 + r:DK1 + r + 1, :], bs_h[:, r * EXPERTS:(r + 1) * EXPERTS]).then_inc(ld_w, 16)

            def patch_step(s):
                if valid(s, 8):
                    for u in range(2):
                        act.wait_ge(pix_T, s.n * 2 + u + 1)
                        at_least(act, emb_mm, 2 * (s.n - 1))
                        for q in (0, 1):
                            last = act.activation(*pix_move(s, u, q, *WP_BANKS[q]), ACT.Copy)
                        last.then_inc(pix_ev_a, 1)

            patch_pipeline(act, patch_step, between, later_on)

            def step(group):
                nxt, prv, pp, p3 = group.shift(1), group.shift(-1), group.shift(-2), group.shift(-3)
                par = group.par

                def tanh(q):
                    if not valid(group):
                        return
                    at_least(act, proj_mm, 4 * group.n + q + 1)
                    if q == 0:
                        at_least(act, y2_done, 3 * (group.n - 1))
                        at_least(act, y_mm, 3 * (group.n - 1))
                        at_least(act, G_mm, group.n - 1)
                    b = pair(q)
                    if q < 3:
                        act.activation(zs[par][:, q, :], ps[:, b, 0:384], ACT.Tanh, scale=inv_in[:, 0:1])
                        act.activation(xs[par][:, q, :], ps[:, b + 1, 0:384], ACT.Tanh, scale=inv_in[:, 0:1]).then_inc(th_done, 1)
                    else:
                        act.activation(Bs[par], ps[0:D_STATE, b, 0:384], ACT.Tanh, scale=inv_in[0:D_STATE, 0:1])
                        act.activation(Cs[par], ps[0:D_STATE, b + 1, 0:384], ACT.Tanh, scale=inv_in[0:D_STATE, 0:1]).then_inc(th_done, 1)

                def square(k):
                    if not valid(prv):
                        return
                    at_least(act, y2_done, 3 * prv.n + k + 1)
                    if k == 0:
                        at_least(act, rsy_c, 2 * prv.n)
                    at_least(act, sq_done, 3 * prv.n + k)
                    act.activation(sq, y[:, k, :], ACT.Square, accum_out=ssq[:, k:k + 1]).then_inc(sq_done, 1)

                def move_y(k):
                    if not valid(prv):
                        return
                    if k == 0:
                        at_least(act, o_mm, 3 * prv.n)
                    at_least(act, t2_mm, 3 * prv.n + k + 1)
                    act.activation(yT[:, k, :], ps[:, T2_BANK[k], 0:384], ACT.Copy).then_inc(t2_ev, 1)

                def move_split(AC, DD, E, sem_):
                    act.activation(AC, ps[:, 0, 0:384].bitcast(f16).rearrange("p (a k t) -> p a k t", a=2, k=GT), ACT.Copy).then_inc(sem_, 1)
                    src = ps[:, 1, 0:192].bitcast(f16).rearrange("p (k t) -> p k t", k=GT)
                    act.activation(DD, src, ACT.Copy).then_inc(sem_, 1)
                    act.activation(E[0:DK1], src[0:DK1], ACT.Copy).then_inc(sem_, 1)

                tanh(0)
                if valid(p3):
                    at_least(act, t3_mm, p3.n + 1)
                    at_least(act, lg_mm, p3.n)
                    move_split(nAC, nD, nE, t3_ev)
                if valid(prv):
                    at_least(act, L_mm, prv.n + 1)
                    at_least(act, M_v, prv.n)
                    at_least(act, M_g, 2 * prv.n)
                    act.activation(decay, ps[:, 6, 0:GT * HEADS * TIMES], ACT.Exp).then_inc(E_done, 1)
                tanh(1)
                if valid(nxt):
                    at_least(act, ln1_p, 4 * (nxt.n + 1))
                    at_least(act, t1_mm, nxt.n)
                    at_least(act, xlo_done, nxt.n)
                    for k in range(GT):
                        last = act.activation(xn32[:, k, :], h_in[nxt.par][:, k, :], ACT.Identity, scale=rs1[:, k:k + 1], bias=shift1[:, k:k + 1])
                    last.then_inc(x32_done, 1)
                    at_least(act, x32_done, nxt.n + 1)
                    act.activation(xn_h[:, :, 0:D], xn32, ACT.Copy).then_inc(xhi_done, 1)
                square(0)
                if valid(p3):
                    at_least(act, lg_read, p3.n + 1)
                    act.activation(le_, ld_, ACT.Exp, scale=inv_logit[:, 0:1]).then_inc(sm_exp, 1)
                tanh(2)
                if valid(group):
                    at_least(act, dt_c, DT_LINKS * group.n + 1)
                    act.activation(u_, nabs, ACT.Exp).then_inc(u_done, 1)
                tanh(3)
                if valid(nxt):
                    at_least(act, t1_mm, nxt.n + 1)
                    at_least(act, proj_mm, 4 * nxt.n)
                    move_split(xAC, xDD, xE, t1_ev)
                move_y(0)
                move_y(1)
                if valid(pp):
                    at_least(act, ln2_p, 4 * (pp.n + 1))
                    at_least(act, nlo_done, pp.n)
                    for k in range(GT):
                        last = act.activation(n32[:, k, :], rows[pp.par][:, k, D:2 * D], ACT.Identity, scale=rs2[:, k:k + 1], bias=shift2[:, k:k + 1])
                    last.then_inc(n32_done, 1)
                    at_least(act, n32_done, pp.n + 1)
                    act.activation(rows_h[pp.par][:, :, 0:D], n32, ACT.Copy).then_inc(nhi_done, 1)
                square(1)
                square(2)
                move_y(2)
                e = split_of(group)
                if e is not None:
                    act.wait_ge(ld_stage, 64 * (EXPERTS + e + 1))
                    act.wait_ge(sc_v, SC_ALL)
                    act.activation(W1A[:, e, :], stage[:, 0:D_FF], ACT.Identity, scale=scale[:, 2:3])
                    act.activation(W1D[:, e, :], stage[:, D_FF:2 * D_FF], ACT.Identity, scale=scale[:, 2:3])
                    act.activation(W2hi[:, e].rearrange("p c d -> p (c d)"), stage[:, 2 * D_FF:STAGE], ACT.Identity, scale=scale[:, 3:4]).then_inc(cv_hi, 1)

            pipeline(act, step)

            act.wait_ge(rt_g, 4)
            with act.Fori(0, TILES // HOT) as j:
                k0 = act.snap(j * HOT)
                ks = bass.ds(k0, HOT)
                act.wait_ge(hot_k, j + 1)
                act.activation(at_i[:, ks, 1, :], at_i[:, ks, 1, :], ACT.Identity, scale=row_p1).then_inc(hot_p, 1)
            act.wait_ge(rt_slots, 1)
            act.activation(sums, ps[:, 0, 0:2 * SL], ACT.Copy).then_inc(rt_a, 1)

            def slot_step(t):
                if slot_valid(t):
                    at_least(act, hid_mm, t.n + 1)
                    for i, bank in enumerate((3, 1)):
                        at_least(act, lo_done[i], t.n)
                        act.activation(g32[i].rearrange("p (b f) -> p b f", b=2), ps[:, bank:bank + 2, 0:384], ACT.Gelu, scale=inv_h[:, 0:1]).then_inc(gelu_done[i], 1)
                        at_least(act, gelu_done[i], t.n + 1)
                        at_least(act, two_mm, t.n - 1)
                        act.activation(g_hi[i][t.par], g32[i], ACT.Identity, scale=g_scale[:, 0:1]).then_inc(hi_done[i], 1)

            slot_pipeline(act, slot_step)

        @block.vector
        def _(dve):
            def cut(group):
                for u in range(2):
                    at_least(dve, ld_pix[u], 16 * (group.n + 1))
                    at_least(dve, pix_T, 2 * group.n + u - 1)
                    dve.tensor_copy(pix_by_patch[u].rearrange("p (w i j) -> p w i j", i=8, j=16),
                                    pix[u].rearrange("p (i w j) -> p w i j", i=8, j=16)).then_inc(pix_cut, 1)
                    if not isinstance(group.n, int) or group.n > 0:
                        move_pixels(group.shift(-1), u)

            def move_pixels(group, u):
                at_least(dve, pix_T, group.n * 2 + u + 1)
                at_least(dve, emb_mm, 2 * (group.n - 1))
                dve.tensor_copy(*pix_move(group, u, 2, *WP_BANKS[2])).then_inc(pix_ev_v, 1)

            ch = Chain(dve, prep_v, 0, 0)
            cut(Group(0, 0))
            dve.wait_ge(prep_pe, 1)
            for n, bank in enumerate((0, 7, 4)):
                dve.tensor_copy(patch_WT[:, n], ps[:, bank, 0:2 * D].rearrange("p (i d) -> p i d", i=2)).then_inc(prep_v, 1)
            ch.k = 3

            def set_scales(cols, links):
                c = Chain(dve, sc_v, 0, 0)
                c.k = links
                c.link(dve.tensor_scalar(magnitude_all[:, cols], magnitude_all[:, cols], 2.0 ** -20, 2.0 ** 60, ALU.max, ALU.min))
                c.link(dve.tensor_scalar(bits[:, cols].bitcast(i32), magnitude_all[:, cols].bitcast(i32), 0x7f800000, None, ALU.bitwise_and))
                c.step(dve.tensor_scalar(scale[:, cols].bitcast(i32), bits[:, cols].bitcast(i32), -1.0, float(268 << 23), ALU.mult, ALU.add))
                c.link(dve.tensor_scalar(inverse[:, cols], bits[:, cols], 2.0 ** -14, None, ALU.mult))
                return c

            def between():
                dve.memset(ones[:, :], 1.0)
                dve.wait_ge(ld_w, 16 * N_SMALL_LOADS)
                tap = conv_bc.rearrange("p (c k) -> p c k", k=4)[:, :, 3]
                for W in (Wa, Wb):
                    ch.step(dve.tensor_scalar(W[:, 0:384], W[:, 0:384], 0.5, None, ALU.mult))
                    ch.step(dve.scalar_tensor_tensor(W[:, 384:768], W[:, 384:768], 0.5, tap[:, 0:384], ALU.mult, ALU.mult))
                    ch.step(dve.scalar_tensor_tensor(W[:, PROJ:IN_W], W[:, PROJ:IN_W], 0.5, tap[:, 384:512], ALU.mult, ALU.mult))
                ch.step(dve.memset(in_bias[:, 0:384], 0.0))
                ch.step(dve.tensor_scalar(in_bias[:, 384:768], in_bias[:, 384:768], 0.5, None, ALU.mult))
                ch.step(dve.tensor_scalar(in_bias[:, PROJ:IN_W], in_bias[:, PROJ:IN_W], 0.5, None, ALU.mult))
                for c in range(3):
                    ch.step(dve.tensor_scalar(Wo[:, c, :], Wo[:, c, :], nw[:, c:c + 1], None, ALU.mult))
                dve.wait_ge(prep_a, 1)
                ch.step(dve.tensor_scalar(neg_A[:, :], neg_A[:, :], -1.0, None, ALU.mult))
                dve.wait_ge(prep_g, 12)
                ch.step(dve.tensor_reduce(causal16[:, :], causal[:, :].rearrange("p (n j) -> p j n", j=TIMES), AX.X, ALU.add))
                ch.sync()
                mx = Chain(dve, mx_v, 0, 0)

                def largest(dst, src):
                    return dve.tensor_reduce(dst, src, AX.X, ALU.max, apply_absolute_value=True)

                mx.step(largest(magnitude[:, 0:1], ws_in[:, :]))
                mx.step(largest(sizes[:, 0:1], Wa))
                mx.step(largest(sizes[:, 1:2], Wb))
                mx.step(dve.memset(sizes[:, 2:4], 0.0))
                mx.sync()
                mx.step(largest(sizes[0:1, 2:3], in_bias))
                mx.link(largest(sizes[0:1, 3:4], bs_in[:, :]))
                mx.step(dve.tensor_reduce(magnitude[:, 1:2], sizes[:, 0:3], AX.X, ALU.max))
                mx.step(dve.tensor_tensor(magnitude[:, 0:1], magnitude[:, 0:1], sizes[:, 3:4], ALU.max))
                assert mx.k == MX_FIRST, mx.k
                mx.sync()

            def split_small():
                dve.wait_ge(sc_g, 1)
                sc = set_scales(slice(0, 2), 0)
                s0, s1 = scale[:, 0:1], scale[:, 1:2]
                sc.step(dve.tensor_scalar(inv_logit[:, :], inverse[:, 0:1], 1.0 / X_SCALE, None, ALU.mult))
                sc.link(dve.tensor_scalar(inv_in[:, :], inverse[:, 1:2], 1.0 / X_SCALE, None, ALU.mult))
                sc.link(dve.tensor_tensor(inv_in2[:, :], inv_in[:, :], inv_in[:, :], ALU.mult))
                sc.step(dve.tensor_scalar(causal_s[:, :], causal[:, :], inv_in2[:, :], None, ALU.mult))
                for src_a, src_b, bias, bias_hl, by, (A, B, DD, E) in (
                        (ws_in[:, 0:EXPERTS], ws_in[:, EXPERTS:2 * EXPERTS], bs_in[:, :], (bs_h[:, 0:EXPERTS], bs_h[:, EXPERTS:2 * EXPERTS]), s0, (WsA, WsB, WsD, WsE)),
                        (Wa, Wb, in_bias, (in_bias_h[:, 0, :], in_bias_h[:, 1, :]), s1, (WiA, WiB, WiD, WiE))):
                    sc.step(dve.tensor_scalar(A[:, :], src_a, by, None, ALU.mult))
                    sc.step(dve.tensor_scalar(DD[:, :], src_b, by, None, ALU.mult))
                    sc.link(dve.tensor_scalar(bias_hl[0], bias, by[0:1], None, ALU.mult))
                    sc.step(dve.scalar_tensor_tensor(B[:, :], src_a, by, A[:, :], ALU.mult, ALU.subtract))
                    sc.step(dve.scalar_tensor_tensor(E[0:DK1, :], src_b[0:DK1], by[0:DK1], DD[0:DK1, :], ALU.mult, ALU.subtract))
                    dve.scalar_tensor_tensor(bias_hl[1], bias, by[0:1], bias_hl[0], ALU.mult, ALU.subtract).then_inc(bias_v, 1)
                assert sc.k == SC_ROUTER, sc.k

            def patch_step(s):
                nxt, prv = s.shift(1), s.shift(-1)
                if valid(nxt, 8):
                    cut(nxt)
                elif valid(s, 8):
                    for u in range(2):
                        move_pixels(s, u)
                if valid(prv, 8):
                    if not valid(prv.shift(-1)):
                        dve.wait_ge(ld_tb, 16)
                    for b in range(2):
                        at_least(dve, emb_mm, 2 * prv.n + b + 1)
                        at_least(dve, st_emb[b], 16 * prv.n)
                        dve.tensor_tensor(hp[b], ps[0:ET, 7 * b, 0:2 * D].rearrange("p (f d) -> p f d", f=2),
                                          tok_b_bc[0:ET, :].unsqueeze(1).to_broadcast([ET, 2, D]), ALU.add).then_inc(emb_v, 1)
                at_least(dve, ld_stage, 64 * (s.n + 1))
                dve.tensor_reduce(sizes[:, bass.ds(s.n, 1)], stage[:, 0:2 * D_FF], AX.X, ALU.max, apply_absolute_value=True)
                dve.tensor_reduce(sizes2[:, bass.ds(s.n, 1)], stage[:, 2 * D_FF:STAGE], AX.X, ALU.max, apply_absolute_value=True).then_inc(mx_done, 1)

            patch_pipeline(dve, patch_step, between, split_small)
            dve.memset(xE[DK1:E_ROWS], X_SCALE)
            dve.memset(nE[DK1:E_ROWS], X_SCALE).then_inc(prep_v, 1)

            def expert_scales():
                dve.wait_ge(ld_b, 32)
                dve.wait_ge(mx_done, EXPERTS)
                mx = Chain(dve, mx_v, 0, 0)
                mx.k = MX_FIRST
                dve.wait_ge(sc_v, SC_ROUTER)
                mx.step(dve.memset(sizes2[:, EXPERTS:EXPERTS + 1], 0.0))
                mx.link(dve.tensor_reduce(sizes[:, EXPERTS:EXPERTS + 1], b1_in[:, :], AX.X, ALU.max, apply_absolute_value=True))
                mx.link(dve.tensor_reduce(sizes2[0:B2P, EXPERTS:EXPERTS + 1], b2_in[:, :], AX.X, ALU.max, apply_absolute_value=True))
                mx.step(dve.tensor_reduce(magnitude[:, 2:3], sizes[:, :], AX.X, ALU.max))
                mx.step(dve.tensor_reduce(magnitude[:, 3:4], sizes2[:, :], AX.X, ALU.max))
                assert mx.k == MX_V, mx.k
                dve.wait_ge(sc_g, 2)
                sc = set_scales(slice(2, 4), SC_ROUTER)
                sc.step(dve.tensor_scalar(inv_h[:, :], inverse[:, 2:3], 1.0 / X_SCALE, None, ALU.mult))
                sc.link(dve.tensor_scalar(g_scale[:, :], scale[:, 2:3], 2.0 ** -7, 2.0 ** 15, ALU.mult, ALU.min))
                sc.link(dve.tensor_scalar(g_scale[:, :], g_scale[:, :], 2.0 ** -14, None, ALU.max))
                sc.step(dve.tensor_scalar(g_scale_row[:, :], ones[0:2, :], g_scale[0:2, :], None, ALU.mult))
                sc.link(dve.reciprocal(inv_out[:, :], g_scale[:, :]))
                sc.link(dve.tensor_scalar(inv_out[:, :], inv_out[:, :], inverse[:, 3:4], None, ALU.mult))
                sc.step(dve.tensor_scalar(neg_inv_out[:, :], inv_out[:, :], -1.0, None, ALU.mult))
                assert sc.k == SC_ALL, sc.k
                for src, hi, lo, by, n in ((b1_in, b1_hi, b1_lo, scale[:, 2:3], P), (b2_in, b2_hi, b2_lo, scale[:, 3:4], B2P)):
                    sc.link(dve.tensor_scalar(hi[:, :], src[:, :], by[0:n], None, ALU.mult))
                    dve.scalar_tensor_tensor(lo[:, :], src[:, :], by[0:n], hi[:, :], ALU.mult, ALU.subtract).then_inc(bias_v, 1)

            def step(group):
                nxt, prv, pp, p3 = group.shift(1), group.shift(-1), group.shift(-2), group.shift(-3)
                par = group.par
                e3 = lambda t: t.rearrange("p (k e) -> p k e", k=GT)
                bc = lambda t: t.unsqueeze(2).to_broadcast([P, GT, EXPERTS])
                cd = Chain(dve, dt_c, group.n, DT_LINKS)

                def silu(q):
                    if not valid(group):
                        return
                    at_least(dve, th_done, 4 * group.n + q + 1)
                    b = pair(q)
                    if q < 3:
                        if q == 0:
                            at_least(dve, dec_in_done, group.n)
                            at_least(dve, dt_c, DT_LINKS * group.n)
                        dve.tensor_scalar(dtv[:, q * HEADS:(q + 1) * HEADS], ps[:, b + 1, 384:390], inv_in[:, 0:1], None, ALU.mult)
                        dve.scalar_tensor_tensor(zs[par][:, q, :], zs[par][:, q, :], 1.0, ps[:, b, 0:384], ALU.add, ALU.mult)
                        dve.scalar_tensor_tensor(xs[par][:, q, :], xs[par][:, q, :], 1.0, ps[:, b + 1, 0:384], ALU.add, ALU.mult).then_inc(silu_done, 1)
                    else:
                        dve.scalar_tensor_tensor(Bs[par], Bs[par], 1.0, ps[0:D_STATE, b, 0:384], ALU.add, ALU.mult)
                        dve.scalar_tensor_tensor(Cs[par], Cs[par], 1.0, ps[0:D_STATE, b + 1, 0:384], ALU.add, ALU.mult).then_inc(silu_done, 1)

                def y_tile(k):
                    if not valid(prv):
                        return
                    at_least(dve, y_mm, 3 * prv.n + k + 1)
                    if k == 0:
                        at_least(dve, xD_done, prv.n + 1)
                        at_least(dve, t2_mm, 3 * prv.n)
                        at_least(dve, sq_done, 3 * prv.n)
                    dve.tensor_tensor(y[:, k, :], ps[:, Y_BANK[k], 0:384], xD[:, k, :], ALU.add).then_inc(y1_done, 1)
                    at_least(dve, y1_done, 3 * prv.n + k + 1)
                    dve.scalar_tensor_tensor(y[:, k, :], y[:, k, :], inv_in2[:, 0:1], zs[prv.par][:, k, :], ALU.mult, ALU.mult).then_inc(y2_done, 1)

                def statistics(ch, st, mv, src):
                    for k in range(GT):
                        ch.step(dve.bn_stats(st[:, 6 * k:6 * k + 6], src[:, k]))
                    ch.sync()
                    settle(dve, settled_v)
                    for k in range(GT):
                        ch.step(dve.bn_aggr(mv[:, 2 * k:2 * k + 2], st[:, 6 * k:6 * k + 6]))
                    ch.done()

                silu(0)
                if valid(nxt):
                    c1 = Chain(dve, ln1_c, nxt.n, 6)
                    at_least(dve, ld_h[nxt.par], 16 * (nxt.j + 1))
                    at_least(dve, ln1_p, 4 * nxt.n)
                    statistics(c1, st1, mv1, h_in[nxt.par])
                silu(1)
                if valid(prv):
                    at_least(dve, E_done, prv.n + 1)
                    dve.tensor_tensor(decay.rearrange("p (s j) -> p s j", j=TIMES), decay.rearrange("p (s j) -> p s j", j=TIMES),
                                      dts.unsqueeze(2).to_broadcast([P, SH, TIMES]), ALU.mult).then_inc(dec_done, 1)
                    at_least(dve, dec_done, prv.n + 1)
                    at_least(dve, Gm_done, prv.n + 1)
                    at_least(dve, y_mm, 3 * prv.n)
                    form_M(dve, 0).then_inc(M_v, 1)
                if valid(p3):
                    cs = Chain(dve, sm_c, p3.n, SM_LINKS)
                    at_least(dve, lg_mm, p3.n + 1)
                    if valid(pp):
                        at_least(dve, o_mm, 3 * (pp.n + 1))
                    lg = ps[:, 0, 384:384 + GT * EXPERTS].rearrange("p (k e) -> p k e", k=GT)
                    at_least(dve, row_done, p3.n)
                    cs.step(dve.tensor_reduce(lmax, lg, AX.X, ALU.max))
                if valid(pp):
                    at_least(dve, rsy_c, 2 * (pp.n + 1))
                    at_least(dve, ld_res[pp.par], 16 * (pp.j + 1))
                    for k in range(GT):
                        at_least(dve, o_mm, 3 * pp.n + max(k + 1, 2))
                        dve.scalar_tensor_tensor(rows[pp.par][:, k, D:2 * D], ps[:, O_BANK[k], O_COL[k]:O_COL[k] + D], rsy[:, k:k + 1],
                                                 rows[pp.par][:, k, D:2 * D], ALU.mult, ALU.add).then_inc(h2_done, 1)
                y_tile(0)
                if valid(p3):
                    cs.sync()
                    dve.tensor_tensor(e3(ld_), lg, bc(lmax), ALU.subtract).then_inc(lg_read, 1)
                if valid(pp):
                    c2 = Chain(dve, ln2_c, pp.n, 6)
                    at_least(dve, ln2_p, 4 * pp.n)
                    at_least(dve, h2_done, 3 * (pp.n + 1))
                    statistics(c2, st2, mv2, rows[pp.par][:, :, D:2 * D])
                silu(2)
                if valid(group):
                    at_least(dve, silu_done, 4 * group.n + 3)
                    cd.step(dve.scalar_tensor_tensor(nabs, dtv, -1.0, dtv, ALU.mult, ALU.min))
                y_tile(1)
                silu(3)
                y_tile(2)
                dt_on, sm_on = valid(group), valid(p3)
                if sm_on:
                    r_now = routes[:, bass.ds(p3.n * GT, GT)]
                    at_least(dve, sm_exp, p3.n + 1)
                    cs.step(dve.tensor_reduce(rsum, e3(le_), AX.X, ALU.add))
                if dt_on:
                    at_least(dve, u_done, group.n + 1)
                    cd.step(dve.tensor_scalar(den, u_, 2.0, None, ALU.add))
                if sm_on:
                    cs.sync()
                    cs.step(dve.reciprocal(rrec, rsum))
                if dt_on:
                    cd.sync()
                    cd.step(dve.reciprocal(rec, den))
                if sm_on:
                    cs.sync()
                    cs.step(dve.tensor_tensor(e3(pr_), e3(le_), bc(rrec), ALU.mult))
                if dt_on:
                    cd.sync()
                    cd.step(dve.tensor_tensor(s_, u_, rec, ALU.mult))
                if sm_on:
                    cs.sync()
                    cs.step(dve.tensor_reduce(pmax, e3(pr_), AX.X, ALU.max))
                if dt_on:
                    cd.sync()
                    cd.step(dve.tensor_tensor(w_, s_, s_, ALU.mult))
                if sm_on:
                    cs.sync()
                    cs.step(dve.tensor_tensor(e3(eq_), e3(pr_), bc(pmax), ALU.is_equal))
                if dt_on:
                    cd.sync()
                    cd.step(dve.tensor_scalar(ser, w_, 1.0 / (2 * LOG1P_TERMS - 1), None, ALU.mult))
                if sm_on:
                    cs.sync()
                    cs.step(dve.scalar_tensor_tensor(e3(cand), e3(eq_), -9.0, iota9p9[:, :].unsqueeze(1).to_broadcast([P, GT, EXPERTS]), ALU.mult, ALU.add))
                if dt_on:
                    cd.sync()
                    cd.step(dve.scalar_tensor_tensor(ser, ser, 1.0 / (2 * LOG1P_TERMS - 3), w_, ALU.add, ALU.mult))
                if sm_on:
                    cs.sync()
                    cs.step(dve.tensor_reduce(r_now, e3(cand), AX.X, ALU.min))
                if dt_on:
                    cd.sync()
                    cd.step(dve.scalar_tensor_tensor(ser, ser, 1.0 / (2 * LOG1P_TERMS - 5), w_, ALU.add, ALU.mult))
                if sm_on:
                    cs.sync()
                    cs.done()
                    dve.scalar_tensor_tensor(rows[p3.par][:, :, 2 * D:ROW_W].rearrange("p k a -> p (k a)"), r_now, 0.5, pmax,
                                             ALU.is_gt, ALU.mult).then_inc(row_done, 1)
                if dt_on:
                    cd.sync()
                    cd.step(dve.tensor_scalar(relu, dtv, 0.0, None, ALU.max))
                    for m in range(LOG1P_TERMS - 4, 0, -1):
                        cd.link(dve.scalar_tensor_tensor(ser, ser, 1.0 / (2 * m + 1), w_, ALU.add, ALU.mult))
                    cd.link(dve.scalar_tensor_tensor(ser, ser, 1.0, s_, ALU.add, ALU.mult))
                    at_least(dve, dec_done, group.n)
                    cd.link(dve.scalar_tensor_tensor(dts, ser, 2.0, relu, ALU.mult, ALU.add))
                    cd.link(dve.tensor_tensor(a_.rearrange("p (k h) -> p k h", k=GT), dts.rearrange("p (k h) -> p k h", k=GT),
                                              neg_A[:, :].unsqueeze(1).to_broadcast([P, GT, HEADS]), ALU.mult))
                    cd.done()
                    at_least(dve, L_mm, group.n)
                    dve.tensor_tensor(decay_in.rearrange("p (s j) -> p s j", j=TIMES),
                                      a_.unsqueeze(2).to_broadcast([P, SH, TIMES]),
                                      causal16[:, :].unsqueeze(1).to_broadcast([P, SH, TIMES]), ALU.mult).then_inc(dec_in_done, 1)
                if valid(group):
                    at_least(dve, G_mm, group.n + 1)
                    at_least(dve, M_v, group.n)
                    at_least(dve, M_g, 2 * group.n)
                    dve.tensor_tensor(G_m, ps[:, 7, 0:384].rearrange("p (k t) -> p k t", k=GT),
                                      causal_s[:, :].unsqueeze(1).to_broadcast([P, GT, P]), ALU.mult).then_inc(Gm_done, 1)
                if isinstance(group.n, int) and group.n == -1:
                    expert_scales()
                e = split_of(group)
                if e is not None:
                    dve.wait_ge(cv_hi, e + 1)
                    s1, s2 = scale[:, 2:3], scale[:, 3:4]
                    dve.scalar_tensor_tensor(W1B[:, e, :], stage[:, 0:D_FF], s1, W1A[:, e, :], ALU.mult, ALU.subtract)
                    dve.scalar_tensor_tensor(W1E[0:DK1, e, :], stage[0:DK1, D_FF:2 * D_FF], s1[0:DK1], W1D[0:DK1, e, :], ALU.mult, ALU.subtract)
                    dve.scalar_tensor_tensor(W2lo[:, e].rearrange("p c d -> p (c d)"), stage[:, 2 * D_FF:STAGE], s2,
                                             W2hi[:, e].rearrange("p c d -> p (c d)"), ALU.mult, ALU.subtract).then_inc(cv_lo, 1)

            pipeline(dve, step)

            dve.wait_ge(st_rows[0], 16 * (GROUPS // 2))
            dve.wait_ge(st_rows[1], 16 * (GROUPS // 2))
            dve.wait_ge(cv_lo, EXPERTS)
            rc = Chain(dve, rt_v, 0, 0)
            full = TOKENS // P
            rc.step(dve.memset(routes[TOKENS - full * P:P, full:full + 1], float(EXPERTS)))
            rc.step(dve.memset(routes[:, full + 1:TILES], float(EXPERTS)))
            rc.link(dve.memset(no_add, 0.0))
            for e in range(EXPERTS):
                rc.step(dve.tensor_scalar(onehot[:, e, :], routes[:, :], float(e), None, ALU.is_equal))
            rc.sync()
            flat = onehot.rearrange("p e k -> p (e k)")
            rc.link(dve.tensor_tensor_scan(running, flat, no_add, 0.0, ALU.add, ALU.add))
            r3 = running.rearrange("p (e k) -> p e k", e=EXPERTS)
            rc.link(dve.tensor_tensor(to_slot, r3, onehot, ALU.subtract))
            rc.link(dve.tensor_copy(seg0, to_slot[:, :, 0]))
            rc.link(dve.tensor_tensor(count, r3[:, :, TILES - 1], seg0, ALU.subtract))
            assert rc.k == RT_COUNT, rc.k
            dve.wait_ge(rt_count, 1)
            rc.step(dve.tensor_copy(before, ps[:, 1, 0:EXPERTS]))
            rc.link(dve.tensor_scalar(total_e, ps[:, 2, 0:EXPERTS], float(P - 1), None, ALU.add))
            rc.link(dve.tensor_copy(cnt_i, total_e))
            rc.link(dve.tensor_scalar(cnt_i, cnt_i, 7, None, ALU.logical_shift_right))
            rc.link(dve.tensor_copy(tiles_e, cnt_i))
            rc.link(dve.tensor_tensor_scan(tile_end, tiles_e, no_add[:, 0:EXPERTS], 0.0, ALU.add, ALU.add))
            rc.link(dve.tensor_tensor(slot0, tile_end, tiles_e, ALU.subtract))
            rc.link(dve.scalar_tensor_tensor(slot0, slot0, float(P), before, ALU.mult, ALU.add))
            rc.link(dve.tensor_tensor(slot0, slot0, seg0, ALU.subtract))
            rc.link(dve.tensor_tensor(to_slot, to_slot, slot0.unsqueeze(2).to_broadcast([P, EXPERTS, TILES]), ALU.add))
            rc.link(dve.tensor_tensor(to_slot, to_slot, onehot, ALU.mult))
            rc.link(dve.tensor_reduce(slot, to_slot.rearrange("p e k -> p k e"), AX.X, ALU.add))
            rc.link(dve.tensor_scalar(is_pad, routes[:, :], EXPERTS - 0.5, float(2 * SL * P), ALU.is_gt, ALU.mult))
            rc.link(dve.tensor_tensor(slot, slot, is_pad, ALU.add))
            rc.link(dve.tensor_copy(ints[0], slot))
            rc.step(dve.tensor_scalar(ints[1], ints[0], P - 1, None, ALU.bitwise_and))
            rc.link(dve.tensor_scalar(ints[2], ints[0], 7, None, ALU.logical_shift_right))
            rc.step(dve.tensor_copy(slot_q, ints[1]))
            rc.link(dve.tensor_copy(slot_i, ints[2]))
            assert rc.k == RT_SLOT, rc.k
            dve.wait_ge(rt_g, 6)
            with dve.Fori(0, TILES // HOT) as j:
                k0 = dve.snap(j * HOT)
                ks = bass.ds(k0, HOT)
                dve.tensor_tensor(at_i[:, ks, 1, :], iota_i16.unsqueeze(1).to_broadcast([P, HOT, SL]),
                                  slot_i[:, ks].unsqueeze(2).to_broadcast([P, HOT, SL]), ALU.is_equal).then_inc(hot_i, 1)
                dve.tensor_tensor(at_q[:, ks, :], iota_q.unsqueeze(1).to_broadcast([P, HOT, P]),
                                  slot_q[:, ks].unsqueeze(2).to_broadcast([P, HOT, P]), ALU.is_equal).then_inc(hot_q, 1)
            rc.link(dve.tensor_tensor(past, iota_i.unsqueeze(2).to_broadcast([P, SL, EXPERTS]),
                                      tile_end.unsqueeze(1).to_broadcast([P, SL, EXPERTS]), ALU.is_ge))
            rc.link(dve.tensor_reduce(expert_f, past, AX.X, ALU.add))
            rc.link(dve.tensor_scalar(expert_f, expert_f, float(EXPERTS - 1), None, ALU.min))
            rc.link(dve.tensor_copy(expert_ids, expert_f))
            dve.wait_ge(rt_a, 1)
            rc.link(dve.tensor_scalar(empty, sums[:, SL:2 * SL], 0.5, float(ROWS), ALU.is_lt, ALU.mult))
            rc.link(dve.scalar_tensor_tensor(row_f, sums[:, 0:SL], float(P), sums[:, SL:2 * SL], ALU.mult, ALU.add))
            rc.link(dve.scalar_tensor_tensor(row_f, row_f, -1.0, empty, ALU.add, ALU.add))
            rc.link(dve.tensor_copy(row_ids, row_f))
            rc.link(dve.tensor_scalar(row_tmp, row_ids, TIMES - 1, None, ALU.bitwise_and))
            rc.link(dve.tensor_copy(time_f, row_tmp))
            rc.link(dve.tensor_scalar(row_tmp, row_ids, 4, None, ALU.logical_shift_right))
            rc.link(dve.tensor_copy(row_f, row_tmp))
            rc.step(dve.tensor_scalar(empty, row_f, N_TEXT - 0.5, -float(POSITIONS), ALU.is_gt, ALU.mult))
            rc.link(dve.tensor_scalar(sums[:, 0:SL], row_f, POSITIONS - 0.5, float(POSITIONS), ALU.is_gt, ALU.mult))
            rc.link(dve.scalar_tensor_tensor(empty, empty, float(N_PATCH), sums[:, 0:SL], ALU.add, ALU.add))
            rc.link(dve.tensor_tensor(row_f, row_f, empty, ALU.add))
            rc.link(dve.scalar_tensor_tensor(row_f, time_f, float(POSITIONS), row_f, ALU.mult, ALU.add))
            dve.tensor_copy(out_ids, row_f).then_inc(rt_done, 1)
            dve.wait_ge(rt_done, 1)
            for b in range(2):
                last = dve.memset(fE[b][DK1:E_ROWS, :], X_SCALE)
            last.then_inc(rt_done, 1)

            def slot_step(t):
                nxt, prv = t.shift(1), t.shift(-1)
                if slot_valid(nxt):
                    at_least(dve, fx_mm, nxt.n + 1)
                    at_least(dve, hid_mm, nxt.n - 1)
                    fx = ps[:, 0, 0:3 * P // 2].bitcast(f16)
                    dve.tensor_copy(fT[nxt.par], fx)
                    dve.tensor_copy(fE[nxt.par][0:DK1, :], fx[0:DK1, 2 * P:3 * P]).then_inc(fx_ev, 1)
                if slot_valid(prv):
                    w = tok_row[prv.r][:, 2 * D:ROW_W]
                    cm = Chain(dve, mix_c, prv.n, 3)
                    at_least(dve, mix_done, prv.n - 1)
                    wc, wo = w_common[prv.par], w_own[prv.par]
                    cm.step(dve.tensor_scalar(wc, w, neg_inv_out[:, 0:1], inv_out[:, 0:1], ALU.mult, ALU.add))
                    cm.step(dve.tensor_scalar(wo, w, inv_out[:, 0:1], None, ALU.mult))
                    at_least(dve, two_mm, prv.n + 1)
                    at_least(dve, f_out[prv.shift(-2).r], 16 * prv.shift(2).j)
                    cm.sync()
                    o = ps[:, 6 + prv.par, :]
                    cm.link(dve.scalar_tensor_tensor(mixed[prv.par], o[:, 0:D], wc, tok_row[prv.r][:, D:2 * D], ALU.mult, ALU.add))
                    cm.done()
                    dve.scalar_tensor_tensor(mixed[prv.par], o[:, D:2 * D], wo, mixed[prv.par], ALU.mult, ALU.add).then_inc(mix_done, 1)
                if slot_valid(t):
                    for i in range(2):
                        at_least(dve, hi_done[i], t.n + 1)
                        at_least(dve, two_mm, t.n - 1)
                        dve.scalar_tensor_tensor(g_lo[i][t.par], g32[i], g_scale[:, 0:1], g_hi[i][t.par], ALU.mult, ALU.subtract).then_inc(lo_done[i], 1)

            slot_pipeline(dve, slot_step)

        @block.tensor
        def _(pe):
            pe.wait_ge(prep_g, 3)
            pe.wait_ge(ld_pw, 16)
            pw = patch_W.rearrange("p a (i q c) -> p a i q c", i=2, c=3)
            for c, bank in enumerate((0, 7, 4)):
                for i in range(2):
                    for a in range(2):
                        last = nc.tensor.transpose(ps[:, bank, i * D + a * 96:i * D + (a + 1) * 96], pw[:, a, i, :, c], ident[0:96, 0:96])
            last.then_inc(prep_pe, 1)

            def patch_step(s):
                prv = s.shift(-1)
                if valid(s, 8):
                    for u in range(2):
                        at_least(pe, pix_cut, s.n * 2 + u + 1)
                        at_least(pe, pix_ev_a, s.n * 2 + u - 1)
                        at_least(pe, pix_ev_v, s.n * 2 + u - 1)
                        if isinstance(s.n, int) and s.n == 0 and u == 1:
                            pe.wait_ge(prep_v, 3)
                        for q, (w0, nw_) in enumerate(WP_BANKS):
                            for w in range(nw_):
                                last = nc.tensor.transpose(ps[:, 1 + 3 * u + q, w * RB:(w + 1) * RB], pix_by_patch[u][:, (w0 + w) * P:(w0 + w + 1) * P], ident[0:RB, 0:RB])
                        last.then_inc(pix_T, 1)
                if valid(prv, 8):
                    at_least(pe, pix_ev_a, 2 * (prv.n + 1))
                    at_least(pe, pix_ev_v, 2 * (prv.n + 1))
                    for b in range(2):
                        at_least(pe, emb_v, 2 * (prv.n - 1) + b + 1)
                        for f in range(2):
                            for m in range(6):
                                c, u = m // 2, m % 2
                                col = (b * 3 + c) * N_PATCH + f * ET
                                last = nc.tensor.matmul(ps[0:ET, 7 * b, f * D:(f + 1) * D], XT[prv.par][u][:, col:col + ET], patch_WT[:, c, u, :],
                                                        start=(m == 0), stop=(m == 5))
                        last.then_inc(emb_mm, 1)

            patch_pipeline(pe, patch_step)
            pe.wait_ge(prep_v, PREP_V + 1)
            pe.wait_ge(emb_v, 2 * 8)
            pe.wait_ge(ld_w, 16 * (N_SMALL_LOADS + 4))

            def step(group):
                nxt, prv, pp, p3 = group.shift(1), group.shift(-1), group.shift(-2), group.shift(-3)
                par = group.par

                def split_T(src, sem_):
                    AC, DD = ps[:, 0, :].bitcast(f16), ps[:, 1, :].bitcast(f16)
                    for k in range(GT):
                        nc.tensor.transpose(AC[:, k * P:(k + 1) * P], src[:, k, 0:DK0], ident_h[:, :])
                        nc.tensor.transpose(AC[:, (GT + k) * P:(GT + k + 1) * P], src[:, k, D + DK1:PK], ident_h[:, :])
                        last = nc.tensor.transpose(DD[:, k * P:(k + 1) * P], src[:, k, DK0:D + DK1], ident_h[:, :])
                    last.then_inc(sem_, 1)

                def proj(group, q):
                    if not valid(group):
                        return
                    b = pair(q)
                    if q == 0:
                        at_least(pe, t1_ev, 3 * (group.n + 1))
                        at_least(pe, t2_ev, 3 * (group.n - 1) - 1)
                    if q == 1:
                        at_least(pe, t2_ev, 3 * (group.n - 1))
                    at_least(pe, silu_done, 4 * group.n + q - 1)
                    for m, (T, W, n) in enumerate(((xAC[:, 0], WiA, P), (xAC[:, 0], WiB, P), (xAC[:, 1], WiA, P), (xDD, WiD, P), (xE, WiE, E_ROWS))):
                        if q < 3:
                            for i, (c0, c1) in enumerate(((0, 384), (384, PROJ))):
                                last = nc.tensor.matmul(ps[:, b + i, 0:c1 - c0], T[0:n, q], W[0:n, c0:c1], start=m == 0, stop=m == 4)
                        else:
                            for i in range(2):
                                c0 = PROJ + i * D_STATE
                                last = nc.tensor.matmul(ps[0:D_STATE, b + i, 0:384], W[0:n, c0:c0 + D_STATE], T[0:n].rearrange("p k t -> p (k t)"),
                                                        start=m == 0, stop=m == 4)
                    last.then_inc(proj_mm, 1)

                def y_tile(k):
                    if not valid(prv):
                        return
                    if k == 0:
                        at_least(pe, M_v, prv.n + 1)
                        at_least(pe, silu_done, 4 * prv.n + 3)
                        at_least(pe, Gm_done, prv.n + 1)
                    if k == 1:
                        at_least(pe, M_g, 2 * prv.n + 1)
                        at_least(pe, E_done, prv.n + 1)
                    if k == 2:
                        at_least(pe, M_g, 2 * prv.n + 2)
                        at_least(pe, y1_done, 3 * prv.n + 1)
                    for h in range(HEADS):
                        last = nc.tensor.matmul(ps[:, Y_BANK[k], h * HEADDIM:(h + 1) * HEADDIM], M_all[:, k, h, :],
                                                xs[prv.par][:, k, h * HEADDIM:(h + 1) * HEADDIM], start=True, stop=True)
                    last.then_inc(y_mm, 1)

                if valid(prv):
                    at_least(pe, dec_in_done, prv.n + 1)
                    if valid(pp):
                        at_least(pe, y1_done, 3 * pp.n + 2)
                    nc.tensor.matmul(ps[:, 6, 0:GT * HEADS * TIMES], later[:, :], decay_in, start=True, stop=True).then_inc(L_mm, 1)
                proj(group, 1)
                if valid(pp) or valid(p3):
                    at_least(pe, t1_ev, 3 * (min(group.n, GROUPS - 1) + 1 if isinstance(group.n, int) else group.n + 1))
                if valid(p3):
                    at_least(pe, t3_ev, 3 * (p3.n + 1))
                    for k in range(GT):
                        o = ps[:, 0, 384 + k * EXPERTS:384 + (k + 1) * EXPERTS]
                        for m, (T, W) in enumerate(((nAC[:, 0, k], WsA[:, :]), (nAC[:, 0, k], WsB[:, :]), (nAC[:, 1, k], WsA[:, :]),
                                                    (nD[:, k], WsD[:, :]), (nE[0:E_ROWS, k], WsE[0:E_ROWS, :]))):
                            last = nc.tensor.matmul(o, T, W, start=m == 0, stop=m == 4)
                    last.then_inc(lg_mm, 1)
                if valid(pp):
                    for k in range(GT):
                        at_least(pe, t2_ev, 3 * pp.n + k + 1)
                        for c in range(3):
                            last = nc.tensor.matmul(ps[:, O_BANK[k], O_COL[k]:O_COL[k] + D], yT[:, k, c * P:(c + 1) * P], Wo[:, c, :],
                                                    start=c == 0, stop=c == 2)
                        last.then_inc(o_mm, 1)
                y_tile(0)
                proj(group, 2)
                y_tile(1)
                proj(group, 3)
                y_tile(2)
                if valid(nxt):
                    at_least(pe, xhi_done, nxt.n + 1)
                    at_least(pe, xlo_done, nxt.n + 1)
                    if valid(pp):
                        at_least(pe, h2_done, 3 * (pp.n + 1))
                    if valid(p3):
                        at_least(pe, lg_read, p3.n + 1)
                    split_T(xn_h, t1_mm)
                if not valid(prv):
                    proj(nxt, 0)
                if valid(prv):
                    at_least(pe, t2_ev, 3 * prv.n)
                    for k in range(GT):
                        if k == 2:
                            proj(nxt, 0)
                        at_least(pe, y2_done, 3 * prv.n + k + 1)
                        at_least(pe, silu_done, 4 * group.n + (3 if k < 2 else 4) if valid(group) else 4 * group.n)
                        for c in range(3):
                            last = nc.tensor.transpose(ps[:, T2_BANK[k], c * P:(c + 1) * P], y[:, k, c * P:(c + 1) * P], ident[:, :])
                        last.then_inc(t2_mm, 1)
                if valid(prv):
                    at_least(pe, y1_done, 3 * (prv.n + 1))
                if valid(group):
                    at_least(pe, silu_done, 4 * (group.n + 1))
                    for k in range(GT):
                        last = nc.tensor.matmul(ps[:, 7, k * P:(k + 1) * P], Bs[par][:, k * P:(k + 1) * P], Cs[par][:, k * P:(k + 1) * P],
                                                start=True, stop=True)
                    last.then_inc(G_mm, 1)
                if valid(pp):
                    at_least(pe, nhi_done, pp.n + 1)
                    at_least(pe, nlo_done, pp.n + 1)
                    if valid(nxt):
                        at_least(pe, t1_ev, 3 * (nxt.n + 1))
                    at_least(pe, h2_done, 3 * (pp.n + 1))
                    if valid(p3):
                        at_least(pe, lg_read, p3.n + 1)
                    split_T(rows_h[pp.par], t3_mm)
            pipeline(pe, step)

            pe.wait_ge(rt_v, RT_COUNT)
            pe.wait_ge(rt_g, 6)
            nc.tensor.matmul(ps[:, 1, 0:EXPERTS], earlier_rows[:, :], count, start=True, stop=True)
            nc.tensor.matmul(ps[:, 2, 0:EXPERTS], ones[:, :], count, start=True, stop=True).then_inc(rt_count, 1)

            def add_tiles(j, first=False, last=False):
                pe.wait_ge(hot_q, j + 1)
                pe.wait_ge(hot_k, j + 1)
                pe.wait_ge(hot_p, j + 1)
                for i in range(HOT):
                    k = j * HOT + i
                    ins = nc.tensor.matmul(ps[:, 0, 0:2 * SL], at_q[:, bass.ds(k, 1), :], at_i[:, bass.ds(k, 1), :, :],
                                           start=first and i == 0, stop=last and i == HOT - 1)
                return ins

            add_tiles(0, first=True)
            with pe.Fori(1, TILES // HOT - 1) as j:
                add_tiles(j)
            add_tiles(TILES // HOT - 1, last=True).then_inc(rt_slots, 1)
            pe.wait_ge(ld_experts, 16 * 2)
            pe.wait_ge(cv_hi, EXPERTS)
            pe.wait_ge(cv_lo, EXPERTS)
            pe.wait_ge(rt_done, 2)

            def load_expert(t):
                return pe.value_load(expert_ids[0:1, bass.ds(t.n, 1)], min_val=0, max_val=EXPERTS - 1)

            def slot_step(t):
                nxt, prv = t.shift(1), t.shift(-1)
                if slot_valid(t):
                    e = load_expert(t)
                    at_least(pe, fx_ev, t.n + 1)
                    T = fT[t.par]
                    at_least(pe, gelu_done[0], t.n)
                    at_least(pe, gelu_done[1], t.n)
                    for c in range(FCH):
                        for m, (W, n, r) in enumerate(((W1A, P, T[:, 0:P]), (W1A, P, T[:, P:2 * P]), (W1B, P, T[:, 0:P]),
                                                       (W1D, P, T[:, 2 * P:3 * P]), (W1E, E_ROWS, fE[t.par][0:E_ROWS, :]))):
                            for i, bank in ((1, 1), (0, 3)):
                                o = ps[:, bank + c // 3, (c % 3) * P:(c % 3 + 1) * P]
                                lhs = W[0:n, 0, c * P:(c + 1) * P] if i else W[0:n, bass.ds(e, 1), c * P:(c + 1) * P]
                                last = nc.tensor.matmul(o, lhs, r, start=m == 0, stop=m == 4)
                    last.then_inc(hid_mm, 1)
                if slot_valid(prv):
                    ep = load_expert(prv)
                if slot_valid(nxt):
                    pe.wait_ge(f_rows[nxt.r], 16 * (nxt.j + 1))
                    at_least(pe, fx_ev, nxt.n)
                    fx = ps[:, 0, 0:3 * P // 2].bitcast(f16)
                    for i, col in enumerate((0, D + DK1, DK0)):
                        last = nc.tensor.transpose(fx[:, i * P:(i + 1) * P], tok_h[nxt.r][:, col:col + P], ident_h[:, :])
                    last.then_inc(fx_mm, 1)
                if slot_valid(prv):
                    at_least(pe, mix_done, prv.n - 1)
                    for i in (1, 0):
                        at_least(pe, hi_done[i], prv.n + 1)
                        at_least(pe, lo_done[i], prv.n + 1)
                        o = ps[:, 6 + prv.par, (1 - i) * D:(2 - i) * D]
                        for c in range(FCH):
                            hi, lo = g_hi[i][prv.par][:, c * P:(c + 1) * P], g_lo[i][prv.par][:, c * P:(c + 1) * P]
                            wc = lambda W: W[:, 0, c, :] if i else W[:, bass.ds(ep, 1), c, :]
                            nc.tensor.matmul(o, hi, wc(W2hi), start=c == 0, stop=False)
                            nc.tensor.matmul(o, hi, wc(W2lo), start=False, stop=False)
                            nc.tensor.matmul(o, lo, wc(W2hi), start=False, stop=False)
                        last = nc.tensor.matmul(o, g_scale_row[:, :], b2h[:, 0, :] if i else b2h[:, bass.ds(ep, 1), :], start=False, stop=True)
                    last.then_inc(two_mm, 1)

            slot_pipeline(pe, slot_step)


_INS = ['x', 'txt', 'L0_tok_W', 'L0_tok_b', 'L0_attn_W_in', 'L0_attn_conv_w', 'L0_attn_conv_b', 'L0_attn_dt_bias',
        'L0_attn_A_log', 'L0_attn_D', 'L0_attn_norm_w', 'L0_attn_W_out', 'L0_ffn_Ws', 'L0_ffn_bs', 'L0_ffn_W1',
        'L0_ffn_b1', 'L0_ffn_W2', 'L0_ffn_b2']
_OUTS = [((TIMES, POSITIONS, D), 'float32')]


def kernel(**inputs):
    import numpy as _np
    import concourse.bacc as _bacc
    from concourse import mybir as _mybir
    from concourse.bass_utils import run_bass_kernel_spmd as _run

    nc = _bacc.Bacc("TRN2", target_bir_lowering=False, num_devices=1)
    arrays, args = {}, []
    for name in _INS:
        a = _np.ascontiguousarray(inputs[name])
        arrays[f"in_{name}_dram"] = a
        args.append(nc.dram_tensor(f"in_{name}_dram", a.shape, _mybir.dt.from_np(a.dtype), kind="ExternalInput").ap())
    for i, (shape, dtype) in enumerate(_OUTS):
        dt = _mybir.dt.from_np(_np.dtype(dtype))
        args.append(nc.dram_tensor(f"out_{i}_dram", shape, dt, kind="ExternalOutput").ap())
    build_kernel(nc, *args)
    r = _run(nc, [arrays], core_ids=[0])
    return r.results[0]["out_0_dram"]
```
